# Optimizing a Trainium2 kernel written in Bass

```python
import numpy as np
import jax
import jax.numpy as jnp

def _softmax(x, axis=-1):
    return jax.nn.softmax(x, axis=axis)

def _gelu(x):
    return jax.nn.gelu(x, approximate=True)

def _silu(x):
    return jax.nn.silu(x)

def _sigmoid(x):
    return jax.nn.sigmoid(x)

def _layernorm(x, axis=-1, eps=1e-05):
    m = jnp.mean(x, axis=axis, keepdims=True)
    v = jnp.var(x, axis=axis, keepdims=True)
    return (x - m) / jnp.sqrt(v + eps)

def _scatter_add(tgt, idx, src, axis=0):
    return tgt.at[idx].add(src)

def _segment_sum(src, seg, n):
    return jax.ops.segment_sum(src, seg, n)
kernel_name = 'mk_decoder_preln_d1_seqx_r2_772a6d'

def setup_inputs(seed: int=0):
    np.random.seed(seed)
    _w = jnp.asarray

    def _rec_inputs():
        import jax
        import jax.numpy as jnp
        _rk = jax.random.key(seed)
        x = 0.0002279 + 0.9999 * jax.random.normal(jax.random.fold_in(_rk, 1), (16, 224, 512), jnp.float32)
        _lenS = 224 - jax.random.randint(jax.random.fold_in(_rk, 7), (16,), 0, max(1, 224 // 4) + 1, jnp.int32)
        _lenS2 = 750 - jax.random.randint(jax.random.fold_in(_rk, 8), (16,), 0, max(1, 750 // 4) + 1, jnp.int32)
        _ctx_1024P = jax.random.normal(jax.random.fold_in(_rk, 11), (16, 16, 512), jnp.float32)
        _ctx_1024c = jax.random.dirichlet(jax.random.fold_in(_rk, 511), 0.3 * jnp.ones((16,), jnp.float32), (16, 750))
        _ctx_1024t = jnp.einsum('bsk,bkd->bsd', _ctx_1024c, _ctx_1024P)
        _ctx_1024t = _ctx_1024t * jax.lax.rsqrt(jnp.mean(jnp.square(_ctx_1024t)) + 1e-12) * 0.953939
        ctx_1024 = 7.22013e-05 + 1.00017 * (_ctx_1024t + 0.3 * jax.random.normal(jax.random.fold_in(_rk, 611), (16, 750, 512), jnp.float32))
        return (x, ctx_1024)
    x, ctx_1024 = _rec_inputs()

    def _L0_attn_setup():
        import math
        import jax, jax.numpy as jnp
        import numpy as np
        D_MODEL = 512
        N_HEADS = 16
        D_HEAD = D_MODEL // N_HEADS
        BLOCK = 1024
        BATCH = 2
        SEQ = 1024

        def _rotate(t, cos, sin):
            t1 = t[..., 0::2]
            t2 = t[..., 1::2]
            r1 = t1 * cos - t2 * sin
            r2 = t1 * sin + t2 * cos
            return jnp.stack([r1, r2], axis=-1).reshape(t.shape)
        key = jax.random.key(seed)
        k1, k2, k3 = jax.random.split(key, 3)
        x = jax.random.normal(k1, (BATCH, SEQ, D_MODEL), dtype=jnp.float32)
        Wqkv = jax.random.normal(k2, (3 * D_MODEL, D_MODEL), dtype=jnp.float32) * 0.02
        Wo = jax.random.normal(k3, (D_MODEL, D_MODEL), dtype=jnp.float32) * 0.02
        log_xi = jnp.full((N_HEADS,), math.log(BLOCK / 2.0), dtype=jnp.float32)
        pi_gate_logit = jnp.full((N_HEADS,), 2.0, dtype=jnp.float32)
        e_gate_logit = jnp.full((N_HEADS,), 2.0, dtype=jnp.float32)
        return {'x': x, 'Wqkv': Wqkv, 'Wo': Wo, 'log_xi': log_xi, 'pi_gate_logit': pi_gate_logit, 'e_gate_logit': e_gate_logit}
    _L0_attn_all = _L0_attn_setup()
    _L0_attn_in = {k: v for k, v in _L0_attn_all.items() if k in ('Wqkv', 'Wo', 'log_xi', 'pi_gate_logit', 'e_gate_logit')}
    del _L0_attn_all

    def _L0_xattn_setup():
        import jax, jax.numpy as jnp
        import numpy as np
        HIDDEN = 512
        H = 16
        HK = 4
        G = H // HK
        D = 64
        EPS = 1e-06

        def rmsnorm(x, w):
            var = jnp.mean(jnp.square(x), axis=-1, keepdims=True)
            return x * jax.lax.rsqrt(var + EPS) * w
        key = jax.random.key(seed)
        ks = jax.random.split(key, 8)
        B, S_KV, S_Q = (2, 2048, 256)
        inputs = jax.random.normal(ks[0], (B, S_KV, HIDDEN), dtype=jnp.float32)
        latent = jax.random.normal(ks[1], (B, S_Q, HIDDEN), dtype=jnp.float32)

        def xavier(k, shape, gain=1.0):
            fan_out, fan_in = shape
            limit = gain * np.sqrt(6.0 / (fan_in + fan_out))
            return jax.random.uniform(k, shape, jnp.float32, -limit, limit)
        wq = xavier(ks[2], (H * D, HIDDEN))
        wk = xavier(ks[3], (HK * D, HIDDEN))
        wv = xavier(ks[4], (HK * D, HIDDEN))
        wo = xavier(ks[5], (HIDDEN, H * D), gain=1.0 / np.sqrt(2.0))
        q_norm_w = jnp.ones((D,), jnp.float32)
        k_norm_w = jnp.ones((D,), jnp.float32)
        return {'inputs': inputs, 'latent': latent, 'wq': wq, 'wk': wk, 'wv': wv, 'wo': wo, 'q_norm_w': q_norm_w, 'k_norm_w': k_norm_w}
    _L0_xattn_all = _L0_xattn_setup()
    _L0_xattn_in = {k: v for k, v in _L0_xattn_all.items() if k in ('wq', 'wk', 'wv', 'wo', 'q_norm_w', 'k_norm_w')}
    del _L0_xattn_all

    def _L0_ffn_setup():
        import jax, jax.numpy as jnp
        import numpy as np
        BLOCK = 32
        W_BITS = 4
        ACT_BITS = 16

        def act_qdq(x):
            qmax = 2.0 ** (ACT_BITS - 1) - 1.0
            scale = jnp.maximum(jnp.max(jnp.abs(x)) / qmax, 1e-12)
            return jnp.clip(jnp.round(x / scale), -qmax - 1.0, qmax) * scale

        def fixed_qdq_u16(x):
            scale = 1.0 / 65536.0
            return jnp.clip(jnp.round(x / scale), 0.0, 65535.0) * scale

        def lpbq_dequant(w):
            O, I = w.shape
            qmax = 2.0 ** (W_BITS - 1) - 1.0
            wb = w.reshape(O, I // BLOCK, BLOCK)
            s = jnp.maximum(jnp.max(jnp.abs(wb), axis=-1, keepdims=True) / qmax, 1e-12)
            wq = jnp.clip(jnp.round(wb / s), -qmax - 1.0, qmax) * s
            return wq.reshape(O, I)
        key = jax.random.key(seed)
        k1, k2, k3, k4 = jax.random.split(key, 4)
        B, S, H, I = (2, 2048, 512, 1536)
        x = jax.random.normal(k1, (B, S, H), jnp.float32)
        w_gate = jax.random.normal(k2, (I, H), jnp.float32) * 0.02
        w_up = jax.random.normal(k3, (I, H), jnp.float32) * 0.02
        w_down = jax.random.normal(k4, (H, I), jnp.float32) * 0.02
        return {'x': x, 'w_gate': w_gate, 'w_up': w_up, 'w_down': w_down}
    _L0_ffn_all = _L0_ffn_setup()
    _L0_ffn_in = {k: v for k, v in _L0_ffn_all.items() if k in ('w_gate', 'w_up', 'w_down')}
    del _L0_ffn_all
    return {'x': x, 'ctx_1024': ctx_1024, 'L0_attn_Wqkv': _L0_attn_in['Wqkv'], 'L0_attn_Wo': _L0_attn_in['Wo'], 'L0_attn_log_xi': _L0_attn_in['log_xi'], 'L0_attn_pi_gate_logit': _L0_attn_in['pi_gate_logit'], 'L0_attn_e_gate_logit': _L0_attn_in['e_gate_logit'], 'L0_xattn_wq': _L0_xattn_in['wq'], 'L0_xattn_wk': _L0_xattn_in['wk'], 'L0_xattn_wv': _L0_xattn_in['wv'], 'L0_xattn_wo': _L0_xattn_in['wo'], 'L0_xattn_q_norm_w': _L0_xattn_in['q_norm_w'], 'L0_xattn_k_norm_w': _L0_xattn_in['k_norm_w'], 'L0_ffn_w_gate': _L0_ffn_in['w_gate'], 'L0_ffn_w_up': _L0_ffn_in['w_up'], 'L0_ffn_w_down': _L0_ffn_in['w_down']}

def reference(x, ctx_1024, L0_attn_Wqkv, L0_attn_Wo, L0_attn_log_xi, L0_attn_pi_gate_logit, L0_attn_e_gate_logit, L0_xattn_wq, L0_xattn_wk, L0_xattn_wv, L0_xattn_wo, L0_xattn_q_norm_w, L0_xattn_k_norm_w, L0_ffn_w_gate, L0_ffn_w_up, L0_ffn_w_down):
    import jax
    import jax.numpy as jnp

    def _L0_attn_ref(x, Wqkv, Wo, log_xi, pi_gate_logit, e_gate_logit):
        import math
        import jax, jax.numpy as jnp
        import numpy as np
        D_MODEL = 512
        N_HEADS = 16
        D_HEAD = D_MODEL // N_HEADS
        BLOCK = 1024
        BATCH = 2
        SEQ = 1024

        def _rotate(t, cos, sin):
            t1 = t[..., 0::2]
            t2 = t[..., 1::2]
            r1 = t1 * cos - t2 * sin
            r2 = t1 * sin + t2 * cos
            return jnp.stack([r1, r2], axis=-1).reshape(t.shape)
        b, n, d = x.shape
        H, dh = (N_HEADS, D_HEAD)
        qkv = (x @ Wqkv.T).reshape(b, n, 3, H, dh)
        q = jnp.transpose(qkv[:, :, 0], (0, 2, 1, 3))
        k = jnp.transpose(qkv[:, :, 1], (0, 2, 1, 3))
        v = jnp.transpose(qkv[:, :, 2], (0, 2, 1, 3))
        pi_g = jax.nn.sigmoid(pi_gate_logit)
        e_g = jax.nn.sigmoid(e_gate_logit)
        kfrac = jnp.arange(0, dh, 2, dtype=jnp.float32) / dh
        pi_inv_freq = jnp.float32(math.pi) ** (1.0 - kfrac)
        pos = jnp.arange(n, dtype=jnp.float32)
        theta = pos[:, None] * pi_inv_freq[None, :]
        theta = theta[None, :, :] * pi_g[:, None, None]
        cos, sin = (jnp.cos(theta), jnp.sin(theta))
        q_rot = _rotate(q, cos, sin)
        k_rot = _rotate(k, cos, sin)
        scores = jnp.einsum('bhqd,bhkd->bhqk', q_rot, k_rot) / jnp.float32(math.sqrt(dh))
        xi = jnp.exp(log_xi)
        i = jnp.arange(n, dtype=jnp.float32)
        d_mat = jnp.abs(i[:, None] - i[None, :])
        decay_bias = -(d_mat[None, :, :] / xi[:, None, None]) * e_g[:, None, None]
        scores = scores + decay_bias[None]
        causal = jnp.tril(jnp.ones((n, n), dtype=bool))
        scores = jnp.where(causal[None, None], scores, jnp.float32(-jnp.inf))
        attn = jax.nn.softmax(scores, axis=-1)
        out = jnp.einsum('bhqk,bhkd->bhqd', attn, v)
        out = jnp.transpose(out, (0, 2, 1, 3)).reshape(b, n, d)
        return out @ Wo.T

    def _L0_xattn_ref(inputs, latent, wq, wk, wv, wo, q_norm_w, k_norm_w):
        import jax, jax.numpy as jnp
        import numpy as np
        HIDDEN = 512
        H = 16
        HK = 4
        G = H // HK
        D = 64
        EPS = 1e-06

        def rmsnorm(x, w):
            var = jnp.mean(jnp.square(x), axis=-1, keepdims=True)
            return x * jax.lax.rsqrt(var + EPS) * w
        B, S_q, _ = latent.shape
        S_kv = inputs.shape[1]
        q = (latent @ wq.T).reshape(B, S_q, H, D)
        k = (inputs @ wk.T).reshape(B, S_kv, HK, D)
        v = (inputs @ wv.T).reshape(B, S_kv, HK, D)
        q = rmsnorm(q, q_norm_w)
        k = rmsnorm(k, k_norm_w)
        q = q.transpose(0, 2, 1, 3).reshape(B, HK, G, S_q, D)
        k = k.transpose(0, 2, 1, 3)
        v = v.transpose(0, 2, 1, 3)
        scores = jnp.einsum('bkgqd,bksd->bkgqs', q, k)
        attn = jax.nn.softmax(scores.astype(jnp.float32), axis=-1).astype(q.dtype)
        out = jnp.einsum('bkgqs,bksd->bkgqd', attn, v)
        out = out.reshape(B, H, S_q, D).transpose(0, 2, 1, 3).reshape(B, S_q, H * D)
        return out @ wo.T

    def _L0_ffn_ref(x, w_gate, w_up, w_down):
        import jax, jax.numpy as jnp
        import numpy as np
        BLOCK = 32
        W_BITS = 4
        ACT_BITS = 16

        def act_qdq(x):
            qmax = 2.0 ** (ACT_BITS - 1) - 1.0
            scale = jnp.maximum(jnp.max(jnp.abs(x)) / qmax, 1e-12)
            return jnp.clip(jnp.round(x / scale), -qmax - 1.0, qmax) * scale

        def fixed_qdq_u16(x):
            scale = 1.0 / 65536.0
            return jnp.clip(jnp.round(x / scale), 0.0, 65535.0) * scale

        def lpbq_dequant(w):
            O, I = w.shape
            qmax = 2.0 ** (W_BITS - 1) - 1.0
            wb = w.reshape(O, I // BLOCK, BLOCK)
            s = jnp.maximum(jnp.max(jnp.abs(wb), axis=-1, keepdims=True) / qmax, 1e-12)
            wq = jnp.clip(jnp.round(wb / s), -qmax - 1.0, qmax) * s
            return wq.reshape(O, I)
        x = act_qdq(x)
        up = act_qdq(x @ lpbq_dequant(w_up).T)
        gate = act_qdq(x @ lpbq_dequant(w_gate).T)
        sig = fixed_qdq_u16(jax.nn.sigmoid(gate))
        gate = act_qdq(gate * sig)
        o = act_qdq(gate * up)
        return o @ lpbq_dequant(w_down).T
    x = x + _L0_attn_ref(_layernorm(x, axis=-1), L0_attn_Wqkv, L0_attn_Wo, L0_attn_log_xi, L0_attn_pi_gate_logit, L0_attn_e_gate_logit)
    x = x + _L0_xattn_ref(ctx_1024, _layernorm(x, axis=-1), L0_xattn_wq, L0_xattn_wk, L0_xattn_wv, L0_xattn_wo, L0_xattn_q_norm_w, L0_xattn_k_norm_w)
    x = x + _L0_ffn_ref(_layernorm(x, axis=-1), L0_ffn_w_gate, L0_ffn_w_up, L0_ffn_w_down)
    return x

_drawn_inputs = setup_inputs


def setup_inputs(seed=0):
    import zlib

    import numpy as np

    out = dict(_drawn_inputs(seed))
    spreads = {'L0_attn_log_xi': (6.2383246421813965, 0.2),
     'L0_attn_pi_gate_logit': (2.0, 0.2),
     'L0_attn_e_gate_logit': (2.0, 0.2),
     'L0_xattn_q_norm_w': (1.0, 0.2),
     'L0_xattn_k_norm_w': (1.0, 0.2)}
    factors = {}
    for name, (base, spread) in spreads.items():
        noise = np.random.default_rng([zlib.crc32(name.encode()), seed]).standard_normal(out[name].shape)
        drawn = base * np.exp(spread * noise) if base else spread * noise
        out[name] = jnp.asarray(drawn.astype(out[name].dtype))
    for name, factor in factors.items():
        out[name] = (out[name] * factor).astype(out[name].dtype)
    return out
```

```python
import math
from contextlib import ExitStack, contextmanager

import concourse.bass as bass
import concourse.mybir as mybir
import numpy as np

F32 = mybir.dt.float32
F32R = mybir.dt.float32r
I16 = mybir.dt.int16
I32 = mybir.dt.int32
ALU = mybir.AluOpType
ACT = mybir.ActivationFunctionType
AX = mybir.AxisListType
MAXIMUM = bass.bass_isa.ReduceOp.max

P = 128
BATCH, SEQ, D = 16, 224, 512
TQ = SEQ // 2
NQ = SEQ // TQ
KD = D // P
CTX = 750
LN_EPS = 1e-5
RMS_EPS = 1e-6

AH, ADH = 16, 32
GH = P // ADH
AG = AH // GH
SW = TQ + SEQ
MASKED = -1e30


def at(b, per, n):
    return b * per + n


def wait(eng, sem, value):
    if isinstance(value, int) and value <= 0:
        return
    eng.wait_ge(sem, value)


@contextmanager
def semaphores(nc):
    made = []
    with ExitStack() as ctx:
        def new_semaphore(name):
            made.append(ctx.enter_context(nc.semaphore(name)))
            return made[-1]

        yield new_semaphore
        with nc.Block() as block:
            @block.sync
            def _(sp):
                for s in made:
                    sp.sem_clear(s)


def split_matmul(pe, out, stat, mov, start, stop):
    (sh, sl), (mh, ml) = stat, mov
    pe.matmul(out, sh, mh, start=start, stop=False)
    pe.matmul(out, sl, mh, start=False, stop=False)
    return pe.matmul(out, sh, ml, start=False, stop=stop)


def bits(ap):
    return ap.bitcast(F32)


class Own:

    def __init__(self, eng, sem):
        self.eng, self.sem, self.n = eng, sem, 0

    def done(self, ins):
        ins.then_inc(self.sem, 1)
        self.n += 1
        self.eng.wait_ge(self.sem, self.n)

    def restart(self):
        self.eng.sem_clear(self.sem)
        self.n = 0


def refine_root(dve, own, root, var, tmp):
    own.done(dve.tensor_tensor(tmp, root, root, ALU.mult))
    own.done(dve.scalar_tensor_tensor(tmp, tmp, -0.5, var, ALU.mult, ALU.mult))
    own.done(dve.scalar_tensor_tensor(root, tmp, 1.5, root, ALU.add, ALU.mult))


def split_weights(nc, name, jobs):
    W = max(src.shape[-1] for src, _, _ in jobs)
    with semaphores(nc) as new_semaphore, ExitStack() as ctx:
        raw = ctx.enter_context(nc.sbuf_tensor(f"{name}_raw", [P, 2, W], F32))
        loaded = [new_semaphore(f"{name}_loaded{i}") for i in range(2)]
        high_done = new_semaphore(f"{name}_high_done")
        low_done = new_semaphore(f"{name}_low_done")
        block = ctx.enter_context(nc.Block())

        @block.sync
        def _(sp):
            for n, (src, hi, lo) in enumerate(jobs):
                wait(sp, low_done, n - 1)
                sp.dma_start(raw[:, n % 2, 0:src.shape[-1]], src).then_inc(loaded[n % 2], 16)

        @block.scalar
        def _(act):
            for n, (src, hi, lo) in enumerate(jobs):
                act.wait_ge(loaded[n % 2], 16 * (n // 2 + 1))
                act.activation(hi, raw[:, n % 2, 0:src.shape[-1]], ACT.Copy).then_inc(high_done, 1)

        @block.vector
        def _(dve):
            for n, (src, hi, lo) in enumerate(jobs):
                dve.wait_ge(high_done, n + 1)
                dve.tensor_tensor(lo, raw[:, n % 2, 0:src.shape[-1]], bits(hi), ALU.subtract).then_inc(low_done, 1)


def attention_tables(nc, theta_base, log_xi, pi_gate, e_gate, ident, cos, sin, decay, kpad):
    NF = NQ * AH * ADH // 2
    with semaphores(nc) as new_semaphore, ExitStack() as ctx:
        def sb(name, shape, dt=F32):
            return ctx.enter_context(nc.sbuf_tensor("t_" + name, shape, dt))

        def sem(name):
            return new_semaphore("t_" + name)

        base = sb("base", [TQ, NQ, ADH // 2])
        gates = sb("gates", [TQ, 3, AH])
        ex = sb("ex", [TQ, 3, AH])
        inv = sb("inv", [TQ, 3, AH])
        rate = sb("rate", [TQ, AH])
        theta = sb("theta", [TQ, NQ, AH, ADH // 2])
        turns = sb("turns", [TQ, NF])
        whole = sb("whole", [TQ, NF], I32)
        wrapped = [sb(f"wrapped{i}", [TQ, NF]) for i in range(2)]
        gap_i = sb("gap_i", [TQ, SW], I32)
        gap = sb("gap", [TQ, SW])
        ident_done, loaded, exp_done, gap_done = sem("ident_done"), sem("loaded"), sem("exp_done"), sem("gap_done")
        own_dve, wrap_done, decay_done = sem("own_dve"), sem("wrap_done"), sem("decay_done")
        block = ctx.enter_context(nc.Block())

        @block.sync
        def _(sp):
            sp.dma_start(base[:, :, :], theta_base).then_inc(loaded, 16)
            for i, g in enumerate((log_xi, pi_gate, e_gate)):
                sp.dma_start(gates[:, i, :], g.rearrange("(o h) -> o h", o=1).broadcast_to([TQ, AH])).then_inc(loaded, 16)

        @block.gpsimd
        def _(pool):
            pool.memset(ident[:, :], 0.0).then_inc(ident_done, 1)
            pool.wait_ge(ident_done, 1)
            pool.affine_select(out=ident[:, :], in_=ident[:, :], compare_op=ALU.not_equal, fill=1.0,
                               base=0, pattern=[[-1, P]], channel_multiplier=1)
            pool.iota(gap_i[:, 0:TQ], pattern=[[1, TQ]], base=0, channel_multiplier=-1).then_inc(gap_done, 1)
            pool.iota(gap_i[:, TQ:SW], pattern=[[1, SEQ]], base=-TQ, channel_multiplier=-1).then_inc(gap_done, 1)
            for i in range(2):
                for s in range(2):
                    pool.memset(bits(kpad[i][s][:, :, :]), 0.0)
            for h in range(AH):
                pool.wait_ge(decay_done, h + 1)
                pool.affine_select(out=decay[:, h, 0:TQ], in_=decay[:, h, 0:TQ], compare_op=ALU.is_ge, fill=MASKED,
                                   base=0, pattern=[[-1, TQ]], channel_multiplier=1)
                pool.affine_select(out=decay[:, h, TQ:SW], in_=decay[:, h, TQ:SW], compare_op=ALU.is_ge, fill=MASKED,
                                   base=TQ, pattern=[[-1, SEQ]], channel_multiplier=1)

        @block.scalar
        def _(act):
            act.wait_ge(loaded, 64)
            act.activation(ex[:, :, :], gates[:, :, :], ACT.Exp, scale=-1.0).then_inc(exp_done, 1)
            act.wait_ge(wrap_done, 2)
            for i, out in enumerate((sin, cos)):
                act.activation(out[:, :, :, :], wrapped[i][:, :].rearrange("p (q h f) -> p q h f", q=NQ, h=AH), ACT.Sin)

        @block.vector
        def _(dve):
            own = Own(dve, own_dve)
            dve.wait_ge(exp_done, 1)
            own.done(dve.tensor_scalar(inv[:, :, :], ex[:, :, :], 1.0, None, ALU.add))
            own.done(dve.reciprocal(inv[:, :, :], inv[:, :, :]))
            for q in range(NQ):
                own.done(dve.tensor_tensor(theta[:, q, :, :], base[:, q, None, :].broadcast_to([TQ, AH, ADH // 2]),
                                           inv[:, 1, :, None].broadcast_to([TQ, AH, ADH // 2]), ALU.mult))
            flat = theta[:, :, :, :].rearrange("p q h f -> p (q h f)")
            two_pi = [6.28125, 0.0019350051879882812, 2.0 * math.pi - 6.28125 - 0.0019350051879882812]
            for i, quarter in enumerate((0.0, 0.25)):
                own.done(dve.tensor_scalar(whole[:, :], flat, 1.0 / (2 * math.pi), quarter, ALU.mult, ALU.add))
                own.done(dve.tensor_copy(turns[:, :], whole[:, :]))
                w = wrapped[i][:, :]
                own.done(dve.scalar_tensor_tensor(w, turns[:, :], -two_pi[0], flat, ALU.mult, ALU.add))
                own.done(dve.scalar_tensor_tensor(w, turns[:, :], -two_pi[1], w, ALU.mult, ALU.add))
                own.done(dve.scalar_tensor_tensor(w, turns[:, :], -two_pi[2], w, ALU.mult, ALU.add))
                own.done(dve.tensor_scalar(w, w, quarter * 2 * math.pi, 3.1415925, ALU.add, ALU.min))
                dve.tensor_scalar(w, w, -3.1415925, None, ALU.max).then_inc(wrap_done, 1)
            own.done(dve.tensor_tensor(rate[:, :], ex[:, 0, :], inv[:, 2, :], ALU.mult))
            own.done(dve.tensor_scalar(rate[:, :], rate[:, :], math.sqrt(ADH), None, ALU.mult))
            dve.wait_ge(gap_done, 2)
            own.done(dve.tensor_copy(gap[:, :], gap_i[:, :]))
            for h in range(AH):
                dve.tensor_scalar(decay[:, h, :], gap[:, :], rate[:, h:h + 1], None, ALU.mult).then_inc(decay_done, 1)


def self_attention(nc, ident, x, wqkv_t, wo_t, theta_base, log_xi, pi_gate, e_gate, x1, NB=BATCH):
    SCALE = 1.0 / math.sqrt(ADH)
    NW = 3 * D
    x_v = x.rearrange("b (q p) d -> b p q d", p=TQ)
    x1_v = x1.rearrange("b (q p) d -> b p q d", p=TQ)
    with semaphores(nc) as new_semaphore, ExitStack() as ctx:
        def sb(name, shape, dt=F32):
            return ctx.enter_context(nc.sbuf_tensor("a_" + name, shape, dt))

        def pair(name, shape):
            return [sb(f"{name}_{s}", shape, F32R) for s in ("high", "low")]

        def sem(name):
            return new_semaphore("a_" + name)

        wqkv = pair("wqkv", [P, KD, NW])
        wo = pair("wo", [P, KD, D])
        cos = sb("cos", [TQ, NQ, AH, ADH // 2])
        sin = sb("sin", [TQ, NQ, AH, ADH // 2])
        decay = sb("decay", [TQ, AH, SW])
        kpad = [pair(f"kpad{i}", [P, GH, SEQ]) for i in range(2)]

        split_weights(nc, "a_w", [(wqkv_t[:, k, :], wqkv[0][:, k, :], wqkv[1][:, k, :]) for k in range(KD)]
                      + [(wo_t[:, k, :], wo[0][:, k, :], wo[1][:, k, :]) for k in range(KD)])
        attention_tables(nc, theta_base, log_xi, pi_gate, e_gate, ident, cos, sin, decay, kpad)

        xn = sb("xn", [TQ, NQ, D])
        stats = sb("stats", [TQ, NQ, 6])
        moments = sb("moments", [TQ, NQ, 2])
        var = sb("var", [TQ, NQ])
        root = sb("root", [TQ, NQ])
        newton = sb("newton", [TQ, NQ])
        xnt = pair("xnt", [P, KD, SEQ])
        rot_a = sb("rot_a", [TQ, 2, D])
        rot_b = sb("rot_b", [TQ, 2, D])
        qk = [sb(f"qk{i}", [TQ, 2, NQ, D]) for i in range(2)]
        v = [pair(f"v{i}", [TQ, NQ, D]) for i in range(2)]
        qt_ = [pair(f"qt{i}", [P, SEQ]) for i in range(2)]
        prob = [sb(f"prob{i}", [TQ, GH, SW]) for i in range(2)]
        neg_max = sb("neg_max", [TQ, NQ, GH])
        total = sb("total", [TQ, NQ, GH])
        inv_total = sb("inv_total", [TQ, NQ, GH])
        probt = pair("probt", [TQ, NQ, GH, SEQ])
        attnt = pair("attnt", [P, AG, SEQ])
        xres = sb("xres", [TQ, NQ, D])
        xout = sb("xout", [TQ, NQ, D])

        score_bank = [ctx.enter_context(nc.psum_tensor(f"a_score{i}", [P, 512], F32)) for i in range(3)]
        turn_bank = [ctx.enter_context(nc.psum_tensor(f"a_turn{i}", [P, 512], F32)) for i in range(2)]
        pv_bank = [ctx.enter_context(nc.psum_tensor(f"a_pv{i}", [P, 512], F32)) for i in range(2)]
        piece_bank = ctx.enter_context(nc.psum_tensor("a_piece", [P, 512], F32))

        x_in, res_in, x1_out = sem("x_in"), sem("res_in"), sem("x1_out")
        var_done, root_done, norm_done = sem("var_done"), sem("root_done"), sem("norm_done")
        xt_done, xt_high, xt_low = sem("xt_done"), sem("xt_high"), sem("xt_low")
        proj_done, proj_read, v_high = sem("proj_done"), sem("proj_read"), sem("v_high")
        rot_done = sem("rot_done")
        qkt_done, qkt_high, qkt_low = sem("qkt_done"), sem("qkt_high"), sem("qkt_low")
        score_done, score_read = sem("score_done"), sem("score_read")
        max_done, exp_done, recip_done, prob_done = sem("max_done"), sem("exp_done"), sem("recip_done"), sem("prob_done")
        turn_done, turn_high, turn_low = sem("turn_done"), sem("turn_high"), sem("turn_low")
        pv_done, pv_high, pv_low = sem("pv_done"), sem("pv_high"), sem("pv_low")
        wo_done, wo_read = sem("wo_done"), sem("wo_read")
        own_dve, own_act, own_pool = sem("own_dve"), sem("own_act"), sem("own_pool")

        PIECES = [[("x", 0), ("x", 1), ("qkt", 1), ("proj", 0)],
                  [("wo", 0), ("wo", 1), ("qkt", 2), ("proj", 1)],
                  [("proj", 2), ("proj", 3), ("qkt", 3)],
                  [("proj", 4), ("proj", 5), ("qkt", 0)]]

        def steps(eng, front0, slot, last, restart):
            front0()
            for g in range(AG):
                slot(0, g, 0, True, False)
            if NB > 2:
                with eng.Fori(0, (NB - 2) // 2) as j:
                    restart()
                    for u in range(2):
                        for g in range(AG):
                            slot(2 * j + 1 + u, g, (1 + u) % 2, True, True)
            for g in range(AG):
                slot(NB - 1, g, (NB - 1) % 2, False, True)
            last()

        block = ctx.enter_context(nc.Block())

        @block.sync
        def _(sp):
            def load_x(f):
                wait(sp, xt_done, at(f - 1, 2, 2) if not (isinstance(f, int) and f == 0) else 0)
                sp.dma_start(xn[:, :, :], x_v[f]).then_inc(x_in, 16)

            def slot(b, g, par, front, back):
                if g == 0:
                    if front:
                        load_x(b + 1)
                if g == 1 and back:
                    store(b - 1)

            def store(b):
                if not (isinstance(b, int) and b == 0):
                    sp.wait_ge(wo_read, at(b - 1, 2, 2))
                sp.dma_start(xres[:, :, :], x_v[b]).then_inc(res_in, 16)
                sp.wait_ge(wo_read, at(b, 2, 2))
                sp.dma_start(x1_v[b], xout[:, :, :]).then_inc(x1_out, 16)

            steps(sp, lambda: load_x(0), slot, lambda: store(NB - 1), lambda: None)
            sp.wait_ge(x1_out, 16 * NB)

        @block.tensor
        def _(pe):
            held = [None]

            def take_bank(sem_, value):
                if held[0]:
                    pe.wait_ge(*held[0])
                held[0] = (sem_, value)

            def turn_x(f, q):
                pe.wait_ge(norm_done, f + 1)
                take_bank(xt_low, at(f, 2, q + 1))
                for k in range(KD):
                    m = pe.transpose(piece_bank[:, k * TQ:(k + 1) * TQ], xn[:, q, k * P:(k + 1) * P], ident[0:TQ, 0:TQ])
                m.then_inc(xt_done, 1)

            def project(f, n):
                q, part = n % 2, n // 2
                pe.wait_ge(xt_low, at(f, 2, 2))
                take_bank(proj_read, at(f, 6, n + 1))
                for k in range(KD):
                    m = split_matmul(pe, piece_bank[0:TQ, 0:D], [t[:, k, q * TQ:(q + 1) * TQ] for t in xnt],
                                     [t[:, k, part * D:(part + 1) * D] for t in wqkv], k == 0, k == KD - 1)
                m.then_inc(proj_done, 1)

            def turn_qk(b, g, par):
                pe.wait_ge(rot_done, at(b, 4, 4))
                take_bank(qkt_low, at(b, 4, g + 1))
                for s in range(2):
                    for q in range(NQ):
                        m = pe.transpose(piece_bank[:, (s * NQ + q) * TQ:(s * NQ + q + 1) * TQ],
                                         qk[par][:, s, q, g * P:(g + 1) * P], ident[0:TQ, 0:TQ])
                m.then_inc(qkt_done, 1)

            def output(b, q):
                pe.wait_ge(pv_low, at(b, 8, 8))
                take_bank(wo_read, at(b, 2, q + 1))
                for k in range(AG):
                    m = split_matmul(pe, piece_bank[0:TQ, 0:D], [t[:, k, q * TQ:(q + 1) * TQ] for t in attnt],
                                     [t[:, k, :] for t in wo], k == 0, k == AG - 1)
                m.then_inc(wo_done, 1)

            def piece(b, par, kind, n, front, back):
                if kind == "x" and front:
                    turn_x(b + 1, n)
                elif kind == "proj" and front:
                    project(b + 1, n)
                elif kind == "wo" and back:
                    output(b - 1, n)
                elif kind == "qkt" and n:
                    turn_qk(b, n, par)
                elif kind == "qkt" and front:
                    turn_qk(b + 1, 0, 1 - par)

            def scores(b, g):
                i = g % 2
                pe.wait_ge(qkt_low, at(b, 4, g + 1))
                tiles = [(0, 0, GH, TQ), (1, 0, 2, SEQ), (1, 2, 4, SEQ)]
                for n, (q, h0, h1, keys) in enumerate(tiles):
                    wait(pe, score_read, at(b, 12, 3 * (g - 1) + n + 1))
                    out = score_bank[n][0:TQ, 0:(h1 - h0) * keys].rearrange("p (h k) -> p h k", k=keys)
                    split_matmul(pe, out, [t[:, q * TQ:(q + 1) * TQ] for t in qt_[i]],
                                 [t[:, h0:h1, 0:keys] for t in kpad[i]], True, True).then_inc(score_done, 1)

            def turn_prob(b, g, n):
                wait(pe, turn_low, at(b, 12, 3 * g + n - 1))
                pe.wait_ge(prob_done, at(b, 8, 2 * g + 2))
                bank, pr = turn_bank[(3 * g + n) % 2], prob[g % 2]
                if n < 2:
                    for h in range(2 * n, 2 * n + 2):
                        for q in range(NQ):
                            c = (h % 2) * SEQ + q * TQ
                            m = pe.transpose(bank[0:TQ, c:c + TQ], pr[:, h, q * TQ:(q + 1) * TQ], ident[0:TQ, 0:TQ])
                else:
                    for h in range(GH):
                        m = pe.transpose(bank[0:TQ, h * TQ:(h + 1) * TQ], pr[:, h, 2 * TQ:3 * TQ], ident[0:TQ, 0:TQ])
                m.then_inc(turn_done, 1)

            def weigh_values(b, g, par, n):
                pe.wait_ge(turn_low, at(b, 12, 3 * g + 3))
                wait(pe, pv_low, at(b, 8, 2 * (g - 1) + n + 1))
                for t in range(NQ):
                    m = split_matmul(pe, pv_bank[n][:, 0:2 * SEQ].rearrange("p (h k) -> p h k", k=SEQ),
                                     [s[:, t, g * P:(g + 1) * P] for s in v[par]],
                                     [s[:, t, 2 * n:2 * n + 2, :] for s in probt], t == 0, t == NQ - 1)
                m.then_inc(pv_done, 1)

            def slot(b, g, par, front, back):
                if g == 0:
                    held[0] = (qkt_low, at(b, 4, 1))
                scores(b, g)
                pieces = PIECES[g]
                pb, pg, pp = (b, g - 1, par) if g else (b - 1, AG - 1, 1 - par)
                late = g or back
                piece(b, par, *pieces[0], front, back)
                if late:
                    turn_prob(pb, pg, 0)
                    turn_prob(pb, pg, 1)
                piece(b, par, *pieces[1], front, back)
                if late:
                    turn_prob(pb, pg, 2)
                for pc in pieces[2:3]:
                    piece(b, par, *pc, front, back)
                if late:
                    weigh_values(pb, pg, pp, 0)
                    weigh_values(pb, pg, pp, 1)
                for pc in pieces[3:]:
                    piece(b, par, *pc, front, back)

            def front0():
                for q in range(NQ):
                    turn_x(0, q)
                for n in range(6):
                    project(0, n)
                turn_qk(0, 0, 0)

            def last():
                par = (NB - 1) % 2
                for n in range(3):
                    turn_prob(NB - 1, AG - 1, n)
                for n in range(2):
                    weigh_values(NB - 1, AG - 1, par, n)
                for q in range(NQ):
                    output(NB - 1, q)

            steps(pe, front0, slot, last, lambda: None)

        @block.scalar
        def _(act):
            own = Own(act, own_act)

            def root_guess(f):
                act.wait_ge(var_done, f + 1)
                own.done(act.activation(root[:, :], var[:, :], ACT.Ln))
                act.activation(root[:, :], root[:, :], ACT.Exp, scale=-0.5).then_inc(root_done, 1)

            def high_x(f, q):
                act.wait_ge(xt_done, at(f, 2, q + 1))
                wait(act, proj_done, at(f - 1, 6, 6))
                act.activation(xnt[0][:, :, q * TQ:(q + 1) * TQ], piece_bank[:, 0:KD * TQ].rearrange("p (k t) -> p k t", k=KD),
                               ACT.Copy).then_inc(xt_high, 1)

            def high_v(f, q, par):
                act.wait_ge(proj_done, at(f, 6, 4 + q + 1))
                act.activation(v[par][0][:, q, :], piece_bank[0:TQ, 0:D], ACT.Copy).then_inc(v_high, 1)

            def high_qk(b, g):
                i = g % 2
                act.wait_ge(qkt_done, at(b, 4, g + 1))
                wait(act, score_done, at(b, 12, 3 * (g - 1)))
                act.activation(qt_[i][0][:, :], piece_bank[:, 0:SEQ], ACT.Copy)
                for h in range(GH):
                    r = slice(h * ADH, (h + 1) * ADH)
                    m = act.activation(kpad[i][0][r, h, :], piece_bank[r, SEQ:2 * SEQ], ACT.Copy)
                m.then_inc(qkt_high, 1)

            def exponents(b, g):
                i = g % 2
                act.wait_ge(max_done, at(b, 4, g + 1))
                wait(act, recip_done, at(b, 4, g))
                for q in range(NQ):
                    for h in range(GH):
                        c = slice(0, TQ) if q == 0 else slice(TQ, SW)
                        act.activation(prob[i][:, h, c], prob[i][:, h, c], ACT.Exp, bias=neg_max[:, q, h:h + 1],
                                       scale=SCALE, accum_out=total[:, q, h:h + 1]).then_inc(exp_done, 1)

            def high_prob(b, g, n):
                act.wait_ge(turn_done, at(b, 12, 3 * g + n + 1))
                wait(act, pv_done, at(b, 8, 2 * g))
                bank = turn_bank[(3 * g + n) % 2]
                if n < 2:
                    act.activation(probt[0][:, 0, 2 * n:2 * n + 2, :], bank[0:TQ, 0:2 * SEQ].rearrange("p (h k) -> p h k", h=2),
                                   ACT.Copy).then_inc(turn_high, 1)
                else:
                    act.activation(probt[0][:, 1, :, TQ:SEQ], bank[0:TQ, 0:GH * TQ].rearrange("p (h k) -> p h k", h=GH),
                                   ACT.Copy).then_inc(turn_high, 1)

            def high_attn(b, g, n):
                act.wait_ge(pv_done, at(b, 8, 2 * g + n + 1))
                wait(act, wo_done, at(b - 1, 2, 2))
                for h in range(2 * n, 2 * n + 2):
                    r = slice(h * ADH, (h + 1) * ADH)
                    m = act.activation(attnt[0][r, g, :], pv_bank[n][r, (h % 2) * SEQ:(h % 2 + 1) * SEQ], ACT.Copy)
                m.then_inc(pv_high, 1)

            def piece(b, par, kind, n, front, back):
                if kind == "x" and front:
                    high_x(b + 1, n)
                elif kind == "proj" and front and n >= 4:
                    high_v(b + 1, n - 4, 1 - par)
                elif kind == "qkt" and n:
                    high_qk(b, n)
                elif kind == "qkt" and front:
                    high_qk(b + 1, 0)

            def slot(b, g, par, front, back):
                if g == 0 and front:
                    root_guess(b + 1)
                exponents(b, g)
                pieces = PIECES[g]
                pb, pg = (b, g - 1) if g else (b - 1, AG - 1)
                late = g or back
                piece(b, par, *pieces[0], front, back)
                if late:
                    high_prob(pb, pg, 0)
                    high_prob(pb, pg, 1)
                piece(b, par, *pieces[1], front, back)
                if late:
                    high_prob(pb, pg, 2)
                piece(b, par, *pieces[2], front, back)
                if late:
                    high_attn(pb, pg, 0)
                    high_attn(pb, pg, 1)
                for pc in pieces[3:]:
                    piece(b, par, *pc, front, back)

            def front0():
                root_guess(0)
                for q in range(NQ):
                    high_x(0, q)
                for q in range(NQ):
                    high_v(0, q, 0)
                high_qk(0, 0)

            def last():
                for n in range(3):
                    high_prob(NB - 1, AG - 1, n)
                for n in range(2):
                    high_attn(NB - 1, AG - 1, n)

            act.preload_act_table_set("natural_log_exp_and_others")
            steps(act, front0, slot, last, own.restart)

        @block.vector
        def _(dve):
            own = Own(dve, own_dve)

            def variance(f):
                dve.wait_ge(x_in, at(f, 16, 16))
                for q in range(NQ):
                    m = dve.bn_stats(stats[:, q, :], xn[:, q, :])
                own.done(m)
                for q in range(NQ):
                    m = dve.bn_aggr(moments[:, q, :], stats[:, q, :])
                own.done(m)
                dve.tensor_scalar(var[:, :], moments[:, :, 1], LN_EPS, None, ALU.add).then_inc(var_done, 1)

            def normalise(f):
                dve.wait_ge(root_done, f + 1)
                refine_root(dve, own, root[:, :], var[:, :], newton[:, :])
                for q in range(NQ):
                    m = dve.tensor_scalar(xn[:, q, :], xn[:, q, :], moments[:, q, 0:1], root[:, q:q + 1],
                                          ALU.subtract, ALU.mult)
                m.then_inc(norm_done, 1)

            def low_x(f, q):
                dve.wait_ge(xt_high, at(f, 2, q + 1))
                dve.tensor_tensor(xnt[1][:, :, q * TQ:(q + 1) * TQ], piece_bank[:, 0:KD * TQ].rearrange("p (k t) -> p k t", k=KD),
                                  bits(xnt[0][:, :, q * TQ:(q + 1) * TQ]), ALU.subtract).then_inc(xt_low, 1)

            def rotate(f, n):
                q, i = n % 2, n % 2
                dve.wait_ge(proj_done, at(f, 6, n + 1))
                wait(dve, rot_done, at(f, 4, n - 1))
                src = piece_bank[0:TQ, 0:D].rearrange("p (g e) -> p g e", e=2)
                a = rot_a[:, i, :].rearrange("p (g e) -> p g e", e=2)
                r = rot_b[:, i, :].rearrange("p (g e) -> p g e", e=2)
                c = cos[:, q, :, :].rearrange("p h f -> p (h f)")
                s = sin[:, q, :, :].rearrange("p h f -> p (h f)")
                dve.tensor_tensor(a, src, c[:, :, None].broadcast_to([TQ, D // 2, 2]), ALU.mult)
                dve.scalar_tensor_tensor(r[:, :, 0], src[:, :, 1], -1.0, s, ALU.mult, ALU.mult)
                dve.tensor_tensor(r[:, :, 1], src[:, :, 0], s, ALU.mult).then_inc(proj_read, 1)

            def low_v(f, q, par):
                dve.wait_ge(v_high, at(f, 2, q + 1))
                dve.tensor_tensor(v[par][1][:, q, :], piece_bank[0:TQ, 0:D], bits(v[par][0][:, q, :]),
                                  ALU.subtract).then_inc(proj_read, 1)

            def low_qk(b, g):
                i = g % 2
                dve.wait_ge(qkt_high, at(b, 4, g + 1))
                dve.tensor_tensor(qt_[i][1][:, :], piece_bank[:, 0:SEQ], bits(qt_[i][0][:, :]), ALU.subtract)
                for h in range(GH):
                    r = slice(h * ADH, (h + 1) * ADH)
                    m = dve.tensor_tensor(kpad[i][1][r, h, :], piece_bank[r, SEQ:2 * SEQ], bits(kpad[i][0][r, h, :]),
                                          ALU.subtract)
                m.then_inc(qkt_low, 1)

            def residual(b, q):
                dve.wait_ge(wo_done, at(b, 2, q + 1))
                if q == 0:
                    dve.wait_ge(res_in, at(b, 16, 16))
                    wait(dve, x1_out, at(b, 16, 0))
                dve.tensor_tensor(xout[:, q, :], piece_bank[0:TQ, 0:D], xres[:, q, :], ALU.add).then_inc(wo_read, 1)

            def maxima(b, g):
                i = g % 2
                pr = prob[i]
                wait(dve, turn_done, at(b, 12, 3 * (g - 1)))
                spans = [(0, GH, 0, TQ), (0, 2, TQ, SW), (2, 4, TQ, SW)]
                for n, (h0, h1, c0, c1) in enumerate(spans):
                    dve.wait_ge(score_done, at(b, 12, 3 * g + n + 1))
                    src = score_bank[n][0:TQ, 0:(h1 - h0) * (c1 - c0)].rearrange("p (h k) -> p h k", h=h1 - h0)
                    dve.tensor_tensor(pr[:, h0:h1, c0:c1], src, decay[:, GH * g + h0:GH * g + h1, c0:c1],
                                      ALU.add).then_inc(score_read, 1)
                dve.wait_ge(score_read, at(b, 12, 3 * g + 3))
                wait(dve, exp_done, at(b, 32, 8 * g))
                dve.tensor_reduce(neg_max[:, 0, :], pr[:, :, 0:TQ], AX.X, ALU.max, negate=True)
                own.done(dve.tensor_reduce(neg_max[:, 1, :], pr[:, :, TQ:SW], AX.X, ALU.max, negate=True))
                dve.tensor_scalar(neg_max[:, :, :], neg_max[:, :, :], SCALE, None, ALU.mult).then_inc(max_done, 1)

            def reciprocals(b, g):
                dve.wait_ge(exp_done, at(b, 32, 8 * g + 8))
                wait(dve, prob_done, at(b, 8, 2 * g))
                dve.reciprocal(inv_total[:, :, :], total[:, :, :]).then_inc(recip_done, 1)

            def low_prob(b, g, n):
                dve.wait_ge(turn_high, at(b, 12, 3 * g + n + 1))
                bank = turn_bank[(3 * g + n) % 2]
                if n < 2:
                    dst, hi = [t[:, 0, 2 * n:2 * n + 2, :] for t in (probt[1], probt[0])]
                    src = bank[0:TQ, 0:2 * SEQ].rearrange("p (h k) -> p h k", h=2)
                else:
                    dst, hi = [t[:, 1, :, TQ:SEQ] for t in (probt[1], probt[0])]
                    src = bank[0:TQ, 0:GH * TQ].rearrange("p (h k) -> p h k", h=GH)
                dve.tensor_tensor(dst, src, bits(hi), ALU.subtract).then_inc(turn_low, 1)

            def low_attn(b, g, n):
                dve.wait_ge(pv_high, at(b, 8, 2 * g + n + 1))
                for h in range(2 * n, 2 * n + 2):
                    r = slice(h * ADH, (h + 1) * ADH)
                    m = dve.tensor_tensor(attnt[1][r, g, :], pv_bank[n][r, (h % 2) * SEQ:(h % 2 + 1) * SEQ],
                                          bits(attnt[0][r, g, :]), ALU.subtract)
                m.then_inc(pv_low, 1)

            def piece(b, par, kind, n, front, back):
                if kind == "x" and front:
                    low_x(b + 1, n)
                elif kind == "proj" and front and n < 4:
                    rotate(b + 1, n)
                elif kind == "proj" and front:
                    low_v(b + 1, n - 4, 1 - par)
                elif kind == "wo" and back:
                    residual(b - 1, n)
                elif kind == "qkt" and n:
                    low_qk(b, n)
                elif kind == "qkt" and front:
                    low_qk(b + 1, 0)

            def slot(b, g, par, front, back):
                if g == 0 and front:
                    variance(b + 1)
                maxima(b, g)
                if g == 0 and front:
                    normalise(b + 1)
                pieces = PIECES[g]
                pb, pg = (b, g - 1) if g else (b - 1, AG - 1)
                late = g or back
                piece(b, par, *pieces[0], front, back)
                if late:
                    low_prob(pb, pg, 0)
                    low_prob(pb, pg, 1)
                reciprocals(b, g)
                piece(b, par, *pieces[1], front, back)
                if late:
                    low_prob(pb, pg, 2)
                piece(b, par, *pieces[2], front, back)
                if late:
                    low_attn(pb, pg, 0)
                    low_attn(pb, pg, 1)
                for pc in pieces[3:]:
                    piece(b, par, *pc, front, back)

            def front0():
                for s in probt:
                    dve.memset(bits(s[:, 1, :, 0:TQ]), 0.0)
                variance(0)
                normalise(0)
                for q in range(NQ):
                    low_x(0, q)
                for n in range(4):
                    rotate(0, n)
                for q in range(NQ):
                    low_v(0, q, 0)
                low_qk(0, 0)

            def last():
                for n in range(3):
                    low_prob(NB - 1, AG - 1, n)
                for n in range(2):
                    low_attn(NB - 1, AG - 1, n)
                for q in range(NQ):
                    residual(NB - 1, q)

            steps(dve, front0, slot, last, own.restart)

        @block.gpsimd
        def _(pool):
            def add_rotated(f, n, par):
                i = n % 2
                pool.wait_ge(proj_read, at(f, 6, n + 1))
                pool.tensor_tensor(qk[par][:, n // 2, n % 2, :], rot_a[:, i, :], rot_b[:, i, :], ALU.add).then_inc(rot_done, 1)

            def divide(b, g):
                pool.wait_ge(recip_done, at(b, 4, g + 1))
                pr = prob[g % 2]
                for q, (c0, c1) in enumerate(((0, TQ), (TQ, SW))):
                    pool.tensor_tensor(pr[:, :, c0:c1], pr[:, :, c0:c1], inv_total[:, q, :, None].broadcast_to([TQ, GH, c1 - c0]),
                                       ALU.mult).then_inc(prob_done, 1)

            def slot(b, g, par, front, back):
                first = [n for kind, n in PIECES[g][:2] if kind == "proj" and n < 4]
                rest = [n for kind, n in PIECES[g][2:] if kind == "proj" and n < 4]
                if front:
                    for n in (first if g != 2 else first[:1]):
                        add_rotated(b + 1, n, 1 - par)
                divide(b, g)
                if front:
                    for n in (rest if g != 2 else first[1:] + rest):
                        add_rotated(b + 1, n, 1 - par)

            def front0():
                for n in range(4):
                    add_rotated(0, n, 0)

            steps(pool, front0, slot, lambda: None, lambda: None)


XH, XD = 16, 64
KVH = 4
XG = XH // KVH
NT = BATCH * SEQ // P


def query_projection(nc, ident, x1, wq_t, qn, TILES=NT):
    NWQ = XH * XD
    HALF = 512
    x_v = x1.rearrange("b s d -> (b s) d").rearrange("(t p) d -> t p d", p=P)
    q_v = qn.rearrange("b s d -> (b s) d").rearrange("(t p) d -> t p d", p=P)
    with semaphores(nc) as new_semaphore, ExitStack() as ctx:
        def sb(name, shape, dt=F32):
            return ctx.enter_context(nc.sbuf_tensor("q_" + name, shape, dt))

        def pair(name, shape):
            return [sb(f"{name}_{s}", shape, F32R) for s in ("high", "low")]

        def sem(name):
            return new_semaphore("q_" + name)

        wq = pair("wq", [P, KD, NWQ])
        split_weights(nc, "q_w", [(wq_t[:, k, :], wq[0][:, k, :], wq[1][:, k, :]) for k in range(KD)])
        xb = [sb(f"x{i}", [P, D]) for i in range(2)]
        stats = sb("stats", [P, 6])
        moments = sb("moments", [P, 2])
        var, root, newton = sb("var", [P, 1]), sb("root", [P, 1]), sb("newton", [P, 1])
        xnt = [pair(f"xnt{i}", [P, KD, P]) for i in range(2)]
        raw = [sb(f"raw{i}", [P, XH, XD]) for i in range(2)]
        square = sb("square", [P, XH, XD])
        mean_sq = sb("mean_sq", [P, XH])
        q_root, q_newton = sb("q_root", [P, XH]), sb("q_newton", [P, XH])
        turn_bank = [ctx.enter_context(nc.psum_tensor(f"q_turn{i}", [P, 512], F32)) for i in range(2)]
        proj_bank = [ctx.enter_context(nc.psum_tensor(f"q_proj{i}", [P, 512], F32)) for i in range(4)]

        x_in = [sem(f"x_in{i}") for i in range(2)]
        q_out = [sem(f"q_out{i}") for i in range(2)]
        var_done, root_done, norm_done = sem("var_done"), sem("root_done"), sem("norm_done")
        xt_done, xt_high, xt_low = sem("xt_done"), sem("xt_high"), sem("xt_low")
        proj_done, raw_done = sem("proj_done"), sem("raw_done")
        square_done, mean_done, q_root_done, refined, scaled = (
            sem("square_done"), sem("mean_done"), sem("q_root_done"), sem("refined"), sem("scaled"))
        own_dve, own_act = sem("own_dve"), sem("own_act")

        def steps(eng, front0, step, last, restart=lambda: None):
            front0()
            step(0, 0, True, False)
            step(1, 1, True, True)
            with eng.Fori(0, (TILES - 4) // 2) as j:
                restart()
                for u in range(2):
                    step(2 * j + 2 + u, u, True, True)
            step(TILES - 2, 0, True, True)
            step(TILES - 1, 1, False, True)
            last()

        block = ctx.enter_context(nc.Block())

        @block.sync
        def _(sp):
            def load(t, par):
                wait(sp, xt_done, t - 1)
                sp.dma_start(xb[par][:, :], x_v[t]).then_inc(x_in[par], 16)

            def store(t, par):
                sp.wait_ge(scaled, t + 1)
                sp.dma_start(q_v[t], raw[par][:, :, :].rearrange("p h d -> p (h d)")).then_inc(q_out[par], 16)

            def step(t, par, front, back):
                if front:
                    load(t + 1, 1 - par)
                if back:
                    store(t - 1, 1 - par)

            steps(sp, lambda: load(0, 0), step, lambda: store(TILES - 1, (TILES - 1) % 2))
            for par in range(2):
                sp.wait_ge(q_out[par], 16 * (TILES // 2))

        def half(t):
            return t // 2

        @block.tensor
        def _(pe):
            def turn(t, par):
                pe.wait_ge(norm_done, t + 1)
                wait(pe, xt_low, t - 1)
                for k in range(KD):
                    m = pe.transpose(turn_bank[par][:, k * P:(k + 1) * P], xb[par][:, k * P:(k + 1) * P], ident)
                m.then_inc(xt_done, 1)

            def project(t, par, n):
                pe.wait_ge(xt_low, t + 1)
                wait(pe, raw_done, at(t - 2, 2, n + 1))
                for k in range(KD):
                    m = split_matmul(pe, proj_bank[2 * par + n][:, 0:HALF], [s[:, k, :] for s in xnt[par]],
                                     [s[:, k, n * HALF:(n + 1) * HALF] for s in wq], k == 0, k == KD - 1)
                m.then_inc(proj_done, 1)

            def step(t, par, front, back):
                project(t, par, 0)
                if front:
                    turn(t + 1, 1 - par)
                project(t, par, 1)

            steps(pe, lambda: turn(0, 0), step, lambda: None)

        @block.scalar
        def _(act):
            own = Own(act, own_act)

            def root_guess(t):
                act.wait_ge(var_done, t + 1)
                own.done(act.activation(root[:, :], var[:, :], ACT.Ln))
                act.activation(root[:, :], root[:, :], ACT.Exp, scale=-0.5).then_inc(root_done, 1)

            def q_root_guess(t):
                act.wait_ge(mean_done, t + 1)
                own.done(act.activation(q_root[:, :], mean_sq[:, :], ACT.Ln))
                act.activation(q_root[:, :], q_root[:, :], ACT.Exp, scale=-0.5).then_inc(q_root_done, 1)

            def high(t, par):
                act.wait_ge(xt_done, t + 1)
                wait(act, proj_done, at(t - 2, 2, 2))
                act.activation(xnt[par][0][:, :, :], turn_bank[par][:, :].rearrange("p (k t) -> p k t", k=KD),
                               ACT.Copy).then_inc(xt_high, 1)

            def copy_raw(t, par, n):
                act.wait_ge(proj_done, at(t, 2, n + 1))
                if n == 0 and not (isinstance(t, int) and t < 2):
                    act.wait_ge(q_out[par], 16 * half(t))
                hh = XH // 2
                act.activation(raw[par][:, n * hh:(n + 1) * hh, :],
                               proj_bank[2 * par + n][:, :].rearrange("p (h d) -> p h d", h=hh),
                               ACT.Copy).then_inc(raw_done, 1)

            def step(t, par, front, back):
                if front:
                    root_guess(t + 1)
                if back:
                    q_root_guess(t - 1)
                copy_raw(t, par, 0)
                if front:
                    high(t + 1, 1 - par)
                copy_raw(t, par, 1)

            def front0():
                root_guess(0)
                high(0, 0)

            act.preload_act_table_set("natural_log_exp_and_others")
            steps(act, front0, step, lambda: q_root_guess(TILES - 1), own.restart)

        @block.vector
        def _(dve):
            own = Own(dve, own_dve)

            def variance(t, par):
                dve.wait_ge(x_in[par], 16 * half(t) + 16)
                own.done(dve.bn_stats(stats[:, :], xb[par][:, :]))
                own.done(dve.bn_aggr(moments[:, :], stats[:, :]))
                dve.tensor_scalar(var[:, :], moments[:, 1:2], LN_EPS, None, ALU.add).then_inc(var_done, 1)

            def normalise(t, par):
                dve.wait_ge(root_done, t + 1)
                refine_root(dve, own, root[:, :], var[:, :], newton[:, :])
                dve.tensor_scalar(xb[par][:, :], xb[par][:, :], moments[:, 0:1], root[:, 0:1],
                                  ALU.subtract, ALU.mult).then_inc(norm_done, 1)

            def low(t, par):
                dve.wait_ge(xt_high, t + 1)
                dve.tensor_tensor(xnt[par][1][:, :, :], turn_bank[par][:, :].rearrange("p (k t) -> p k t", k=KD),
                                  bits(xnt[par][0][:, :, :]), ALU.subtract).then_inc(xt_low, 1)

            def mean_square(t):
                dve.wait_ge(square_done, t + 1)
                own.done(dve.tensor_reduce(mean_sq[:, :], square[:, :, :], AX.X, ALU.add))
                dve.tensor_scalar(mean_sq[:, :], mean_sq[:, :], 1.0 / XD, RMS_EPS, ALU.mult, ALU.add).then_inc(mean_done, 1)

            def refine(t):
                dve.wait_ge(q_root_done, t + 1)
                own.done(dve.tensor_tensor(q_newton[:, :], q_root[:, :], q_root[:, :], ALU.mult))
                own.done(dve.scalar_tensor_tensor(q_newton[:, :], q_newton[:, :], -0.5, mean_sq[:, :], ALU.mult, ALU.mult))
                dve.scalar_tensor_tensor(q_root[:, :], q_newton[:, :], 1.5, q_root[:, :], ALU.add, ALU.mult).then_inc(refined, 1)

            def step(t, par, front, back):
                if front:
                    variance(t + 1, 1 - par)
                if back:
                    mean_square(t - 1)
                if front:
                    normalise(t + 1, 1 - par)
                if back:
                    refine(t - 1)
                if front:
                    low(t + 1, 1 - par)

            def front0():
                variance(0, 0)
                normalise(0, 0)
                low(0, 0)

            def last():
                mean_square(TILES - 1)
                refine(TILES - 1)

            steps(dve, front0, step, last, own.restart)

        @block.gpsimd
        def _(pool):
            def squares(t, par):
                pool.wait_ge(raw_done, at(t, 2, 2))
                wait(pool, mean_done, t)
                pool.tensor_tensor(square[:, :, :], raw[par][:, :, :], raw[par][:, :, :], ALU.mult).then_inc(square_done, 1)

            def scale(t, par):
                pool.wait_ge(refined, t + 1)
                pool.tensor_tensor(raw[par][:, :, :], raw[par][:, :, :], q_root[:, :, None].broadcast_to([P, XH, XD]),
                                   ALU.mult).then_inc(scaled, 1)

            def step(t, par, front, back):
                if back:
                    scale(t - 1, 1 - par)
                squares(t, par)

            steps(pool, lambda: None, step, lambda: scale(TILES - 1, (TILES - 1) % 2))


CW = 125
CT = CTX // CW
KVW = KVH * XD
SPLIT = 376


def cross_attention(nc, ident, ctx_t, qn, x1, wkv_t, wo_t, norm_w, x2, NB=BATCH):
    q_v = qn.rearrange("b (q p) (h d) -> b p q h d", p=TQ, d=XD)
    x1_v = x1.rearrange("b (q p) d -> b p q d", p=TQ)
    x2_v = x2.rearrange("b (q p) d -> b p q d", p=TQ)
    with semaphores(nc) as new_semaphore, ExitStack() as ctx:
        def sb(name, shape, dt=F32):
            return ctx.enter_context(nc.sbuf_tensor("b_" + name, shape, dt))

        def pair(name, shape):
            return [sb(f"{name}_{s}", shape, F32R) for s in ("high", "low")]

        def sem(name):
            return new_semaphore("b_" + name)

        NWO = 2 * XG
        wkv = pair("wkv", [P, KD, 2 * KVW])
        wo = pair("wo", [P, NWO, D])
        split_weights(nc, "b_w", [(wkv_t[:, k, :], wkv[0][:, k, :], wkv[1][:, k, :]) for k in range(KD)]
                      + [(wo_t[:, k, :], wo[0][:, k, :], wo[1][:, k, :]) for k in range(NWO)])

        weights = sb("weights", [P, 2])
        k_weight = sb("k_weight", [P, 1])
        craw = [sb(f"craw{i}", [P, KD, CW]) for i in range(2)]
        cpair = [pair(f"cpair{i}", [P, KD, CW]) for i in range(2)]
        kn = sb("kn", [CW, CT, KVH, 2, XD])
        vn = sb("vn", [CW, CT, KVW])
        square = sb("square", [CW, KVH, XD])
        mean_sq = sb("mean_sq", [CW, KVH])
        k_root, newton = sb("k_root", [CW, KVH]), sb("newton", [CW, KVH])
        kt = pair("kt", [P, KVH, CTX])
        v = pair("v", [CW, CT, KVW])
        q2 = [sb(f"q2_{i}", [TQ, NQ, 2, 2, XD]) for i in range(4)]
        qs = sb("qs", [P, XH, SEQ], F32R)
        prob = [sb(f"prob{i}", [TQ, 4, CTX]) for i in range(2)]
        neg_max = sb("neg_max", [TQ, 4])
        total = [sb(f"total{i}", [TQ, 4]) for i in range(2)]
        inv_total = sb("inv_total", [TQ, 4])
        probt = pair("probt", [CW, 3, 2 * SEQ])
        attnt = pair("attnt", [P, NWO, SEQ])
        xres = sb("xres", [TQ, NQ, D])
        xout = sb("xout", [TQ, NQ, D])

        score_bank = [ctx.enter_context(nc.psum_tensor(f"b_score{i}", [P, 1024], F32)) for i in range(2)]
        turn_bank = [ctx.enter_context(nc.psum_tensor(f"b_turn{i}", [P, 512], F32)) for i in range(2)]
        pv_bank = ctx.enter_context(nc.psum_tensor("b_pv", [P, 512], F32))
        piece_bank = ctx.enter_context(nc.psum_tensor("b_piece", [P, 512], F32))

        w_in = sem("w_in")
        res_in, x2_out = sem("res_in"), sem("x2_out")
        c_in = [sem(f"c_in{i}") for i in range(2)]
        q_in = [sem(f"q_in{i}") for i in range(4)]
        c_high, c_low = sem("c_high"), sem("c_low")
        kv_done, kv_raw = sem("kv_done"), sem("kv_raw")
        square_done, mean_done, root_done, refined, k_scaled = (
            sem("square_done"), sem("mean_done"), sem("root_done"), sem("refined"), sem("k_scaled"))
        v_high, v_low = sem("v_high"), sem("v_low")
        kt_done, kt_high, kt_low = sem("kt_done"), sem("kt_high"), sem("kt_low")
        qt_done, qt_high, qt_low = sem("qt_done"), sem("qt_high"), sem("qt_low")
        score_done, max_done, exp_done = sem("score_done"), sem("max_done"), sem("exp_done")
        recip_done, prob_done = sem("recip_done"), sem("prob_done")
        turn_done, turn_high, turn_low = sem("turn_done"), sem("turn_high"), sem("turn_low")
        ring_used = sem("ring_used")
        pv_high, pv_low = sem("pv_high"), sem("pv_low")
        wo_done, wo_read = sem("wo_done"), sem("wo_read")
        own_dve, own_act = sem("own_dve"), sem("own_act")

        U = 8
        PIECES = [[("kt", 3), ("kt", 4), ("kt", 5), ("qt", 4)],
                  [("wo", 0), ("wo", 1), ("qt", 5)],
                  [("qt", 6), ("qt", 7), ("kv", 0)],
                  [("kv", 1), ("kv", 2)],
                  [("kv", 3), ("kv", 4)],
                  [("kv", 5), ("qt", 0), ("qt", 1)],
                  [("kt", 0), ("kt", 1), ("qt", 2)],
                  [("kt", 2), ("qt", 3)]]

        def next_batch(kind, n):
            return kind == "kv" or (kind == "kt" and n < 3) or (kind == "qt" and n < 4)

        CTX_LOADS = {0: (0, 1), 2: (2, 3), 3: (4,), 4: (5,)}
        Q_LOADS = {0: ((0, 6), (0, 7)), 3: ((1, 0), (1, 1)), 4: ((1, 2), (1, 3)), 7: ((1, 4), (1, 5))}

        ORDER = ["s0", "p0", "t0", "t1", "s1", "p1", "t2", "t3", "s2", "p2", "t4", "t5", "s3", "o", "p3"]

        def steps(eng, front0, slot, last, restart=lambda: None):
            front0()
            for u in range(U):
                slot(0, u, True, False)
            if NB > 2:
                with eng.Fori(0, NB - 2) as j:
                    restart()
                    for u in range(U):
                        slot(j + 1, u, True, True)
            for u in range(U):
                slot(NB - 1, u, False, True)
            last()

        def pieces_of(u):
            return {f"p{i}": pc for i, pc in enumerate(PIECES[u])}

        def walk(b, u, front, back, do):
            pb, pu = (b, u - 1) if u else (b - 1, U - 1)
            pcs = pieces_of(u)
            for o in ORDER:
                if o[0] == "s":
                    do["s"](b, u, int(o[1]))
                elif o[0] == "t" and (u or back):
                    do["t"](pb, pu, int(o[1]))
                elif o == "o" and (u or back):
                    do["o"](pb, pu)
                elif o in pcs:
                    kind, n = pcs[o]
                    if kind == "wo":
                        if back:
                            do["wo"](b - 1, n)
                    elif not next_batch(kind, n):
                        do[kind](b, n)
                    elif front:
                        do[kind](b + 1, n)

        FIRST = [("kv", n) for n in range(CT)] + [("kt", n) for n in range(3)] + [("qt", n) for n in range(4)]

        block = ctx.enter_context(nc.Block())

        @block.sync
        def _(sp):
            def load_ctx(b, n):
                wait(sp, c_low, at(b, CT, n - 1))
                sp.dma_start(craw[n % 2][:, :, :], ctx_t[b, n]).then_inc(c_in[n % 2], 16)

            def load_q(b, n):
                wait(sp, qt_done, at(b, 8, n - 3))
                for twice in range(2):
                    for h in range(2):
                        sp.dma_start(q2[n % 4][:, :, h, twice, :], q_v[b, :, :, 2 * n + h, :]).then_inc(q_in[n % 4], 16)

            def load_residual(b):
                wait(sp, wo_read, at(b, 2, 0))
                sp.dma_start(xres[:, :, :], x1_v[b]).then_inc(res_in, 16)

            def store(b):
                sp.wait_ge(wo_read, at(b, 2, 2))
                sp.dma_start(x2_v[b], xout[:, :, :]).then_inc(x2_out, 16)

            def slot(b, u, front, back):
                if u == 2 and back:
                    store(b - 1)
                if u == 3:
                    load_residual(b)
                if front:
                    for n in CTX_LOADS.get(u, ()):
                        load_ctx(b + 1, n)
                for ahead, n in Q_LOADS.get(u, ()):
                    if ahead == 0:
                        load_q(b, n)
                    elif front:
                        load_q(b + 1, n)

            def front0():
                for half in range(2):
                    for i, w in enumerate(norm_w):
                        sp.dma_start(weights[half * XD:(half + 1) * XD, i:i + 1], w.rearrange("(d o) -> d o", o=1)).then_inc(w_in, 16)
                for n in range(2):
                    load_ctx(0, n)
                for n in range(4):
                    load_q(0, n)
                for n in range(2, CT):
                    load_ctx(0, n)
                for n in range(4, 6):
                    load_q(0, n)

            steps(sp, front0, slot, lambda: store(NB - 1))
            sp.wait_ge(x2_out, 16 * NB)

        @block.tensor
        def _(pe):
            held = [None]

            def take_bank(sem_, value):
                if held[0]:
                    pe.wait_ge(*held[0])
                held[0] = (sem_, value)

            def project(b, n):
                pe.wait_ge(c_low, at(b, CT, n + 1))
                take_bank(kv_raw, at(b, CT, n + 1))
                for k in range(KD):
                    m = split_matmul(pe, piece_bank[0:CW, 0:2 * KVW], [s[:, k, :] for s in cpair[n % 2]],
                                     [s[:, k, :] for s in wkv], k == 0, k == KD - 1)
                m.then_inc(kv_done, 1)

            def turn_k(b, n):
                half, c = n // 3, n % 3
                pe.wait_ge(k_scaled, at(b, CT, CT))
                take_bank(kt_low, at(b, 6, n + 1))
                for j in range(2):
                    for i in range(2):
                        m = pe.transpose(piece_bank[:, (2 * j + i) * CW:(2 * j + i + 1) * CW],
                                         kn[:, 2 * c + i, 2 * half + j, :, :].rearrange("p a d -> p (a d)"),
                                         ident[0:CW, 0:CW])
                m.then_inc(kt_done, 1)

            def turn_q(b, n):
                pe.wait_ge(q_in[n % 4], at(b, 128, 64 * (n // 4) + 64))
                take_bank(qt_low, at(b, 8, n + 1))
                for h in range(2):
                    for q in range(NQ):
                        c = h * SEQ + q * TQ
                        m = pe.transpose(piece_bank[:, c:c + TQ], q2[n % 4][:, q, h, :, :].rearrange("p a d -> p (a d)"),
                                         ident[0:TQ, 0:TQ])
                m.then_inc(qt_done, 1)

            def output(b, q):
                pe.wait_ge(pv_low, at(b, U, U))
                take_bank(wo_read, at(b, 2, q + 1))
                for k in range(NWO):
                    m = split_matmul(pe, piece_bank[0:TQ, 0:D], [t[:, k, q * TQ:(q + 1) * TQ] for t in attnt],
                                     [t[:, k, :] for t in wo], k == 0, k == NWO - 1)
                m.then_inc(wo_done, 1)

            def scores(b, u, s):
                h, q, j = 2 * u + s // 2, s % 2, u // 2
                pe.wait_ge(qt_low, at(b, 8, u + 1))
                pe.wait_ge(kt_low, at(b, 6, 3 * (j // 2) + 3))
                wait(pe, exp_done, at(b, 32, 4 * u + s - 1))
                st = qs[:, h, q * TQ:(q + 1) * TQ]
                for c0, c1 in ((0, 512), (512, CTX)):
                    pe.matmul(score_bank[s % 2][0:TQ, c0:c1], st, kt[0][:, j, c0:c1], start=True, stop=False)
                    m = pe.matmul(score_bank[s % 2][0:TQ, c0:c1], st, kt[1][:, j, c0:c1], start=False, stop=True)
                m.then_inc(score_done, 1)

            def turn_prob(b, u, t):
                pe.wait_ge(prob_done, at(b, 32, 4 * u + 4))
                wait(pe, turn_low, at(b, 48, 6 * u + t - 1))
                bank = turn_bank[t % 2]
                for s in range(4):
                    m = pe.transpose(bank[0:CW, s * TQ:(s + 1) * TQ], prob[u % 2][:, s, t * CW:(t + 1) * CW], ident[0:TQ, 0:TQ])
                m.then_inc(turn_done, 1)
                if t >= 1:
                    weigh_values(b, u, t - 1)

            def weigh_values(b, u, t):
                j = u // 2
                pe.wait_ge(turn_low, at(b, 48, 6 * u + t + 1))
                pe.wait_ge(v_low, at(b, 2, j // 2 + 1))
                if t == 0:
                    wait(pe, pv_low, at(b, U, u))
                c0, c1 = (j * XD, (j + 1) * XD) if j % 2 == 0 else ((j - 1) * XD, (j + 1) * XD)
                split_matmul(pe, pv_bank[0:c1 - c0, 0:2 * SEQ], [s[:, t, c0:c1] for s in v],
                             [s[:, t % 3, :] for s in probt], t == 0, t == CT - 1).then_inc(ring_used, 1)

            do = {"s": scores, "t": turn_prob, "o": lambda b, u: weigh_values(b, u, CT - 1),
                  "wo": output, "kv": project, "kt": turn_k, "qt": turn_q}

            def slot(b, u, front, back):
                if u == 0:
                    held[0] = (qt_low, at(b, 8, 4))
                walk(b, u, front, back, do)

            def front0():
                for kind, n in FIRST:
                    do[kind](0, n)

            def last():
                for t in range(CT):
                    turn_prob(NB - 1, U - 1, t)
                weigh_values(NB - 1, U - 1, CT - 1)
                for q in range(NQ):
                    output(NB - 1, q)

            steps(pe, front0, slot, last)

        @block.scalar
        def _(act):
            own = Own(act, own_act)

            def high_ctx(b, n):
                act.wait_ge(c_in[n % 2], at(b, 48, 16 * (n // 2) + 16))
                wait(act, kv_done, at(b, CT, n - 1))
                act.activation(cpair[n % 2][0][:, :, :], craw[n % 2][:, :, :], ACT.Copy).then_inc(c_high, 1)

            def kv_piece(b, n):
                act.wait_ge(kv_done, at(b, CT, n + 1))
                if n == 0:
                    wait(act, v_low, at(b - 1, 2, 2))
                    wait(act, v_high, at(b - 1, 2, 2))
                    wait(act, kt_done, at(b - 1, 6, 6))
                keys = piece_bank[0:CW, 0:KVW].rearrange("p (j d) -> p j d", j=KVH)
                act.activation(kn[:, n, :, :, :], keys[:, :, None, :].broadcast_to([CW, KVH, 2, XD]), ACT.Copy)
                act.activation(vn[:, n, :], piece_bank[0:CW, KVW:2 * KVW], ACT.Copy).then_inc(kv_raw, 1)
                if n + 2 < CT:
                    high_ctx(b, n + 2)
                act.wait_ge(mean_done, at(b, CT, n + 1))
                own.done(act.activation(k_root[:, :], mean_sq[:, :], ACT.Ln))
                act.activation(k_root[:, :], k_root[:, :], ACT.Exp, scale=-0.5).then_inc(root_done, 1)

            def high_k(b, n):
                half, c = n // 3, n % 3
                act.wait_ge(kt_done, at(b, 6, n + 1))
                if n % 3 == 0:
                    wait(act, score_done, at(b - 1, 32, 16 * half + 16))
                act.activation(kt[0][:, 2 * half:2 * half + 2, 2 * c * CW:2 * (c + 1) * CW],
                               piece_bank[:, 0:4 * CW].rearrange("p (j t) -> p j t", j=2), ACT.Copy,
                               scale=k_weight[:, 0:1]).then_inc(kt_high, 1)

            def high_q(b, n):
                act.wait_ge(qt_done, at(b, 8, n + 1))
                wait(act, score_done, at(b - 1, 32, 4 * n + 4))
                act.activation(qs[:, 2 * n:2 * n + 2, :], piece_bank[:, 0:2 * SEQ].rearrange("p (h t) -> p h t", h=2),
                               ACT.Copy).then_inc(qt_high, 1)

            def exponent(b, u, s):
                i = 4 * u + s
                act.wait_ge(max_done, at(b, 32, i + 1))
                act.activation(prob[u % 2][:, s, :], score_bank[s % 2][0:TQ, 0:CTX], ACT.Exp, bias=neg_max[:, s:s + 1],
                               accum_out=total[u % 2][:, s:s + 1]).then_inc(exp_done, 1)

            def high_prob(b, u, t):
                act.wait_ge(turn_done, at(b, 48, 6 * u + t + 1))
                wait(act, ring_used, at(b, 48, 6 * u + t - 2))
                act.activation(probt[0][:, t % 3, :], turn_bank[t % 2][0:CW, 0:2 * SEQ], ACT.Copy).then_inc(turn_high, 1)

            def high_attn(b, u):
                j, m = u // 2, u % 2
                r = slice((j % 2) * XD, (j % 2 + 1) * XD)
                act.wait_ge(ring_used, at(b, 48, 6 * u + 6))
                wait(act, wo_done, at(b - 1, 2, 2))
                k = (j // 2) * XG + 2 * m
                act.activation(attnt[0][r, k:k + 2, :], pv_bank[r, 0:2 * SEQ].rearrange("p (h t) -> p h t", h=2),
                               ACT.Copy).then_inc(pv_high, 1)

            def split_values(b, half):
                act.wait_ge(kv_raw, at(b, CT, CT))
                wait(act, ring_used, at(b - 1, 48, 24 * half + 24))
                act.activation(v[0][:, :, 2 * half * XD:2 * (half + 1) * XD], vn[:, :, 2 * half * XD:2 * (half + 1) * XD],
                               ACT.Copy).then_inc(v_high, 1)

            do = {"s": exponent, "t": high_prob, "o": high_attn, "wo": lambda b, n: None, "kv": kv_piece,
                  "kt": high_k, "qt": high_q}

            def slot(b, u, front, back):
                if u == 1 and front:
                    for n in range(2):
                        high_ctx(b + 1, n)
                walk(b, u, front, back, do)
                if u == 7 and front:
                    split_values(b + 1, 0)
                if u == 0:
                    split_values(b, 1)

            def front0():
                for n in range(2):
                    high_ctx(0, n)
                for kind, n in FIRST:
                    do[kind](0, n)
                split_values(0, 0)

            def last():
                for t in range(CT):
                    high_prob(NB - 1, U - 1, t)
                high_attn(NB - 1, U - 1)

            act.preload_act_table_set("natural_log_exp_and_others")
            steps(act, front0, slot, last, own.restart)

        @block.vector
        def _(dve):
            own = Own(dve, own_dve)

            def kv_piece(b, n):
                dve.wait_ge(square_done, at(b, CT, n + 1))
                own.done(dve.tensor_reduce(mean_sq[:, :], square[:, :, :], AX.X, ALU.add))
                dve.tensor_scalar(mean_sq[:, :], mean_sq[:, :], 1.0 / XD, RMS_EPS, ALU.mult, ALU.add).then_inc(mean_done, 1)
                dve.wait_ge(mean_done, at(b, CT, n + 1))
                dve.wait_ge(root_done, at(b, CT, n + 1))
                own.done(dve.tensor_tensor(newton[:, :], k_root[:, :], k_root[:, :], ALU.mult))
                own.done(dve.scalar_tensor_tensor(newton[:, :], newton[:, :], -0.5, mean_sq[:, :], ALU.mult, ALU.mult))
                own.done(dve.scalar_tensor_tensor(k_root[:, :], newton[:, :], 1.5, k_root[:, :], ALU.add, ALU.mult))
                both = kn[:, n, :, :, :].rearrange("p j a d -> p j (a d)")
                dve.tensor_tensor(both, both, k_root[:, :, None].broadcast_to([CW, KVH, 2 * XD]), ALU.mult).then_inc(k_scaled, 1)

            def low_k(b, n):
                half, c = n // 3, n % 3
                dve.wait_ge(kt_high, at(b, 6, n + 1))
                sel = (slice(None), slice(2 * half, 2 * half + 2), slice(2 * c * CW, 2 * (c + 1) * CW))
                dve.scalar_tensor_tensor(kt[1][sel], piece_bank[:, 0:4 * CW].rearrange("p (j t) -> p j t", j=2),
                                         k_weight[:, 0:1], bits(kt[0][sel]), ALU.mult, ALU.subtract).then_inc(kt_low, 1)

            def low_q(b, n):
                dve.wait_ge(qt_high, at(b, 8, n + 1))
                low = qs[XD:P, 2 * n:2 * n + 2, :]
                dve.tensor_tensor(low, piece_bank[XD:P, 0:2 * SEQ].rearrange("p (h t) -> p h t", h=2), bits(low),
                                  ALU.subtract).then_inc(qt_low, 1)

            def maximum(b, u, s):
                dve.wait_ge(score_done, at(b, 32, 4 * u + s + 1))
                wait(dve, exp_done, at(b, 32, 4 * u + s - 3))
                dve.tensor_reduce(neg_max[:, s:s + 1], score_bank[s % 2][0:TQ, 0:CTX], AX.X, ALU.max,
                                  negate=True).then_inc(max_done, 1)
                if s >= 1:
                    reciprocal(b, u, s - 1)

            def reciprocal(b, u, s):
                dve.wait_ge(exp_done, at(b, 32, 4 * u + s + 1))
                wait(dve, prob_done, at(b, 32, 4 * u + s - 3))
                dve.reciprocal(inv_total[:, s:s + 1], total[u % 2][:, s:s + 1]).then_inc(recip_done, 1)

            def low_prob(b, u, t):
                dve.wait_ge(turn_high, at(b, 48, 6 * u + t + 1))
                dve.tensor_tensor(probt[1][:, t % 3, :], turn_bank[t % 2][0:CW, 0:2 * SEQ], bits(probt[0][:, t % 3, :]),
                                  ALU.subtract).then_inc(turn_low, 1)

            def low_attn(b, u):
                j, m = u // 2, u % 2
                r = slice((j % 2) * XD, (j % 2 + 1) * XD)
                dve.wait_ge(pv_high, at(b, U, u + 1))
                k = (j // 2) * XG + 2 * m
                dve.tensor_tensor(attnt[1][r, k:k + 2, :], pv_bank[r, 0:2 * SEQ].rearrange("p (h t) -> p h t", h=2),
                                  bits(attnt[0][r, k:k + 2, :]), ALU.subtract).then_inc(pv_low, 1)

            def residual(b, q):
                dve.wait_ge(wo_done, at(b, 2, q + 1))
                if q == 0:
                    dve.wait_ge(res_in, at(b, 16, 16))
                    wait(dve, x2_out, at(b, 16, 0))
                dve.tensor_tensor(xout[:, q, :], piece_bank[0:TQ, 0:D], xres[:, q, :], ALU.add).then_inc(wo_read, 1)

            def split_values(b, half):
                dve.wait_ge(v_high, at(b, 2, half + 1))
                sel = (slice(None), slice(None), slice(2 * half * XD, 2 * (half + 1) * XD))
                dve.tensor_tensor(v[1][sel], vn[sel], bits(v[0][sel]), ALU.subtract).then_inc(v_low, 1)

            do = {"s": maximum, "t": low_prob, "o": low_attn, "wo": residual, "kv": kv_piece, "kt": low_k, "qt": low_q}

            def slot(b, u, front, back):
                walk(b, u, front, back, do)
                reciprocal(b, u, 3)
                if u == 7 and front:
                    split_values(b + 1, 0)
                if u == 0:
                    split_values(b, 1)

            def front0():
                dve.wait_ge(w_in, 64)
                own.done(dve.tensor_tensor(k_weight[:, :], weights[:, 0:1], weights[:, 1:2], ALU.mult))
                for kind, n in FIRST:
                    do[kind](0, n)
                split_values(0, 0)

            def last():
                for t in range(CT):
                    low_prob(NB - 1, U - 1, t)
                low_attn(NB - 1, U - 1)
                for q in range(NQ):
                    residual(NB - 1, q)

            steps(dve, front0, slot, last, own.restart)

        @block.gpsimd
        def _(pool):
            def low_ctx(b, n):
                pool.wait_ge(c_high, at(b, CT, n + 1))
                pool.tensor_tensor(cpair[n % 2][1][:, :, :], craw[n % 2][:, :, :], bits(cpair[n % 2][0][:, :, :]),
                                   ALU.subtract).then_inc(c_low, 1)

            def kv_piece(b, n):
                pool.wait_ge(kv_raw, at(b, CT, n + 1))
                wait(pool, mean_done, at(b, CT, n))
                pool.tensor_tensor(square[:, :, :], kn[:, n, :, 0, :], kn[:, n, :, 0, :], ALU.mult).then_inc(square_done, 1)
                if n + 2 < CT:
                    low_ctx(b, n + 2)

            def divide(b, u, s):
                pool.wait_ge(recip_done, at(b, 32, 4 * u + s + 1))
                pr = prob[u % 2][:, s, :]
                pool.tensor_tensor(pr, pr, inv_total[:, s:s + 1].broadcast_to([TQ, CTX]), ALU.mult).then_inc(prob_done, 1)

            def nothing(*_):
                pass

            do = {"s": lambda b, u, s: divide(b, u, s - 1) if s else None, "t": nothing, "o": nothing, "wo": nothing,
                  "kv": kv_piece, "kt": nothing, "qt": nothing}

            def slot(b, u, front, back):
                if u == 1 and front:
                    for n in range(2):
                        low_ctx(b + 1, n)
                walk(b, u, front, back, do)
                divide(b, u, 3)

            def front0():
                for n in range(2):
                    low_ctx(0, n)
                for n in range(CT):
                    kv_piece(0, n)

            steps(pool, front0, slot, nothing)


FF = 1536
FT = FF // P
WBLOCK = 32
NB_BLOCK = D // WBLOCK
W_MAX, A_MAX = 7.0, 32767.0
SIG_STEPS = 65536.0
TINY = 1e-12
CHUNK = 512
NCH = BATCH * SEQ // CHUNK
CTILES = CHUNK // P


def quantise_weights(nc, name, ident, outer, ring, src, dst):
    with semaphores(nc) as new_semaphore, ExitStack() as ctx:
        def sb(nm, shape, dt=F32):
            return ctx.enter_context(nc.sbuf_tensor(f"{name}_{nm}", shape, dt))

        def sem(nm):
            return new_semaphore(f"{name}_{nm}")

        raw = [sb(f"raw{r}", [P, NB_BLOCK, WBLOCK]) for r in range(ring)]
        steps_ = [sb(f"steps{r}", [P, NB_BLOCK, WBLOCK], I16) for r in range(ring)]
        scale = [sb(f"scale{r}", [P, NB_BLOCK]) for r in range(ring)]
        inv = sb("inv", [P, NB_BLOCK])
        bank = [ctx.enter_context(nc.psum_tensor(f"{name}_turn{r}", [P, 512], F32)) for r in range(ring)]
        loaded = [sem(f"loaded{r}") for r in range(ring)]
        stepped, valued, turned, high_done, low_done, own_dve = (
            sem("stepped"), sem("valued"), sem("turned"), sem("high_done"), sem("low_done"), sem("own_dve"))

        def each(eng, step, restart=lambda: None):
            for r in range(ring):
                step(0, r)
            with eng.Fori(0, outer - 1) as j:
                restart()
                for r in range(ring):
                    step(j + 1, r)

        def before(i, r):
            return (i, r - 1) if r else (i - 1, ring - 1)

        block = ctx.enter_context(nc.Block())

        @block.sync
        def _(sp):
            def step(i, r):
                wait(sp, turned, at(i - 1, ring, r + 1))
                sp.dma_start(raw[r][:, :, :].rearrange("p b w -> p (b w)"), src(i, r)).then_inc(loaded[r], 16)

            each(sp, step)

        @block.vector
        def _(dve):
            own = Own(dve, own_dve)

            def quantise(i, r):
                dve.wait_ge(loaded[r], at(i, 16, 16))
                own.done(dve.tensor_reduce(scale[r][:, :], raw[r][:, :, :], AX.X, ALU.max, apply_absolute_value=True))
                own.done(dve.tensor_scalar(scale[r][:, :], scale[r][:, :], 1.0 / W_MAX, TINY, ALU.mult, ALU.max))
                own.done(dve.reciprocal(inv[:, :], scale[r][:, :]))
                dve.tensor_tensor(steps_[r][:, :, :], raw[r][:, :, :], inv[:, :, None].broadcast_to([P, NB_BLOCK, WBLOCK]),
                                  ALU.mult).then_inc(stepped, 1)
                dve.wait_ge(stepped, at(i, ring, r + 1))
                dve.tensor_tensor(raw[r][:, :, :], steps_[r][:, :, :], scale[r][:, :, None].broadcast_to([P, NB_BLOCK, WBLOCK]),
                                  ALU.mult).then_inc(valued, 1)

            def low(i, r):
                dve.wait_ge(high_done, at(i, ring, r + 1))
                hi, lo = dst(i, r)
                dve.tensor_tensor(lo, bank[r][:, :].rearrange("p (k o) -> p k o", k=4), bits(hi), ALU.subtract).then_inc(low_done, 1)

            def step(i, r):
                quantise(i, r)
                if not (isinstance(i, int) and i == 0 and r == 0):
                    low(*before(i, r))

            each(dve, step, own.restart)
            low(outer - 1, ring - 1)

        @block.tensor
        def _(pe):
            def step(i, r):
                pe.wait_ge(valued, at(i, ring, r + 1))
                wait(pe, low_done, at(i - 1, ring, r + 1))
                flat = raw[r][:, :, :].rearrange("p b w -> p (b w)")
                for k in range(4):
                    m = pe.transpose(bank[r][:, k * P:(k + 1) * P], flat[:, k * P:(k + 1) * P], ident)
                m.then_inc(turned, 1)

            each(pe, step)

        @block.scalar
        def _(act):
            def step(i, r):
                act.wait_ge(turned, at(i, ring, r + 1))
                act.activation(dst(i, r)[0], bank[r][:, :].rearrange("p (k o) -> p k o", k=4), ACT.Copy).then_inc(high_done, 1)

            each(act, step)


class Scalars:

    def __init__(self, ctx, nc):
        def sb(name, n=1):
            return ctx.enter_context(nc.sbuf_tensor("s_" + name, [P, n], F32))

        self.peak_x = sb("peak_x", BATCH * SEQ // P)
        self.peak_g, self.peak_u = sb("peak_g", 2 * NCH * FT), sb("peak_u", 2 * NCH * FT)
        self.peak_p, self.peak_o = sb("peak_p", NCH * FT), sb("peak_o", NCH * FT)
        self.s_x, self.r_x = sb("s_x"), sb("r_x")
        self.s_g, self.r_g = sb("s_g"), sb("r_g")
        self.s_u, self.r_u = sb("s_u"), sb("r_u")
        self.s_p, self.r_p = sb("s_p"), sb("r_p")
        self.s_o, self.r_o = sb("s_o"), sb("r_o")
        self.unit = sb("unit")


def scale_from_peak(nc, name, jobs):
    n = len(jobs)
    with semaphores(nc) as new_semaphore, ExitStack() as ctx:
        peak = ctx.enter_context(nc.sbuf_tensor(f"{name}_peak", [P, n], F32))
        whole = ctx.enter_context(nc.sbuf_tensor(f"{name}_whole", [P, n], F32))
        unit_ = ctx.enter_context(nc.sbuf_tensor(f"{name}_unit", [P, n], F32))
        inv = ctx.enter_context(nc.sbuf_tensor(f"{name}_inv", [P, n], F32))
        peak_done, whole_done, own_dve = [new_semaphore(f"{name}_{s}") for s in ("peak_done", "whole_done", "own_dve")]
        block = ctx.enter_context(nc.Block())

        @block.vector
        def _(dve):
            own = Own(dve, own_dve)
            for i, (peaks, _, _, _) in enumerate(jobs):
                dve.tensor_reduce(peak[:, i:i + 1], peaks, AX.X, ALU.max).then_inc(peak_done, 1)
            dve.wait_ge(whole_done, 1)
            for i, (_, (ua, ub), scale, factor) in enumerate(jobs):
                u = unit_[:, i:i + 1]
                own.done(dve.tensor_scalar(u, ua, ub, None, ALU.mult) if ua is not None else dve.memset(u, ub))
                own.done(dve.tensor_scalar(scale[:, :], whole[:, i:i + 1], u, 1.0 / A_MAX, ALU.mult, ALU.mult))
                own.done(dve.tensor_scalar(scale[:, :], scale[:, :], TINY, None, ALU.max))
                own.done(dve.reciprocal(inv[:, i:i + 1], scale[:, :]))
                own.done(dve.tensor_scalar(factor[:, :], inv[:, i:i + 1], u, None, ALU.mult))

        @block.gpsimd
        def _(pool):
            pool.wait_ge(peak_done, n)
            pool.partition_all_reduce(whole[:, :], peak[:, :], P, MAXIMUM).then_inc(whole_done, 1)


def normalise_tokens(nc, x2, xn, peaks, TILES):
    x_v = x2.rearrange("b s d -> (b s) d").rearrange("(t p) d -> p t d", p=P)
    RING = 4
    GROUPS = TILES // RING
    with semaphores(nc) as new_semaphore, ExitStack() as ctx:
        def sb(nm, shape, dt=F32):
            return ctx.enter_context(nc.sbuf_tensor("n_" + nm, shape, dt))

        def sem(nm):
            return new_semaphore("n_" + nm)

        stats, moments = sb("stats", [P, RING, 6]), sb("moments", [P, RING, 2])
        var, root, newton = sb("var", [P, RING]), sb("root", [P, RING]), sb("newton", [P, RING])
        loaded = [sem(f"loaded{i}") for i in range(2)]
        seen, var_done, root_done, own_dve, own_act = (
            sem("seen"), sem("var_done"), sem("root_done"), sem("own_dve"), sem("own_act"))

        def each(eng, step, restart=lambda: None):
            step(0, 0, 0)
            step(1, 1, 0)
            rest = (GROUPS - 2) // 2
            if rest:
                with eng.Fori(0, rest) as j:
                    restart()
                    for v in range(2):
                        step(2 * j + 2 + v, v, j + 1)
            for i in range(2 + 2 * rest, GROUPS):
                step(i, i % 2, i // 2)

        block = ctx.enter_context(nc.Block())

        @block.sync
        def _(sp):
            def step(i, par, r):
                wait(sp, seen, i - 1)
                sp.dma_start(xn[:, bass.ds(i * RING, RING), :], x_v[:, bass.ds(i * RING, RING), :]).then_inc(loaded[par], 16)

            each(sp, step)

        @block.scalar
        def _(act):
            own = Own(act, own_act)
            act.preload_act_table_set("natural_log_exp_and_others")

            def step(i, par, r):
                act.wait_ge(var_done, i + 1)
                own.done(act.activation(root[:, :], var[:, :], ACT.Ln))
                act.activation(root[:, :], root[:, :], ACT.Exp, scale=-0.5).then_inc(root_done, 1)

            each(act, step, own.restart)

        @block.vector
        def _(dve):
            own = Own(dve, own_dve)

            def step(i, par, r):
                dve.wait_ge(loaded[par], at(r, 16, 16))
                for t in range(RING):
                    m = dve.bn_stats(stats[:, t, :], xn[:, i * RING + t, :])
                own.done(m)
                for t in range(RING):
                    m = dve.bn_aggr(moments[:, t, :], stats[:, t, :])
                m.then_inc(seen, 1)
                dve.wait_ge(seen, i + 1)
                dve.tensor_scalar(var[:, :], moments[:, :, 1], LN_EPS, None, ALU.add).then_inc(var_done, 1)
                dve.wait_ge(var_done, i + 1)
                dve.wait_ge(root_done, i + 1)
                refine_root(dve, own, root[:, :], var[:, :], newton[:, :])
                for t in range(RING):
                    tile = xn[:, i * RING + t, :]
                    m = dve.tensor_scalar(tile, tile, moments[:, t, 0:1], root[:, t:t + 1], ALU.subtract, ALU.mult)
                own.done(m)
                own.done(dve.tensor_reduce(peaks[:, bass.ds(i * RING, RING)], xn[:, bass.ds(i * RING, RING), :], AX.X, ALU.max,
                                           apply_absolute_value=True))

            each(dve, step, own.restart)


def gate_and_up(nc, ident, xn, wg, wu, s, g_dram, u_dram, CH):
    with semaphores(nc) as new_semaphore, ExitStack() as ctx:
        def sb(nm, shape, dt=F32):
            return ctx.enter_context(nc.sbuf_tensor("g_" + nm, shape, dt))

        def sem(nm):
            return new_semaphore("g_" + nm)

        xs = [sb(f"xs{i}", [P, D]) for i in range(2)]
        xq = sb("xq", [P, KD, P], I16)
        xt = [[sb(f"xt{i}_{h}", [P, KD, CHUNK], F32R) for h in ("high", "low")] for i in range(2)]
        out = [sb(f"out{i}", [P, CHUNK]) for i in range(4)]
        turn_bank = [ctx.enter_context(nc.psum_tensor(f"g_turn{i}", [P, 512], F32)) for i in range(2)]
        prod_bank = [ctx.enter_context(nc.psum_tensor(f"g_prod{i}", [P, 512], F32)) for i in range(4)]
        stored = [sem(f"stored{i}") for i in range(4)]
        staged, turned, quantised = sem("staged"), sem("turned"), sem("quantised")
        x_high, x_low = sem("x_high"), sem("x_low")
        prod_done, copied, peaked = sem("prod_done"), sem("copied"), sem("peaked")
        NPROD = 2 * FT

        def steps(eng, front0, chunk, restart=lambda: None):
            front0()
            chunk(0, 0, CH > 1)
            rest = CH - 2 if CH > 2 else 0
            pairs = rest // 2
            if pairs:
                with eng.Fori(0, pairs) as j:
                    restart()
                    for u in range(2):
                        chunk(2 * j + 1 + u, (1 + u) % 2, True)
            for c in range(1 + 2 * pairs, CH):
                chunk(c, c % 2, c < CH - 1)

        block = ctx.enter_context(nc.Block())

        @block.tensor
        def _(pe):
            def turn(c, t):
                pe.wait_ge(staged, at(c, CTILES, t + 1))
                wait(pe, quantised, at(c, CTILES, t - 1))
                for k in range(KD):
                    m = pe.transpose(turn_bank[t % 2][:, k * P:(k + 1) * P], xs[t % 2][:, k * P:(k + 1) * P], ident)
                m.then_inc(turned, 1)

            def product(c, par, n):
                f, w = n // 2, (wg, wu)[n % 2]
                wait(pe, peaked, at(c, NPROD, n - 3))
                for k in range(KD):
                    m = split_matmul(pe, prod_bank[n % 4][:, :], [s_[:, f, k, :] for s_ in w], [s_[:, k, :] for s_ in xt[par]],
                                     k == 0, k == KD - 1)
                m.then_inc(prod_done, 1)

            def chunk(c, par, front):
                pe.wait_ge(x_low, at(c, CTILES, CTILES))
                for n in range(NPROD):
                    product(c, par, n)
                    if front and n % 6 == 3:
                        turn(c + 1, n // 6)

            def front0():
                for t in range(CTILES):
                    turn(0, t)

            steps(pe, front0, chunk)

        @block.gpsimd
        def _(pool):
            def stage(c):
                for t in range(CTILES):
                    wait(pool, turned, at(c, CTILES, t - 1))
                    pool.tensor_copy(xs[t % 2][:, :], xn[:, c * CTILES + t, :]).then_inc(staged, 1)

            stage(0)
            with pool.Fori(0, CH - 1) as c:
                stage(c + 1)

        @block.scalar
        def _(act):
            def high(c, par, t):
                act.wait_ge(quantised, at(c, CTILES, t + 1))
                wait(act, prod_done, at(c - 1, NPROD, 0))
                act.activation(xt[par][0][:, :, t * P:(t + 1) * P], xq[:, :, :], ACT.Copy).then_inc(x_high, 1)

            def copy(c, n):
                act.wait_ge(prod_done, at(c, NPROD, n + 1))
                if not (isinstance(c, int) and c == 0 and n < 4):
                    act.wait_ge(stored[n % 4], at(c, 16 * NPROD // 4, 16 * (n // 4)))
                    act.wait_ge(peaked, at(c, NPROD, n - 3))
                act.activation(out[n % 4][:, :], prod_bank[n % 4][:, :], ACT.Copy).then_inc(copied, 1)

            def chunk(c, par, front):
                for n in range(NPROD):
                    copy(c, n)
                    if front and n % 6 == 3:
                        high(c + 1, 1 - par, n // 6)

            def front0():
                for t in range(CTILES):
                    high(0, 0, t)

            steps(act, front0, chunk)

        @block.vector
        def _(dve):
            def quantise(c, t):
                dve.wait_ge(turned, at(c, CTILES, t + 1))
                wait(dve, x_low, at(c, CTILES, t))
                dve.tensor_scalar(xq[:, :, :], turn_bank[t % 2][:, :].rearrange("p (k t) -> p k t", k=KD), s.r_x[:, 0:1], None,
                                  ALU.mult).then_inc(quantised, 1)

            def low(c, par, t):
                dve.wait_ge(x_high, at(c, CTILES, t + 1))
                cols = slice(t * P, (t + 1) * P)
                dve.tensor_tensor(xt[par][1][:, :, cols], xq[:, :, :], bits(xt[par][0][:, :, cols]), ALU.subtract).then_inc(x_low, 1)

            def peak(c, n):
                f = n // 2
                dve.wait_ge(copied, at(c, NPROD, n + 1))
                dst = (s.peak_g, s.peak_u)[n % 2]
                dve.tensor_reduce(dst[:, bass.ds(c * FT + f, 1)], out[n % 4][:, :], AX.X, ALU.max,
                                  apply_absolute_value=True).then_inc(peaked, 1)

            def chunk(c, par, front):
                for n in range(NPROD):
                    if front and n % 6 == 4:
                        low(c + 1, 1 - par, n // 6)
                    peak(c, n)
                    if front and n % 6 == 3:
                        quantise(c + 1, n // 6)

            def front0():
                for t in range(CTILES):
                    quantise(0, t)
                    low(0, 0, t)

            steps(dve, front0, chunk)

        @block.sync
        def _(sp):
            def chunk(c, par, front):
                for n in range(NPROD):
                    sp.wait_ge(copied, at(c, NPROD, n + 1))
                    sp.dma_start((g_dram, u_dram)[n % 2][c, n // 2], out[n % 4][:, :]).then_inc(stored[n % 4], 16)

            steps(sp, lambda: None, chunk)
            for i in range(4):
                sp.wait_ge(stored[i], 16 * (NPROD // 4) * CH)


WIDE = 2 * CHUNK


def product_peak(nc, g_dram, prod, s, CH):
    N = CH * FT // 2
    with semaphores(nc) as new_semaphore, ExitStack() as ctx:
        def sb(nm, shape, dt=F32):
            return ctx.enter_context(nc.sbuf_tensor("p_" + nm, shape, dt))

        def sem(nm):
            return new_semaphore("p_" + nm)

        g = [sb(f"g{i}", [P, WIDE]) for i in range(2)]
        gq = [sb(f"gq{i}", [P, WIDE], I16) for i in range(2)]
        sig = [sb(f"sig{i}", [P, WIDE]) for i in range(2)]
        sq = [sb(f"sq{i}", [P, WIDE], I32) for i in range(2)]
        loaded = [sem(f"loaded{i}") for i in range(2)]
        g_done, sig_done, sq_done, prod_done, peaked = sem("g_done"), sem("sig_done"), sem("sq_done"), sem("prod_done"), sem("peaked")
        g_v = g_dram.rearrange("c f p t -> (c f) p t").rearrange("(n f) p t -> n p f t", f=2)

        def tile(n):
            return prod[:, bass.ds(n * WIDE, WIDE)]

        def each(eng, step):
            for n in range(2):
                step(n, n)
            with eng.Fori(0, (N - 2) // 2) as j:
                for u in range(2):
                    step(2 * j + 2 + u, u)

        block = ctx.enter_context(nc.Block())

        @block.sync
        def _(sp):
            def step(n, par):
                wait(sp, g_done, n - 1)
                sp.dma_start(g[par][:, :].rearrange("p (f t) -> p f t", f=2), g_v[n]).then_inc(loaded[par], 16)

            each(sp, step)

        @block.scalar
        def _(act):
            def step(n, par):
                act.wait_ge(g_done, n + 1)
                act.activation(sig[par][:, :], gq[par][:, :], ACT.Sigmoid, scale=s.s_g[:, 0:1]).then_inc(sig_done, 1)
                act.wait_ge(sig_done, n + 1)
                wait(act, prod_done, n - 1)
                act.activation(sq[par][:, :], sig[par][:, :], ACT.Copy, scale=SIG_STEPS).then_inc(sq_done, 1)

            each(act, step)

        @block.vector
        def _(dve):
            def quantise(n, par):
                dve.wait_ge(loaded[par], 16 * (n // 2) + 16)
                wait(dve, sig_done, n - 1)
                wait(dve, prod_done, n - 1)
                dve.tensor_scalar(gq[par][:, :], g[par][:, :], s.r_g[:, 0:1], None, ALU.mult).then_inc(g_done, 1)

            def multiply(n, par):
                dve.wait_ge(sq_done, n + 1)
                dve.scalar_tensor_tensor(tile(n), sq[par][:, :], SIG_STEPS - 1.0, gq[par][:, :], ALU.min,
                                         ALU.mult).then_inc(prod_done, 1)

            def peak(n, par):
                dve.wait_ge(prod_done, n + 1)
                dve.tensor_reduce(s.peak_p[:, bass.ds(n, 1)], tile(n), AX.X, ALU.max,
                                  apply_absolute_value=True).then_inc(peaked, 1)

            def step(n, par):
                if not (isinstance(n, int) and n < 2):
                    multiply(n - 2, par)
                quantise(n, par)
                if not (isinstance(n, int) and n < 2):
                    peak(n - 2, par)

            each(dve, step)
            for n in (N - 2, N - 1):
                multiply(n, n % 2)
                peak(n, n % 2)


def gated_product(nc, prod, u_dram, o_dram, s, CH):
    N = CH * FT // 2
    with semaphores(nc) as new_semaphore, ExitStack() as ctx:
        def sb(nm, shape, dt=F32):
            return ctx.enter_context(nc.sbuf_tensor("o_" + nm, shape, dt))

        def sem(nm):
            return new_semaphore("o_" + nm)

        u = [sb(f"u{i}", [P, WIDE]) for i in range(3)]
        uq = [sb(f"uq{i}", [P, WIDE], I16) for i in range(3)]
        pq = [sb(f"pq{i}", [P, WIDE], I16) for i in range(3)]
        loaded = [sem(f"loaded{i}") for i in range(3)]
        stored = sem("stored")
        u_done, pq_done, o_done, peaked = sem("u_done"), sem("pq_done"), sem("o_done"), sem("peaked")
        u_v = u_dram.rearrange("c f p t -> (c f) p t").rearrange("(n f) p t -> n p f t", f=2)
        o_v = o_dram.rearrange("c f p t -> (c f) p t").rearrange("(n f) p t -> n p f t", f=2)

        def tile(n):
            return prod[:, bass.ds(n * WIDE, WIDE)]

        def each(eng, step):
            for n in range(3):
                step(n, n, 0)
            with eng.Fori(0, (N - 3) // 3) as j:
                for v in range(3):
                    step(3 * j + 3 + v, v, j + 1)

        block = ctx.enter_context(nc.Block())

        @block.sync
        def _(sp):
            def step(n, slot, i):
                wait(sp, u_done, n - 2)
                sp.dma_start(u[slot][:, :].rearrange("p (f t) -> p f t", f=2), u_v[n]).then_inc(loaded[slot], 16)

            each(sp, step)

        @block.gpsimd
        def _(pool):
            def step(n, slot, i):
                pool.wait_ge(o_done, n + 1)
                pool.dma_start(o_v[n], tile(n).rearrange("p (f t) -> p f t", f=2)).then_inc(stored, 16)

            each(pool, step)
            pool.wait_ge(stored, 16 * N)

        @block.scalar
        def _(act):
            def step(n, slot, i):
                wait(act, o_done, n - 2)
                act.activation(pq[slot][:, :], tile(n), ACT.Copy, scale=s.r_p[:, 0:1]).then_inc(pq_done, 1)
                act.wait_ge(loaded[slot], at(i, 16, 16))
                act.activation(uq[slot][:, :], u[slot][:, :], ACT.Copy, scale=s.r_u[:, 0:1]).then_inc(u_done, 1)

            each(act, step)

        @block.vector
        def _(dve):
            def multiply(n, slot):
                dve.wait_ge(u_done, n + 1)
                dve.wait_ge(pq_done, n + 1)
                dve.tensor_tensor(tile(n), pq[slot][:, :], uq[slot][:, :], ALU.mult).then_inc(o_done, 1)

            def peak(n):
                dve.wait_ge(o_done, n + 1)
                dve.tensor_reduce(s.peak_o[:, bass.ds(n, 1)], tile(n), AX.X, ALU.max,
                                  apply_absolute_value=True).then_inc(peaked, 1)

            def step(n, slot, i):
                multiply(n, slot)
                if not (isinstance(n, int) and n == 0):
                    peak(n - 1)

            each(dve, step)
            peak(N - 1)


def down_product(nc, o_dram, wd, s, x2, out, CH):
    x2_v = x2.rearrange("b s d -> (b s) d").rearrange("(t p) d -> t p d", p=P)
    out_v = out.rearrange("b s d -> (b s) d").rearrange("(t p) d -> t p d", p=P)
    with semaphores(nc) as new_semaphore, ExitStack() as ctx:
        def sb(nm, shape, dt=F32):
            return ctx.enter_context(nc.sbuf_tensor("d_" + nm, shape, dt))

        def sem(nm):
            return new_semaphore("d_" + nm)

        o = [sb(f"o{i}", [P, CHUNK]) for i in range(4)]
        oq = [sb(f"oq{i}", [P, CHUNK], I16) for i in range(2)]
        ot = [[sb(f"ot{i}_{h}", [P, FT, CHUNK], F32R) for h in ("high", "low")] for i in range(2)]
        x = [sb(f"x{i}", [P, D]) for i in range(2)]
        y = [sb(f"y{i}", [P, D]) for i in range(2)]
        bank = [ctx.enter_context(nc.psum_tensor(f"d_prod{i}", [P, 512], F32)) for i in range(2)]
        loaded = [sem(f"loaded{i}") for i in range(4)]
        x_in = [sem(f"x_in{i}") for i in range(2)]
        y_out = [sem(f"y_out{i}") for i in range(2)]
        quantised, high_done, low_done = sem("quantised"), sem("high_done"), sem("low_done")
        prod_done, added = sem("prod_done"), sem("added")

        def steps(eng, front0, chunk):
            front0()
            chunk(0, 0, CH > 1)
            pairs = (CH - 2) // 2 if CH > 2 else 0
            if pairs:
                with eng.Fori(0, pairs) as j:
                    for v in range(2):
                        chunk(2 * j + 1 + v, (1 + v) % 2, True)
            for c in range(1 + 2 * pairs, CH):
                chunk(c, c % 2, c < CH - 1)

        PER = FT // CTILES

        block = ctx.enter_context(nc.Block())

        @block.sync
        def _(sp):
            def load(c, f):
                wait(sp, quantised, at(c, FT, f - 3))
                sp.dma_start(o[f % 4][:, :], o_dram[c, f]).then_inc(loaded[f % 4], 16)

            def load_x(c, t):
                wait(sp, added, at(c, CTILES, t - 1))
                sp.dma_start(x[t % 2][:, :], x2_v[c * CTILES + t]).then_inc(x_in[t % 2], 16)

            def store(c, t):
                sp.wait_ge(added, at(c, CTILES, t + 1))
                sp.dma_start(out_v[c * CTILES + t], y[t % 2][:, :]).then_inc(y_out[t % 2], 16)

            def chunk(c, par, front):
                for t in range(CTILES):
                    load_x(c, t)
                    if front:
                        for f in range(PER * t, PER * (t + 1)):
                            load(c + 1, f)
                    store(c, t)

            def front0():
                for f in range(FT):
                    load(0, f)

            steps(sp, front0, chunk)
            for i in range(2):
                sp.wait_ge(y_out[i], 16 * CH * CTILES // 2)

        @block.tensor
        def _(pe):
            def chunk(c, par, front):
                for t in range(CTILES):
                    if t == 0:
                        pe.wait_ge(low_done, at(c, FT, FT))
                    wait(pe, added, at(c, CTILES, t - 1))
                    for f in range(FT):
                        m = split_matmul(pe, bank[t % 2][:, :], [s_[:, f, t * P:(t + 1) * P] for s_ in ot[par]],
                                         [s_[:, f, :] for s_ in wd], f == 0, f == FT - 1)
                    m.then_inc(prod_done, 1)

            steps(pe, lambda: None, chunk)

        @block.scalar
        def _(act):
            def high(c, par, f):
                act.wait_ge(quantised, at(c, FT, f + 1))
                if f == 0:
                    wait(act, prod_done, at(c - 1, CTILES, 0))
                act.activation(ot[par][0][:, f, :], oq[f % 2][:, :], ACT.Copy).then_inc(high_done, 1)

            def chunk(c, par, front):
                if front:
                    for f in range(FT):
                        high(c + 1, 1 - par, f)

            def front0():
                for f in range(FT):
                    high(0, 0, f)

            steps(act, front0, chunk)

        @block.vector
        def _(dve):
            def quantise(c, f):
                dve.wait_ge(loaded[f % 4], at(c, 16 * FT // 4, 16 * (f // 4) + 16))
                wait(dve, low_done, at(c, FT, f - 1))
                dve.tensor_scalar(oq[f % 2][:, :], o[f % 4][:, :], s.r_o[:, 0:1], None, ALU.mult).then_inc(quantised, 1)

            def low(c, par, f):
                dve.wait_ge(high_done, at(c, FT, f + 1))
                dve.tensor_tensor(ot[par][1][:, f, :], oq[f % 2][:, :], bits(ot[par][0][:, f, :]), ALU.subtract).then_inc(low_done, 1)

            def add(c, t):
                dve.wait_ge(prod_done, at(c, CTILES, t + 1))
                dve.wait_ge(x_in[t % 2], at(c, 16 * CTILES // 2, 16 * (t // 2) + 16))
                if not (isinstance(c, int) and c == 0 and t < 2):
                    dve.wait_ge(y_out[t % 2], at(c, 16 * CTILES // 2, 16 * (t // 2)))
                dve.scalar_tensor_tensor(y[t % 2][:, :], bank[t % 2][:, :], s.s_o[:, 0:1], x[t % 2][:, :], ALU.mult,
                                         ALU.add).then_inc(added, 1)

            def prepare(c, par, t):
                for f in range(PER * t, PER * (t + 1)):
                    quantise(c, f)
                    if f:
                        low(c, par, f - 1)
                if t == CTILES - 1:
                    low(c, par, FT - 1)

            def chunk(c, par, front):
                for t in range(CTILES):
                    if front:
                        prepare(c + 1, 1 - par, t)
                    add(c, t)

            def front0():
                for t in range(CTILES):
                    prepare(0, 0, t)

            steps(dve, front0, chunk)


def feed_forward(nc, ident, x2, w_gate, w_up, w_down, g_dram, u_dram, o_dram, out, CH=NCH):
    T = BATCH * SEQ // P if CH == NCH else CH * CTILES
    NF = CH * FT
    with ExitStack() as ctx:
        s = Scalars(ctx, nc)
        with ExitStack() as inner:
            xn = inner.enter_context(nc.sbuf_tensor("f_xn", [P, T, D], F32))
            wgu = [[inner.enter_context(nc.sbuf_tensor(f"f_w{w}_{h}", [P, FT, KD, P], F32R)) for h in ("high", "low")]
                   for w in "gu"]
            src = [w.rearrange("(f p) i -> f p i", p=P) for w in (w_gate, w_up)]
            quantise_weights(nc, "fw", ident, FT, 2, lambda i, r: src[r][i], lambda i, r: [h[:, i, :, :] for h in wgu[r]])
            normalise_tokens(nc, x2, xn, s.peak_x, T)
            scale_from_peak(nc, "fx", [(s.peak_x[:, 0:T], (None, 1.0), s.s_x, s.r_x)])
            gate_and_up(nc, ident, xn, wgu[0], wgu[1], s, g_dram, u_dram, CH)
        scale_from_peak(nc, "fg", [(s.peak_g[:, 0:NF], (s.s_x[:, 0:1], 1.0), s.s_g, s.r_g),
                                   (s.peak_u[:, 0:NF], (s.s_x[:, 0:1], 1.0), s.s_u, s.r_u)])
        with nc.sbuf_tensor("f_prod", [P, NF * CHUNK], F32) as prod:
            product_peak(nc, g_dram, prod, s, CH)
            scale_from_peak(nc, "fp", [(s.peak_p[:, 0:NF // 2], (s.s_g[:, 0:1], 1.0 / SIG_STEPS), s.s_p, s.r_p)])
            gated_product(nc, prod, u_dram, o_dram, s, CH)
        scale_from_peak(nc, "fo", [(s.peak_o[:, 0:NF // 2], (s.s_p[:, 0:1], s.s_u[:, 0:1]), s.s_o, s.r_o)])
        wd = [ctx.enter_context(nc.sbuf_tensor(f"f_wd_{h}", [P, FT, D], F32R)) for h in ("high", "low")]
        wd_src = w_down.rearrange("(o p) (c i) -> o c p i", p=P, i=512)
        quantise_weights(nc, "fd", ident, D // P, 3, lambda i, r: wd_src[i, r],
                         lambda i, r: [h[:, 4 * r:4 * r + 4, bass.ds(i * P, P)] for h in wd])
        down_product(nc, o_dram, wd, s, x2, out, CH)


def build(nc, t):
    x1 = nc.dram_tensor("x1", (BATCH, SEQ, D), F32, kind="Internal").ap()
    x2 = nc.dram_tensor("x2", (BATCH, SEQ, D), F32, kind="Internal").ap()
    qn = nc.dram_tensor("qn", (BATCH, SEQ, XH * XD), F32, kind="Internal").ap()
    g_dram, u_dram, o_dram = [nc.dram_tensor(n, (NCH, FT, P, CHUNK), F32, kind="Internal").ap()
                              for n in ("gate", "up", "gated")]
    with nc.sbuf_tensor("ident", [P, P], F32) as ident:
        eye = ident[:, :]
        self_attention(nc, eye, t["x"], t["wqkv_t"], t["self_wo_t"], t["theta_base"], t["log_xi"], t["pi_gate"], t["e_gate"], x1)
        query_projection(nc, eye, x1, t["wq_t"], qn)
        cross_attention(nc, eye, t["ctx_t"], qn, x1, t["wkv_t"], t["cross_wo_t"], (t["q_norm_w"], t["k_norm_w"]), x2)
        feed_forward(nc, eye, x2, t["w_gate"], t["w_up"], t["w_down"], g_dram, u_dram, o_dram, t["out"])


def kernel(**inputs):
    import numpy as _np
    import concourse.bacc as _bacc
    from concourse import mybir as _mybir
    from concourse.bass_utils import run_bass_kernel_spmd as _run

    a = {name: _np.asarray(v) for name, v in inputs.items()}
    freq = (_np.float32(_np.pi) ** (1 - _np.arange(0, ADH, 2, dtype=_np.float32) / ADH)).astype(_np.float32)
    theta = _np.arange(SEQ, dtype=_np.float32)[:, None] * freq[None]
    laid = {
        "x": a["x"],
        "ctx_t": a["ctx_1024"].reshape(BATCH, CT, CW, KD, P).transpose(0, 1, 4, 3, 2),
        "wqkv_t": a["L0_attn_Wqkv"].T.reshape(KD, P, 3 * D).transpose(1, 0, 2),
        "self_wo_t": a["L0_attn_Wo"].T.reshape(KD, P, D).transpose(1, 0, 2),
        "theta_base": theta.reshape(NQ, TQ, ADH // 2).transpose(1, 0, 2),
        "log_xi": a["L0_attn_log_xi"], "pi_gate": a["L0_attn_pi_gate_logit"], "e_gate": a["L0_attn_e_gate_logit"],
        "wq_t": a["L0_xattn_wq"].T.reshape(KD, P, XH * XD).transpose(1, 0, 2),
        "wkv_t": _np.concatenate([a["L0_xattn_wk"], a["L0_xattn_wv"]], 0).T.reshape(KD, P, 2 * KVW).transpose(1, 0, 2),
        "cross_wo_t": a["L0_xattn_wo"].T.reshape(2, 2, XG, XD, D).transpose(1, 3, 0, 2, 4).reshape(P, 2 * XG, D),
        "q_norm_w": a["L0_xattn_q_norm_w"], "k_norm_w": a["L0_xattn_k_norm_w"],
        "w_gate": a["L0_ffn_w_gate"], "w_up": a["L0_ffn_w_up"], "w_down": a["L0_ffn_w_down"],
    }
    nc = _bacc.Bacc("TRN2", target_bir_lowering=False, num_devices=1)
    arrays, t = {}, {}
    for name, v in laid.items():
        arrays[f"in_{name}_dram"] = v = _np.ascontiguousarray(v)
        t[name] = nc.dram_tensor(f"in_{name}_dram", v.shape, _mybir.dt.from_np(v.dtype), kind="ExternalInput").ap()
    t["out"] = nc.dram_tensor("out_0_dram", (BATCH, SEQ, D), F32, kind="ExternalOutput").ap()
    build(nc, t)
    r = _run(nc, [arrays], core_ids=[0])
    return r.results[0]["out_0_dram"]
```

```python
import math
from contextlib import ExitStack, contextmanager

import concourse.bass as bass
import concourse.mybir as mybir
import numpy as np

F32 = mybir.dt.float32
F32R = mybir.dt.float32r
I16 = mybir.dt.int16
I32 = mybir.dt.int32
ALU = mybir.AluOpType
ACT = mybir.ActivationFunctionType
AX = mybir.AxisListType
MAXIMUM = bass.bass_isa.ReduceOp.max

P = 128
BATCH, SEQ, D = 16, 224, 512
TQ = SEQ // 2
NQ = SEQ // TQ
KD = D // P
CTX = 750
LN_EPS = 1e-5
RMS_EPS = 1e-6

AH, ADH = 16, 32
GH = P // ADH
AG = AH // GH
SW = TQ + SEQ
MASKED = -1e30


def at(b, per, n):
    return b * per + n


def wait(eng, sem, value):
    if isinstance(value, int) and value <= 0:
        return
    eng.wait_ge(sem, value)


@contextmanager
def semaphores(nc):
    made = []
    with ExitStack() as ctx:
        def new_semaphore(name):
            made.append(ctx.enter_context(nc.semaphore(name)))
            return made[-1]

        yield new_semaphore
        with nc.Block() as block:
            @block.sync
            def _(sp):
                for s in made:
                    sp.sem_clear(s)


def split_matmul(pe, out, stat, mov, start, stop):
    (sh, sl), (mh, ml) = stat, mov
    pe.matmul(out, sh, mh, start=start, stop=False)
    pe.matmul(out, sl, mh, start=False, stop=False)
    return pe.matmul(out, sh, ml, start=False, stop=stop)


def bits(ap):
    return ap.bitcast(F32)


class Own:

    def __init__(self, eng, sem):
        self.eng, self.sem, self.n = eng, sem, 0

    def done(self, ins):
        ins.then_inc(self.sem, 1)
        self.n += 1
        self.eng.wait_ge(self.sem, self.n)

    def restart(self):
        self.eng.sem_clear(self.sem)
        self.n = 0


def refine_root(dve, own, root, var, tmp):
    own.done(dve.tensor_tensor(tmp, root, root, ALU.mult))
    own.done(dve.scalar_tensor_tensor(tmp, tmp, -0.5, var, ALU.mult, ALU.mult))
    own.done(dve.scalar_tensor_tensor(root, tmp, 1.5, root, ALU.add, ALU.mult))


def split_weights(nc, name, jobs):
    W = max(src.shape[-1] for src, _, _ in jobs)
    with semaphores(nc) as new_semaphore, ExitStack() as ctx:
        raw = ctx.enter_context(nc.sbuf_tensor(f"{name}_raw", [P, 2, W], F32))
        loaded = [new_semaphore(f"{name}_loaded{i}") for i in range(2)]
        high_done = new_semaphore(f"{name}_high_done")
        low_done = new_semaphore(f"{name}_low_done")
        block = ctx.enter_context(nc.Block())

        @block.sync
        def _(sp):
            for n, (src, hi, lo) in enumerate(jobs):
                wait(sp, low_done, n - 1)
                sp.dma_start(raw[:, n % 2, 0:src.shape[-1]], src).then_inc(loaded[n % 2], 16)

        @block.scalar
        def _(act):
            for n, (src, hi, lo) in enumerate(jobs):
                act.wait_ge(loaded[n % 2], 16 * (n // 2 + 1))
                act.activation(hi, raw[:, n % 2, 0:src.shape[-1]], ACT.Copy).then_inc(high_done, 1)

        @block.vector
        def _(dve):
            for n, (src, hi, lo) in enumerate(jobs):
                dve.wait_ge(high_done, n + 1)
                dve.tensor_tensor(lo, raw[:, n % 2, 0:src.shape[-1]], bits(hi), ALU.subtract).then_inc(low_done, 1)


def attention_tables(nc, theta_base, log_xi, pi_gate, e_gate, ident, cos, sin, decay, kpad):
    NF = NQ * AH * ADH // 2
    with semaphores(nc) as new_semaphore, ExitStack() as ctx:
        def sb(name, shape, dt=F32):
            return ctx.enter_context(nc.sbuf_tensor("t_" + name, shape, dt))

        def sem(name):
            return new_semaphore("t_" + name)

        base = sb("base", [TQ, NQ, ADH // 2])
        gates = sb("gates", [TQ, 3, AH])
        ex = sb("ex", [TQ, 3, AH])
        inv = sb("inv", [TQ, 3, AH])
        rate = sb("rate", [TQ, AH])
        theta = sb("theta", [TQ, NQ, AH, ADH // 2])
        turns = sb("turns", [TQ, NF])
        whole = sb("whole", [TQ, NF], I32)
        wrapped = [sb(f"wrapped{i}", [TQ, NF]) for i in range(2)]
        gap_i = sb("gap_i", [TQ, SW], I32)
        gap = sb("gap", [TQ, SW])
        ident_done, loaded, exp_done, gap_done = sem("ident_done"), sem("loaded"), sem("exp_done"), sem("gap_done")
        own_dve, wrap_done, decay_done = sem("own_dve"), sem("wrap_done"), sem("decay_done")
        block = ctx.enter_context(nc.Block())

        @block.sync
        def _(sp):
            sp.dma_start(base[:, :, :], theta_base).then_inc(loaded, 16)
            for i, g in enumerate((log_xi, pi_gate, e_gate)):
                sp.dma_start(gates[:, i, :], g.rearrange("(o h) -> o h", o=1).broadcast_to([TQ, AH])).then_inc(loaded, 16)

        @block.gpsimd
        def _(pool):
            pool.memset(ident[:, :], 0.0).then_inc(ident_done, 1)
            pool.wait_ge(ident_done, 1)
            pool.affine_select(out=ident[:, :], in_=ident[:, :], compare_op=ALU.not_equal, fill=1.0,
                               base=0, pattern=[[-1, P]], channel_multiplier=1)
            pool.iota(gap_i[:, 0:TQ], pattern=[[1, TQ]], base=0, channel_multiplier=-1).then_inc(gap_done, 1)
            pool.iota(gap_i[:, TQ:SW], pattern=[[1, SEQ]], base=-TQ, channel_multiplier=-1).then_inc(gap_done, 1)
            for i in range(2):
                for s in range(2):
                    pool.memset(bits(kpad[i][s][:, :, :]), 0.0)
            for h in range(AH):
                pool.wait_ge(decay_done, h + 1)
                pool.affine_select(out=decay[:, h, 0:TQ], in_=decay[:, h, 0:TQ], compare_op=ALU.is_ge, fill=MASKED,
                                   base=0, pattern=[[-1, TQ]], channel_multiplier=1)
                pool.affine_select(out=decay[:, h, TQ:SW], in_=decay[:, h, TQ:SW], compare_op=ALU.is_ge, fill=MASKED,
                                   base=TQ, pattern=[[-1, SEQ]], channel_multiplier=1)

        @block.scalar
        def _(act):
            act.wait_ge(loaded, 64)
            act.activation(ex[:, :, :], gates[:, :, :], ACT.Exp, scale=-1.0).then_inc(exp_done, 1)
            act.wait_ge(wrap_done, 2)
            for i, out in enumerate((sin, cos)):
                act.activation(out[:, :, :, :], wrapped[i][:, :].rearrange("p (q h f) -> p q h f", q=NQ, h=AH), ACT.Sin)

        @block.vector
        def _(dve):
            own = Own(dve, own_dve)
            dve.wait_ge(exp_done, 1)
            own.done(dve.tensor_scalar(inv[:, :, :], ex[:, :, :], 1.0, None, ALU.add))
            own.done(dve.reciprocal(inv[:, :, :], inv[:, :, :]))
            for q in range(NQ):
                own.done(dve.tensor_tensor(theta[:, q, :, :], base[:, q, None, :].broadcast_to([TQ, AH, ADH // 2]),
                                           inv[:, 1, :, None].broadcast_to([TQ, AH, ADH // 2]), ALU.mult))
            flat = theta[:, :, :, :].rearrange("p q h f -> p (q h f)")
            two_pi = [6.28125, 0.0019350051879882812, 2.0 * math.pi - 6.28125 - 0.0019350051879882812]
            for i, quarter in enumerate((0.0, 0.25)):
                own.done(dve.tensor_scalar(whole[:, :], flat, 1.0 / (2 * math.pi), quarter, ALU.mult, ALU.add))
                own.done(dve.tensor_copy(turns[:, :], whole[:, :]))
                w = wrapped[i][:, :]
                own.done(dve.scalar_tensor_tensor(w, turns[:, :], -two_pi[0], flat, ALU.mult, ALU.add))
                own.done(dve.scalar_tensor_tensor(w, turns[:, :], -two_pi[1], w, ALU.mult, ALU.add))
                own.done(dve.scalar_tensor_tensor(w, turns[:, :], -two_pi[2], w, ALU.mult, ALU.add))
                own.done(dve.tensor_scalar(w, w, quarter * 2 * math.pi, 3.1415925, ALU.add, ALU.min))
                dve.tensor_scalar(w, w, -3.1415925, None, ALU.max).then_inc(wrap_done, 1)
            own.done(dve.tensor_tensor(rate[:, :], ex[:, 0, :], inv[:, 2, :], ALU.mult))
            own.done(dve.tensor_scalar(rate[:, :], rate[:, :], math.sqrt(ADH), None, ALU.mult))
            dve.wait_ge(gap_done, 2)
            own.done(dve.tensor_copy(gap[:, :], gap_i[:, :]))
            for h in range(AH):
                dve.tensor_scalar(decay[:, h, :], gap[:, :], rate[:, h:h + 1], None, ALU.mult).then_inc(decay_done, 1)


def self_attention(nc, ident, x, wqkv_t, wo_t, theta_base, log_xi, pi_gate, e_gate, x1, NB=BATCH):
    SCALE = 1.0 / math.sqrt(ADH)
    NW = 3 * D
    x_v = x.rearrange("b (q p) d -> b p q d", p=TQ)
    x1_v = x1.rearrange("b (q p) d -> b p q d", p=TQ)
    with semaphores(nc) as new_semaphore, ExitStack() as ctx:
        def sb(name, shape, dt=F32):
            return ctx.enter_context(nc.sbuf_tensor("a_" + name, shape, dt))

        def pair(name, shape):
            return [sb(f"{name}_{s}", shape, F32R) for s in ("high", "low")]

        def sem(name):
            return new_semaphore("a_" + name)

        wqkv = pair("wqkv", [P, KD, NW])
        wo = pair("wo", [P, KD, D])
        cos = sb("cos", [TQ, NQ, AH, ADH // 2])
        sin = sb("sin", [TQ, NQ, AH, ADH // 2])
        decay = sb("decay", [TQ, AH, SW])
        kpad = [pair(f"kpad{i}", [P, GH, SEQ]) for i in range(2)]

        split_weights(nc, "a_w", [(wqkv_t[:, k, :], wqkv[0][:, k, :], wqkv[1][:, k, :]) for k in range(KD)]
                      + [(wo_t[:, k, :], wo[0][:, k, :], wo[1][:, k, :]) for k in range(KD)])
        attention_tables(nc, theta_base, log_xi, pi_gate, e_gate, ident, cos, sin, decay, kpad)

        xn = sb("xn", [TQ, NQ, D])
        stats = sb("stats", [TQ, NQ, 6])
        moments = sb("moments", [TQ, NQ, 2])
        var = sb("var", [TQ, NQ])
        root = sb("root", [TQ, NQ])
        newton = sb("newton", [TQ, NQ])
        xnt = pair("xnt", [P, KD, SEQ])
        rot_a = sb("rot_a", [TQ, 2, D])
        rot_b = sb("rot_b", [TQ, 2, D])
        qk = [sb(f"qk{i}", [TQ, 2, NQ, D]) for i in range(2)]
        v = [pair(f"v{i}", [TQ, NQ, D]) for i in range(2)]
        qt_ = [pair(f"qt{i}", [P, SEQ]) for i in range(2)]
        prob = [sb(f"prob{i}", [TQ, GH, SW]) for i in range(2)]
        neg_max = sb("neg_max", [TQ, NQ, GH])
        total = sb("total", [TQ, NQ, GH])
        inv_total = sb("inv_total", [TQ, NQ, GH])
        probt = pair("probt", [TQ, NQ, GH, SEQ])
        attnt = pair("attnt", [P, AG, SEQ])
        xres = sb("xres", [TQ, NQ, D])
        xout = sb("xout", [TQ, NQ, D])

        score_bank = [ctx.enter_context(nc.psum_tensor(f"a_score{i}", [P, 512], F32)) for i in range(3)]
        turn_bank = [ctx.enter_context(nc.psum_tensor(f"a_turn{i}", [P, 512], F32)) for i in range(2)]
        pv_bank = [ctx.enter_context(nc.psum_tensor(f"a_pv{i}", [P, 512], F32)) for i in range(2)]
        piece_bank = ctx.enter_context(nc.psum_tensor("a_piece", [P, 512], F32))

        x_in, res_in, x1_out = sem("x_in"), sem("res_in"), sem("x1_out")
        var_done, root_done, norm_done = sem("var_done"), sem("root_done"), sem("norm_done")
        xt_done, xt_high, xt_low = sem("xt_done"), sem("xt_high"), sem("xt_low")
        proj_done, proj_read, v_high = sem("proj_done"), sem("proj_read"), sem("v_high")
        rot_done = sem("rot_done")
        qkt_done, qkt_high, qkt_low = sem("qkt_done"), sem("qkt_high"), sem("qkt_low")
        score_done, score_read = sem("score_done"), sem("score_read")
        max_done, exp_done, recip_done, prob_done = sem("max_done"), sem("exp_done"), sem("recip_done"), sem("prob_done")
        turn_done, turn_high, turn_low = sem("turn_done"), sem("turn_high"), sem("turn_low")
        pv_done, pv_high, pv_low = sem("pv_done"), sem("pv_high"), sem("pv_low")
        wo_done, wo_read = sem("wo_done"), sem("wo_read")
        own_dve, own_act, own_pool = sem("own_dve"), sem("own_act"), sem("own_pool")

        PIECES = [[("x", 0), ("x", 1), ("qkt", 1), ("proj", 0)],
                  [("wo", 0), ("wo", 1), ("qkt", 2), ("proj", 1)],
                  [("proj", 2), ("proj", 3), ("qkt", 3)],
                  [("proj", 4), ("proj", 5), ("qkt", 0)]]

        def steps(eng, front0, slot, last, restart):
            front0()
            for g in range(AG):
                slot(0, g, 0, True, False)
            if NB > 2:
                with eng.Fori(0, (NB - 2) // 2) as j:
                    restart()
                    for u in range(2):
                        for g in range(AG):
                            slot(2 * j + 1 + u, g, (1 + u) % 2, True, True)
            for g in range(AG):
                slot(NB - 1, g, (NB - 1) % 2, False, True)
            last()

        block = ctx.enter_context(nc.Block())

        @block.sync
        def _(sp):
            def load_x(f):
                wait(sp, xt_done, at(f - 1, 2, 2) if not (isinstance(f, int) and f == 0) else 0)
                sp.dma_start(xn[:, :, :], x_v[f]).then_inc(x_in, 16)

            def slot(b, g, par, front, back):
                if g == 0:
                    if front:
                        load_x(b + 1)
                if g == 1 and back:
                    store(b - 1)

            def store(b):
                if not (isinstance(b, int) and b == 0):
                    sp.wait_ge(wo_read, at(b - 1, 2, 2))
                sp.dma_start(xres[:, :, :], x_v[b]).then_inc(res_in, 16)
                sp.wait_ge(wo_read, at(b, 2, 2))
                sp.dma_start(x1_v[b], xout[:, :, :]).then_inc(x1_out, 16)

            steps(sp, lambda: load_x(0), slot, lambda: store(NB - 1), lambda: None)
            sp.wait_ge(x1_out, 16 * NB)

        @block.tensor
        def _(pe):
            held = [None]

            def take_bank(sem_, value):
                if held[0]:
                    pe.wait_ge(*held[0])
                held[0] = (sem_, value)

            def turn_x(f, q):
                pe.wait_ge(norm_done, f + 1)
                take_bank(xt_low, at(f, 2, q + 1))
                for k in range(KD):
                    m = pe.transpose(piece_bank[:, k * TQ:(k + 1) * TQ], xn[:, q, k * P:(k + 1) * P], ident[0:TQ, 0:TQ])
                m.then_inc(xt_done, 1)

            def project(f, n):
                q, part = n % 2, n // 2
                pe.wait_ge(xt_low, at(f, 2, 2))
                take_bank(proj_read, at(f, 6, n + 1))
                for k in range(KD):
                    m = split_matmul(pe, piece_bank[0:TQ, 0:D], [t[:, k, q * TQ:(q + 1) * TQ] for t in xnt],
                                     [t[:, k, part * D:(part + 1) * D] for t in wqkv], k == 0, k == KD - 1)
                m.then_inc(proj_done, 1)

            def turn_qk(b, g, par):
                pe.wait_ge(rot_done, at(b, 4, 4))
                take_bank(qkt_low, at(b, 4, g + 1))
                for s in range(2):
                    for q in range(NQ):
                        m = pe.transpose(piece_bank[:, (s * NQ + q) * TQ:(s * NQ + q + 1) * TQ],
                                         qk[par][:, s, q, g * P:(g + 1) * P], ident[0:TQ, 0:TQ])
                m.then_inc(qkt_done, 1)

            def output(b, q):
                pe.wait_ge(pv_low, at(b, 8, 8))
                take_bank(wo_read, at(b, 2, q + 1))
                for k in range(AG):
                    m = split_matmul(pe, piece_bank[0:TQ, 0:D], [t[:, k, q * TQ:(q + 1) * TQ] for t in attnt],
                                     [t[:, k, :] for t in wo], k == 0, k == AG - 1)
                m.then_inc(wo_done, 1)

            def piece(b, par, kind, n, front, back):
                if kind == "x" and front:
                    turn_x(b + 1, n)
                elif kind == "proj" and front:
                    project(b + 1, n)
                elif kind == "wo" and back:
                    output(b - 1, n)
                elif kind == "qkt" and n:
                    turn_qk(b, n, par)
                elif kind == "qkt" and front:
                    turn_qk(b + 1, 0, 1 - par)

            def scores(b, g):
                i = g % 2
                pe.wait_ge(qkt_low, at(b, 4, g + 1))
                tiles = [(0, 0, GH, TQ), (1, 0, 2, SEQ), (1, 2, 4, SEQ)]
                for n, (q, h0, h1, keys) in enumerate(tiles):
                    wait(pe, score_read, at(b, 12, 3 * (g - 1) + n + 1))
                    out = score_bank[n][0:TQ, 0:(h1 - h0) * keys].rearrange("p (h k) -> p h k", k=keys)
                    split_matmul(pe, out, [t[:, q * TQ:(q + 1) * TQ] for t in qt_[i]],
                                 [t[:, h0:h1, 0:keys] for t in kpad[i]], True, True).then_inc(score_done, 1)

            def turn_prob(b, g, n):
                wait(pe, turn_low, at(b, 12, 3 * g + n - 1))
                pe.wait_ge(prob_done, at(b, 8, 2 * g + 2))
                bank, pr = turn_bank[(3 * g + n) % 2], prob[g % 2]
                if n < 2:
                    for h in range(2 * n, 2 * n + 2):
                        for q in range(NQ):
                            c = (h % 2) * SEQ + q * TQ
                            m = pe.transpose(bank[0:TQ, c:c + TQ], pr[:, h, q * TQ:(q + 1) * TQ], ident[0:TQ, 0:TQ])
                else:
                    for h in range(GH):
                        m = pe.transpose(bank[0:TQ, h * TQ:(h + 1) * TQ], pr[:, h, 2 * TQ:3 * TQ], ident[0:TQ, 0:TQ])
                m.then_inc(turn_done, 1)

            def weigh_values(b, g, par, n):
                pe.wait_ge(turn_low, at(b, 12, 3 * g + 3))
                wait(pe, pv_low, at(b, 8, 2 * (g - 1) + n + 1))
                for t in range(NQ):
                    m = split_matmul(pe, pv_bank[n][:, 0:2 * SEQ].rearrange("p (h k) -> p h k", k=SEQ),
                                     [s[:, t, g * P:(g + 1) * P] for s in v[par]],
                                     [s[:, t, 2 * n:2 * n + 2, :] for s in probt], t == 0, t == NQ - 1)
                m.then_inc(pv_done, 1)

            def slot(b, g, par, front, back):
                if g == 0:
                    held[0] = (qkt_low, at(b, 4, 1))
                scores(b, g)
                pieces = PIECES[g]
                pb, pg, pp = (b, g - 1, par) if g else (b - 1, AG - 1, 1 - par)
                late = g or back
                piece(b, par, *pieces[0], front, back)
                if late:
                    turn_prob(pb, pg, 0)
                    turn_prob(pb, pg, 1)
                piece(b, par, *pieces[1], front, back)
                if late:
                    turn_prob(pb, pg, 2)
                for pc in pieces[2:3]:
                    piece(b, par, *pc, front, back)
                if late:
                    weigh_values(pb, pg, pp, 0)
                    weigh_values(pb, pg, pp, 1)
                for pc in pieces[3:]:
                    piece(b, par, *pc, front, back)

            def front0():
                for q in range(NQ):
                    turn_x(0, q)
                for n in range(6):
                    project(0, n)
                turn_qk(0, 0, 0)

            def last():
                par = (NB - 1) % 2
                for n in range(3):
                    turn_prob(NB - 1, AG - 1, n)
                for n in range(2):
                    weigh_values(NB - 1, AG - 1, par, n)
                for q in range(NQ):
                    output(NB - 1, q)

            steps(pe, front0, slot, last, lambda: None)

        @block.scalar
        def _(act):
            own = Own(act, own_act)

            def root_guess(f):
                act.wait_ge(var_done, f + 1)
                own.done(act.activation(root[:, :], var[:, :], ACT.Ln))
                act.activation(root[:, :], root[:, :], ACT.Exp, scale=-0.5).then_inc(root_done, 1)

            def high_x(f, q):
                act.wait_ge(xt_done, at(f, 2, q + 1))
                wait(act, proj_done, at(f - 1, 6, 6))
                act.activation(xnt[0][:, :, q * TQ:(q + 1) * TQ], piece_bank[:, 0:KD * TQ].rearrange("p (k t) -> p k t", k=KD),
                               ACT.Copy).then_inc(xt_high, 1)

            def high_v(f, q, par):
                act.wait_ge(proj_done, at(f, 6, 4 + q + 1))
                act.activation(v[par][0][:, q, :], piece_bank[0:TQ, 0:D], ACT.Copy).then_inc(v_high, 1)

            def high_qk(b, g):
                i = g % 2
                act.wait_ge(qkt_done, at(b, 4, g + 1))
                wait(act, score_done, at(b, 12, 3 * (g - 1)))
                act.activation(qt_[i][0][:, :], piece_bank[:, 0:SEQ], ACT.Copy)
                for h in range(GH):
                    r = slice(h * ADH, (h + 1) * ADH)
                    m = act.activation(kpad[i][0][r, h, :], piece_bank[r, SEQ:2 * SEQ], ACT.Copy)
                m.then_inc(qkt_high, 1)

            def exponents(b, g):
                i = g % 2
                act.wait_ge(max_done, at(b, 4, g + 1))
                wait(act, recip_done, at(b, 4, g))
                for q in range(NQ):
                    for h in range(GH):
                        c = slice(0, TQ) if q == 0 else slice(TQ, SW)
                        act.activation(prob[i][:, h, c], prob[i][:, h, c], ACT.Exp, bias=neg_max[:, q, h:h + 1],
                                       scale=SCALE, accum_out=total[:, q, h:h + 1]).then_inc(exp_done, 1)

            def high_prob(b, g, n):
                act.wait_ge(turn_done, at(b, 12, 3 * g + n + 1))
                wait(act, pv_done, at(b, 8, 2 * g))
                bank = turn_bank[(3 * g + n) % 2]
                if n < 2:
                    act.activation(probt[0][:, 0, 2 * n:2 * n + 2, :], bank[0:TQ, 0:2 * SEQ].rearrange("p (h k) -> p h k", h=2),
                                   ACT.Copy).then_inc(turn_high, 1)
                else:
                    act.activation(probt[0][:, 1, :, TQ:SEQ], bank[0:TQ, 0:GH * TQ].rearrange("p (h k) -> p h k", h=GH),
                                   ACT.Copy).then_inc(turn_high, 1)

            def high_attn(b, g, n):
                act.wait_ge(pv_done, at(b, 8, 2 * g + n + 1))
                wait(act, wo_done, at(b - 1, 2, 2))
                for h in range(2 * n, 2 * n + 2):
                    r = slice(h * ADH, (h + 1) * ADH)
                    m = act.activation(attnt[0][r, g, :], pv_bank[n][r, (h % 2) * SEQ:(h % 2 + 1) * SEQ], ACT.Copy)
                m.then_inc(pv_high, 1)

            def piece(b, par, kind, n, front, back):
                if kind == "x" and front:
                    high_x(b + 1, n)
                elif kind == "proj" and front and n >= 4:
                    high_v(b + 1, n - 4, 1 - par)
                elif kind == "qkt" and n:
                    high_qk(b, n)
                elif kind == "qkt" and front:
                    high_qk(b + 1, 0)

            def slot(b, g, par, front, back):
                if g == 0 and front:
                    root_guess(b + 1)
                exponents(b, g)
                pieces = PIECES[g]
                pb, pg = (b, g - 1) if g else (b - 1, AG - 1)
                late = g or back
                piece(b, par, *pieces[0], front, back)
                if late:
                    high_prob(pb, pg, 0)
                    high_prob(pb, pg, 1)
                piece(b, par, *pieces[1], front, back)
                if late:
                    high_prob(pb, pg, 2)
                piece(b, par, *pieces[2], front, back)
                if late:
                    high_attn(pb, pg, 0)
                    high_attn(pb, pg, 1)
                for pc in pieces[3:]:
                    piece(b, par, *pc, front, back)

            def front0():
                root_guess(0)
                for q in range(NQ):
                    high_x(0, q)
                for q in range(NQ):
                    high_v(0, q, 0)
                high_qk(0, 0)

            def last():
                for n in range(3):
                    high_prob(NB - 1, AG - 1, n)
                for n in range(2):
                    high_attn(NB - 1, AG - 1, n)

            act.preload_act_table_set("natural_log_exp_and_others")
            steps(act, front0, slot, last, own.restart)

        @block.vector
        def _(dve):
            own = Own(dve, own_dve)

            def variance(f):
                dve.wait_ge(x_in, at(f, 16, 16))
                for q in range(NQ):
                    m = dve.bn_stats(stats[:, q, :], xn[:, q, :])
                own.done(m)
                for q in range(NQ):
                    m = dve.bn_aggr(moments[:, q, :], stats[:, q, :])
                own.done(m)
                dve.tensor_scalar(var[:, :], moments[:, :, 1], LN_EPS, None, ALU.add).then_inc(var_done, 1)

            def normalise(f):
                dve.wait_ge(root_done, f + 1)
                refine_root(dve, own, root[:, :], var[:, :], newton[:, :])
                for q in range(NQ):
                    m = dve.tensor_scalar(xn[:, q, :], xn[:, q, :], moments[:, q, 0:1], root[:, q:q + 1],
                                          ALU.subtract, ALU.mult)
                m.then_inc(norm_done, 1)

            def low_x(f, q):
                dve.wait_ge(xt_high, at(f, 2, q + 1))
                dve.tensor_tensor(xnt[1][:, :, q * TQ:(q + 1) * TQ], piece_bank[:, 0:KD * TQ].rearrange("p (k t) -> p k t", k=KD),
                                  bits(xnt[0][:, :, q * TQ:(q + 1) * TQ]), ALU.subtract).then_inc(xt_low, 1)

            def rotate(f, n):
                q, i = n % 2, n % 2
                dve.wait_ge(proj_done, at(f, 6, n + 1))
                wait(dve, rot_done, at(f, 4, n - 1))
                src = piece_bank[0:TQ, 0:D].rearrange("p (g e) -> p g e", e=2)
                a = rot_a[:, i, :].rearrange("p (g e) -> p g e", e=2)
                r = rot_b[:, i, :].rearrange("p (g e) -> p g e", e=2)
                c = cos[:, q, :, :].rearrange("p h f -> p (h f)")
                s = sin[:, q, :, :].rearrange("p h f -> p (h f)")
                dve.tensor_tensor(a, src, c[:, :, None].broadcast_to([TQ, D // 2, 2]), ALU.mult)
                dve.scalar_tensor_tensor(r[:, :, 0], src[:, :, 1], -1.0, s, ALU.mult, ALU.mult)
                dve.tensor_tensor(r[:, :, 1], src[:, :, 0], s, ALU.mult).then_inc(proj_read, 1)

            def low_v(f, q, par):
                dve.wait_ge(v_high, at(f, 2, q + 1))
                dve.tensor_tensor(v[par][1][:, q, :], piece_bank[0:TQ, 0:D], bits(v[par][0][:, q, :]),
                                  ALU.subtract).then_inc(proj_read, 1)

            def low_qk(b, g):
                i = g % 2
                dve.wait_ge(qkt_high, at(b, 4, g + 1))
                dve.tensor_tensor(qt_[i][1][:, :], piece_bank[:, 0:SEQ], bits(qt_[i][0][:, :]), ALU.subtract)
                for h in range(GH):
                    r = slice(h * ADH, (h + 1) * ADH)
                    m = dve.tensor_tensor(kpad[i][1][r, h, :], piece_bank[r, SEQ:2 * SEQ], bits(kpad[i][0][r, h, :]),
                                          ALU.subtract)
                m.then_inc(qkt_low, 1)

            def residual(b, q):
                dve.wait_ge(wo_done, at(b, 2, q + 1))
                if q == 0:
                    dve.wait_ge(res_in, at(b, 16, 16))
                    wait(dve, x1_out, at(b, 16, 0))
                dve.tensor_tensor(xout[:, q, :], piece_bank[0:TQ, 0:D], xres[:, q, :], ALU.add).then_inc(wo_read, 1)

            def maxima(b, g):
                i = g % 2
                pr = prob[i]
                wait(dve, turn_done, at(b, 12, 3 * (g - 1)))
                spans = [(0, GH, 0, TQ), (0, 2, TQ, SW), (2, 4, TQ, SW)]
                for n, (h0, h1, c0, c1) in enumerate(spans):
                    dve.wait_ge(score_done, at(b, 12, 3 * g + n + 1))
                    src = score_bank[n][0:TQ, 0:(h1 - h0) * (c1 - c0)].rearrange("p (h k) -> p h k", h=h1 - h0)
                    dve.tensor_tensor(pr[:, h0:h1, c0:c1], src, decay[:, GH * g + h0:GH * g + h1, c0:c1],
                                      ALU.add).then_inc(score_read, 1)
                dve.wait_ge(score_read, at(b, 12, 3 * g + 3))
                wait(dve, exp_done, at(b, 32, 8 * g))
                dve.tensor_reduce(neg_max[:, 0, :], pr[:, :, 0:TQ], AX.X, ALU.max, negate=True)
                own.done(dve.tensor_reduce(neg_max[:, 1, :], pr[:, :, TQ:SW], AX.X, ALU.max, negate=True))
                dve.tensor_scalar(neg_max[:, :, :], neg_max[:, :, :], SCALE, None, ALU.mult).then_inc(max_done, 1)

            def reciprocals(b, g):
                dve.wait_ge(exp_done, at(b, 32, 8 * g + 8))
                wait(dve, prob_done, at(b, 8, 2 * g))
                dve.reciprocal(inv_total[:, :, :], total[:, :, :]).then_inc(recip_done, 1)

            def low_prob(b, g, n):
                dve.wait_ge(turn_high, at(b, 12, 3 * g + n + 1))
                bank = turn_bank[(3 * g + n) % 2]
                if n < 2:
                    dst, hi = [t[:, 0, 2 * n:2 * n + 2, :] for t in (probt[1], probt[0])]
                    src = bank[0:TQ, 0:2 * SEQ].rearrange("p (h k) -> p h k", h=2)
                else:
                    dst, hi = [t[:, 1, :, TQ:SEQ] for t in (probt[1], probt[0])]
                    src = bank[0:TQ, 0:GH * TQ].rearrange("p (h k) -> p h k", h=GH)
                dve.tensor_tensor(dst, src, bits(hi), ALU.subtract).then_inc(turn_low, 1)

            def low_attn(b, g, n):
                dve.wait_ge(pv_high, at(b, 8, 2 * g + n + 1))
                for h in range(2 * n, 2 * n + 2):
                    r = slice(h * ADH, (h + 1) * ADH)
                    m = dve.tensor_tensor(attnt[1][r, g, :], pv_bank[n][r, (h % 2) * SEQ:(h % 2 + 1) * SEQ],
                                          bits(attnt[0][r, g, :]), ALU.subtract)
                m.then_inc(pv_low, 1)

            def piece(b, par, kind, n, front, back):
                if kind == "x" and front:
                    low_x(b + 1, n)
                elif kind == "proj" and front and n < 4:
                    rotate(b + 1, n)
                elif kind == "proj" and front:
                    low_v(b + 1, n - 4, 1 - par)
                elif kind == "wo" and back:
                    residual(b - 1, n)
                elif kind == "qkt" and n:
                    low_qk(b, n)
                elif kind == "qkt" and front:
                    low_qk(b + 1, 0)

            def slot(b, g, par, front, back):
                if g == 0 and front:
                    variance(b + 1)
                maxima(b, g)
                if g == 0 and front:
                    normalise(b + 1)
                pieces = PIECES[g]
                pb, pg = (b, g - 1) if g else (b - 1, AG - 1)
                late = g or back
                piece(b, par, *pieces[0], front, back)
                if late:
                    low_prob(pb, pg, 0)
                    low_prob(pb, pg, 1)
                reciprocals(b, g)
                piece(b, par, *pieces[1], front, back)
                if late:
                    low_prob(pb, pg, 2)
                piece(b, par, *pieces[2], front, back)
                if late:
                    low_attn(pb, pg, 0)
                    low_attn(pb, pg, 1)
                for pc in pieces[3:]:
                    piece(b, par, *pc, front, back)

            def front0():
                for s in probt:
                    dve.memset(bits(s[:, 1, :, 0:TQ]), 0.0)
                variance(0)
                normalise(0)
                for q in range(NQ):
                    low_x(0, q)
                for n in range(4):
                    rotate(0, n)
                for q in range(NQ):
                    low_v(0, q, 0)
                low_qk(0, 0)

            def last():
                for n in range(3):
                    low_prob(NB - 1, AG - 1, n)
                for n in range(2):
                    low_attn(NB - 1, AG - 1, n)
                for q in range(NQ):
                    residual(NB - 1, q)

            steps(dve, front0, slot, last, own.restart)

        @block.gpsimd
        def _(pool):
            def add_rotated(f, n, par):
                i = n % 2
                pool.wait_ge(proj_read, at(f, 6, n + 1))
                pool.tensor_tensor(qk[par][:, n // 2, n % 2, :], rot_a[:, i, :], rot_b[:, i, :], ALU.add).then_inc(rot_done, 1)

            def divide(b, g):
                pool.wait_ge(recip_done, at(b, 4, g + 1))
                pr = prob[g % 2]
                for q, (c0, c1) in enumerate(((0, TQ), (TQ, SW))):
                    pool.tensor_tensor(pr[:, :, c0:c1], pr[:, :, c0:c1], inv_total[:, q, :, None].broadcast_to([TQ, GH, c1 - c0]),
                                       ALU.mult).then_inc(prob_done, 1)

            def slot(b, g, par, front, back):
                first = [n for kind, n in PIECES[g][:2] if kind == "proj" and n < 4]
                rest = [n for kind, n in PIECES[g][2:] if kind == "proj" and n < 4]
                if front:
                    for n in (first if g != 2 else first[:1]):
                        add_rotated(b + 1, n, 1 - par)
                divide(b, g)
                if front:
                    for n in (rest if g != 2 else first[1:] + rest):
                        add_rotated(b + 1, n, 1 - par)

            def front0():
                for n in range(4):
                    add_rotated(0, n, 0)

            steps(pool, front0, slot, lambda: None, lambda: None)


XH, XD = 16, 64
KVH = 4
XG = XH // KVH
NT = BATCH * SEQ // P


def query_projection(nc, ident, x1, wq_t, qn, TILES=NT):
    NWQ = XH * XD
    HALF = 512
    x_v = x1.rearrange("b s d -> (b s) d").rearrange("(t p) d -> t p d", p=P)
    q_v = qn.rearrange("b s d -> (b s) d").rearrange("(t p) d -> t p d", p=P)
    with semaphores(nc) as new_semaphore, ExitStack() as ctx:
        def sb(name, shape, dt=F32):
            return ctx.enter_context(nc.sbuf_tensor("q_" + name, shape, dt))

        def pair(name, shape):
            return [sb(f"{name}_{s}", shape, F32R) for s in ("high", "low")]

        def sem(name):
            return new_semaphore("q_" + name)

        wq = pair("wq", [P, KD, NWQ])
        split_weights(nc, "q_w", [(wq_t[:, k, :], wq[0][:, k, :], wq[1][:, k, :]) for k in range(KD)])
        xb = [sb(f"x{i}", [P, D]) for i in range(2)]
        stats = sb("stats", [P, 6])
        moments = sb("moments", [P, 2])
        var, root, newton = sb("var", [P, 1]), sb("root", [P, 1]), sb("newton", [P, 1])
        xnt = [pair(f"xnt{i}", [P, KD, P]) for i in range(2)]
        raw = [sb(f"raw{i}", [P, XH, XD]) for i in range(2)]
        square = sb("square", [P, XH, XD])
        mean_sq = sb("mean_sq", [P, XH])
        q_root, q_newton = sb("q_root", [P, XH]), sb("q_newton", [P, XH])
        turn_bank = [ctx.enter_context(nc.psum_tensor(f"q_turn{i}", [P, 512], F32)) for i in range(2)]
        proj_bank = [ctx.enter_context(nc.psum_tensor(f"q_proj{i}", [P, 512], F32)) for i in range(4)]

        x_in = [sem(f"x_in{i}") for i in range(2)]
        q_out = [sem(f"q_out{i}") for i in range(2)]
        var_done, root_done, norm_done = sem("var_done"), sem("root_done"), sem("norm_done")
        xt_done, xt_high, xt_low = sem("xt_done"), sem("xt_high"), sem("xt_low")
        proj_done, raw_done = sem("proj_done"), sem("raw_done")
        square_done, mean_done, q_root_done, refined, scaled = (
            sem("square_done"), sem("mean_done"), sem("q_root_done"), sem("refined"), sem("scaled"))
        own_dve, own_act = sem("own_dve"), sem("own_act")

        def steps(eng, front0, step, last, restart=lambda: None):
            front0()
            step(0, 0, True, False)
            step(1, 1, True, True)
            with eng.Fori(0, (TILES - 4) // 2) as j:
                restart()
                for u in range(2):
                    step(2 * j + 2 + u, u, True, True)
            step(TILES - 2, 0, True, True)
            step(TILES - 1, 1, False, True)
            last()

        block = ctx.enter_context(nc.Block())

        @block.sync
        def _(sp):
            def load(t, par):
                wait(sp, xt_done, t - 1)
                sp.dma_start(xb[par][:, :], x_v[t]).then_inc(x_in[par], 16)

            def store(t, par):
                sp.wait_ge(scaled, t + 1)
                sp.dma_start(q_v[t], raw[par][:, :, :].rearrange("p h d -> p (h d)")).then_inc(q_out[par], 16)

            def step(t, par, front, back):
                if front:
                    load(t + 1, 1 - par)
                if back:
                    store(t - 1, 1 - par)

            steps(sp, lambda: load(0, 0), step, lambda: store(TILES - 1, (TILES - 1) % 2))
            for par in range(2):
                sp.wait_ge(q_out[par], 16 * (TILES // 2))

        def half(t):
            return t // 2

        @block.tensor
        def _(pe):
            def turn(t, par):
                pe.wait_ge(norm_done, t + 1)
                wait(pe, xt_low, t - 1)
                for k in range(KD):
                    m = pe.transpose(turn_bank[par][:, k * P:(k + 1) * P], xb[par][:, k * P:(k + 1) * P], ident)
                m.then_inc(xt_done, 1)

            def project(t, par, n):
                pe.wait_ge(xt_low, t + 1)
                wait(pe, raw_done, at(t - 2, 2, n + 1))
                for k in range(KD):
                    m = split_matmul(pe, proj_bank[2 * par + n][:, 0:HALF], [s[:, k, :] for s in xnt[par]],
                                     [s[:, k, n * HALF:(n + 1) * HALF] for s in wq], k == 0, k == KD - 1)
                m.then_inc(proj_done, 1)

            def step(t, par, front, back):
                project(t, par, 0)
                if front:
                    turn(t + 1, 1 - par)
                project(t, par, 1)

            steps(pe, lambda: turn(0, 0), step, lambda: None)

        @block.scalar
        def _(act):
            own = Own(act, own_act)

            def root_guess(t):
                act.wait_ge(var_done, t + 1)
                own.done(act.activation(root[:, :], var[:, :], ACT.Ln))
                act.activation(root[:, :], root[:, :], ACT.Exp, scale=-0.5).then_inc(root_done, 1)

            def q_root_guess(t):
                act.wait_ge(mean_done, t + 1)
                own.done(act.activation(q_root[:, :], mean_sq[:, :], ACT.Ln))
                act.activation(q_root[:, :], q_root[:, :], ACT.Exp, scale=-0.5).then_inc(q_root_done, 1)

            def high(t, par):
                act.wait_ge(xt_done, t + 1)
                wait(act, proj_done, at(t - 2, 2, 2))
                act.activation(xnt[par][0][:, :, :], turn_bank[par][:, :].rearrange("p (k t) -> p k t", k=KD),
                               ACT.Copy).then_inc(xt_high, 1)

            def copy_raw(t, par, n):
                act.wait_ge(proj_done, at(t, 2, n + 1))
                if n == 0 and not (isinstance(t, int) and t < 2):
                    act.wait_ge(q_out[par], 16 * half(t))
                hh = XH // 2
                act.activation(raw[par][:, n * hh:(n + 1) * hh, :],
                               proj_bank[2 * par + n][:, :].rearrange("p (h d) -> p h d", h=hh),
                               ACT.Copy).then_inc(raw_done, 1)

            def step(t, par, front, back):
                if front:
                    root_guess(t + 1)
                if back:
                    q_root_guess(t - 1)
                copy_raw(t, par, 0)
                if front:
                    high(t + 1, 1 - par)
                copy_raw(t, par, 1)

            def front0():
                root_guess(0)
                high(0, 0)

            act.preload_act_table_set("natural_log_exp_and_others")
            steps(act, front0, step, lambda: q_root_guess(TILES - 1), own.restart)

        @block.vector
        def _(dve):
            own = Own(dve, own_dve)

            def variance(t, par):
                dve.wait_ge(x_in[par], 16 * half(t) + 16)
                own.done(dve.bn_stats(stats[:, :], xb[par][:, :]))
                own.done(dve.bn_aggr(moments[:, :], stats[:, :]))
                dve.tensor_scalar(var[:, :], moments[:, 1:2], LN_EPS, None, ALU.add).then_inc(var_done, 1)

            def normalise(t, par):
                dve.wait_ge(root_done, t + 1)
                refine_root(dve, own, root[:, :], var[:, :], newton[:, :])
                dve.tensor_scalar(xb[par][:, :], xb[par][:, :], moments[:, 0:1], root[:, 0:1],
                                  ALU.subtract, ALU.mult).then_inc(norm_done, 1)

            def low(t, par):
                dve.wait_ge(xt_high, t + 1)
                dve.tensor_tensor(xnt[par][1][:, :, :], turn_bank[par][:, :].rearrange("p (k t) -> p k t", k=KD),
                                  bits(xnt[par][0][:, :, :]), ALU.subtract).then_inc(xt_low, 1)

            def mean_square(t):
                dve.wait_ge(square_done, t + 1)
                own.done(dve.tensor_reduce(mean_sq[:, :], square[:, :, :], AX.X, ALU.add))
                dve.tensor_scalar(mean_sq[:, :], mean_sq[:, :], 1.0 / XD, RMS_EPS, ALU.mult, ALU.add).then_inc(mean_done, 1)

            def refine(t):
                dve.wait_ge(q_root_done, t + 1)
                own.done(dve.tensor_tensor(q_newton[:, :], q_root[:, :], q_root[:, :], ALU.mult))
                own.done(dve.scalar_tensor_tensor(q_newton[:, :], q_newton[:, :], -0.5, mean_sq[:, :], ALU.mult, ALU.mult))
                dve.scalar_tensor_tensor(q_root[:, :], q_newton[:, :], 1.5, q_root[:, :], ALU.add, ALU.mult).then_inc(refined, 1)

            def step(t, par, front, back):
                if front:
                    variance(t + 1, 1 - par)
                if back:
                    mean_square(t - 1)
                if front:
                    normalise(t + 1, 1 - par)
                if back:
                    refine(t - 1)
                if front:
                    low(t + 1, 1 - par)

            def front0():
                variance(0, 0)
                normalise(0, 0)
                low(0, 0)

            def last():
                mean_square(TILES - 1)
                refine(TILES - 1)

            steps(dve, front0, step, last, own.restart)

        @block.gpsimd
        def _(pool):
            def squares(t, par):
                pool.wait_ge(raw_done, at(t, 2, 2))
                wait(pool, mean_done, t)
                pool.tensor_tensor(square[:, :, :], raw[par][:, :, :], raw[par][:, :, :], ALU.mult).then_inc(square_done, 1)

            def scale(t, par):
                pool.wait_ge(refined, t + 1)
                pool.tensor_tensor(raw[par][:, :, :], raw[par][:, :, :], q_root[:, :, None].broadcast_to([P, XH, XD]),
                                   ALU.mult).then_inc(scaled, 1)

            def step(t, par, front, back):
                if back:
                    scale(t - 1, 1 - par)
                squares(t, par)

            steps(pool, lambda: None, step, lambda: scale(TILES - 1, (TILES - 1) % 2))


CW = 125
CT = CTX // CW
KVW = KVH * XD
KROWS = XD + 4


def cross_attention(nc, ident, ctx_t, qn, x1, wkv_t, wo_t, norm_w, x2, NB=BATCH):
    q_v = qn.rearrange("b (q p) (h d) -> b p q h d", p=TQ, d=XD)
    x1_v = x1.rearrange("b (q p) d -> b p q d", p=TQ)
    x2_v = x2.rearrange("b (q p) d -> b p q d", p=TQ)
    with semaphores(nc) as new_semaphore, ExitStack() as ctx:
        def sb(name, shape, dt=F32):
            return ctx.enter_context(nc.sbuf_tensor("b_" + name, shape, dt))

        def pair(name, shape):
            return [sb(f"{name}_{s}", shape, F32R) for s in ("high", "low")]

        def sem(name):
            return new_semaphore("b_" + name)

        RING = 4
        NWO = 2 * XG
        wkv = pair("wkv", [P, KD, 2 * KVW])
        wo = pair("wo", [P, NWO, D])
        split_weights(nc, "b_w", [(wkv_t[:, k, :], wkv[0][:, k, :], wkv[1][:, k, :]) for k in range(KD)]
                      + [(wo_t[:, k, :], wo[0][:, k, :], wo[1][:, k, :]) for k in range(NWO)])

        weights = sb("weights", [P, 2])
        k_weight = sb("k_weight", [P, 1])
        craw = [sb(f"craw{i}", [P, KD, CW]) for i in range(2)]
        cpair = [pair(f"cpair{i}", [P, KD, CW]) for i in range(2)]
        kv = sb("kv", [CW, CT, 2, KVH, XD])
        kn = sb("kn", [CW, CT, KVH, 2, XD])
        square = sb("square", [CW, KVH, XD])
        mean_sq = sb("mean_sq", [CW, CT * KVH])
        k_root, newton = sb("k_root", [CW, CT * KVH]), sb("newton", [CW, CT * KVH])
        k_high = sb("k_high", [P, KVH, CTX], F32R)
        k_low = sb("k_low", [KROWS, KVH, CTX], F32R)
        v = pair("v", [CW, CT, 2, 3, XD])
        q2 = [sb(f"q2_{i}", [TQ, NQ, 2, 2, XD]) for i in range(4)]
        qs = sb("qs", [P, XH, SEQ], F32R)
        q_max = [sb(f"q_max{i}", [KROWS, 2, SEQ], F32R) for i in range(2)]
        neg_max = sb("neg_max", [TQ, 4], F32R)
        eye4 = sb("eye4", [TQ, 4, TQ], F32R)
        own_tile = sb("own_tile", [4, 4, TQ])
        expo = [sb(f"expo{i}", [CW, 2 * SEQ]) for i in range(RING)]
        probt = pair("probt", [CW, RING, 2 * SEQ])
        recip = sb("recip", [P, 2 * SEQ])
        excess = sb("excess", [P, 2 * SEQ])
        attn = sb("attn", [P, 2 * SEQ])
        attnt = pair("attnt", [P, NWO, SEQ])
        xres = sb("xres", [TQ, NQ, D])
        xout = sb("xout", [TQ, NQ, D])

        max_bank = ctx.enter_context(nc.psum_tensor("b_max", [P, 1024], F32))
        score_bank = [ctx.enter_context(nc.psum_tensor(f"b_score{i}", [P, 512], F32)) for i in range(2)]
        pv_bank = [ctx.enter_context(nc.psum_tensor(f"b_pv{i}", [P, 512], F32)) for i in range(2)]
        piece_bank = [ctx.enter_context(nc.psum_tensor(f"b_piece{i}", [P, 512], F32)) for i in range(2)]

        w_in = sem("w_in")
        res_in, x2_out = sem("res_in"), sem("x2_out")
        c_in = [sem(f"c_in{i}") for i in range(2)]
        q_in = [sem(f"q_in{i}") for i in range(4)]
        c_high, c_low = sem("c_high"), sem("c_low")
        kv_done, kv_raw = sem("kv_done"), sem("kv_raw")
        square_done, mean_done = sem("square_done"), sem("mean_done")
        var_done, root_done = sem("var_done"), sem("root_done")
        k_scaled = sem("k_scaled")
        v_high, v_low = sem("v_high"), sem("v_low")
        kt_done, kt_high, kt_low = sem("kt_done"), sem("kt_high"), sem("kt_low")
        qt_done, qt_high, qt_low = sem("qt_done"), sem("qt_high"), sem("qt_low")
        rough_done, max_done = sem("rough_done"), sem("max_done")
        spread_done, shift_done = sem("spread_done"), sem("shift_done")
        score_done, exp_done = sem("score_done"), sem("exp_done")
        prob_high, prob_low, ring_used = sem("prob_high"), sem("prob_low"), sem("ring_used")
        recip_done, attn_done, attn_high, attn_low = (
            sem("recip_done"), sem("attn_done"), sem("attn_high"), sem("attn_low"))
        wo_done, wo_read = sem("wo_done"), sem("wo_read")
        own_dve, own_act = sem("own_dve"), sem("own_act")

        U = 8
        PIECES = [[("kt", 3), ("kt", 4), ("kt", 5), None, None, ("wo", 0)],
                  [("wo", 1), None, None, None, ("kv", 0), None],
                  [("km", 0), ("qt", 6), ("kv", 1), None, ("km", 1), ("kv", 2)],
                  [("km", 2), ("qt", 7), None, None, ("kv", 3), None],
                  [("km", 3), ("qt", 0), None, ("kv", 4), ("km", 4), ("kv", 5)],
                  [("km", 5), ("kr", 0), ("ks", 0), ("ks", 1), ("ks", 2), ("qt", 1)],
                  [("kt", 0), ("kt", 1), ("kt", 2), None, ("qt", 2), ("qt", 3)],
                  [("qt", 4), None, None, ("qt", 5), None, None]]

        def next_batch(kind, n):
            return kind in ("kv", "km", "kr", "ks") or (kind == "kt" and n < 3) or (kind == "qt" and n < 6)

        CTX_LOADS = {0: (0, 1, 2, 3), 3: (4, 5)}
        Q_LOADS = {0: ((0, 6),), 1: ((0, 7),), 2: ((1, 0),), 3: ((1, 1),), 4: ((1, 2), (1, 3)), 6: ((1, 4), (1, 5))}

        ORDER = ("s0 m0 h0 w3 p0 s1 m1 h1 w4 p1 s2 m2 h2 w5 n0 p2 s3 w0 m3 h3 n1 p3 s4 w1 h4 x n2 p4 s5 w2 h5 p5").split()

        def steps(eng, front0, slot, last, restart=lambda: None):
            front0()
            for u in range(U):
                slot(0, u, True, False)
            if NB > 2:
                with eng.Fori(0, NB - 2) as j:
                    restart()
                    for u in range(U):
                        slot(j + 1, u, True, True)
            for u in range(U):
                slot(NB - 1, u, False, True)
            last()

        def walk(b, u, front, back, do):
            last_unit = (b, u - 1) if u else (b - 1, U - 1)
            next_unit = (b, u + 1) if u < U - 1 else (b + 1, 0)
            for o in ORDER:
                kind, n = o[0], int(o[1:] or 0)
                if kind == "p":
                    if PIECES[u][n] is None:
                        continue
                    kind, n = PIECES[u][n]
                    if kind not in do:
                        continue
                    if kind == "wo":
                        if back:
                            do["wo"](b - 1, n)
                    elif not next_batch(kind, n):
                        do[kind](b, n)
                    elif front:
                        do[kind](b + 1, n)
                elif kind not in do:
                    continue
                elif kind in "mx":
                    if u < U - 1 or front:
                        do[kind](*next_unit, n)
                elif kind == "n" or (kind == "w" and n >= CT - 3):
                    if u or back:
                        do[kind](*last_unit, n)
                else:
                    do[kind](b, u, n)

        BANK = {}
        for u in range(U):
            for o in ORDER:
                piece = ("x", (u + 1) % U) if o == "x" else PIECES[u][int(o[1:])] if o[0] == "p" else None
                if piece and piece[0] in ("kv", "kt", "qt", "wo", "x"):
                    BANK[piece] = len(BANK) % 2
        assert len(BANK) % 2 == 0

        FIRST = ([("kv", 0)] + [p for n in range(1, CT) for p in (("kv", n), ("km", n - 1))] + [("km", CT - 1), ("kr", 0)]
                 + [("ks", n) for n in range(3)] + [("kt", n) for n in range(3)] + [("qt", n) for n in range(6)])

        def place(u, t):
            return (CT * u + t) % RING

        def rows(j):
            halves = slice(0, XD), slice(XD, P)
            return halves if j % 2 == 0 else halves[::-1]

        def first(do):
            for kind, n in FIRST:
                if kind in do:
                    do[kind](0, n)
            for n in range(4):
                if "m" in do:
                    do["m"](0, 0, n)
            if "x" in do:
                do["x"](0, 0, 0)

        block = ctx.enter_context(nc.Block())

        @block.sync
        def _(sp):
            def load_ctx(b, n):
                wait(sp, c_low, at(b, CT, n - 1))
                sp.dma_start(craw[n % 2][:, :, :], ctx_t[b, n]).then_inc(c_in[n % 2], 16)

            def load_q(b, n):
                wait(sp, qt_done, at(b, 8, n - 3))
                for twice in range(2):
                    for h in range(2):
                        sp.dma_start(q2[n % 4][:, :, h, twice, :], q_v[b, :, :, 2 * n + h, :]).then_inc(q_in[n % 4], 16)

            def load_residual(b):
                wait(sp, wo_read, at(b, 2, 0))
                sp.dma_start(xres[:, :, :], x1_v[b]).then_inc(res_in, 16)

            def store(b):
                sp.wait_ge(wo_read, at(b, 2, 2))
                sp.dma_start(x2_v[b], xout[:, :, :]).then_inc(x2_out, 16)

            def slot(b, u, front, back):
                if u == 2 and back:
                    store(b - 1)
                if u == 3:
                    load_residual(b)
                if front:
                    for n in CTX_LOADS.get(u, ()):
                        load_ctx(b + 1, n)
                for ahead, n in Q_LOADS.get(u, ()):
                    if ahead == 0:
                        load_q(b, n)
                    elif front:
                        load_q(b + 1, n)

            def front0():
                for half in range(2):
                    for i, w in enumerate(norm_w):
                        sp.dma_start(weights[half * XD:(half + 1) * XD, i:i + 1], w.rearrange("(d o) -> d o", o=1)).then_inc(w_in, 16)
                for n in range(2):
                    load_ctx(0, n)
                for n in range(4):
                    load_q(0, n)
                for n in range(2, CT):
                    load_ctx(0, n)
                for n in range(4, 6):
                    load_q(0, n)

            steps(sp, front0, slot, lambda: store(NB - 1))
            sp.wait_ge(x2_out, 16 * NB)

        @block.tensor
        def _(pe):
            held = [None, None]

            def take_bank(piece, sem_, value):
                bank = BANK[piece]
                if held[bank]:
                    pe.wait_ge(*held[bank])
                held[bank] = (sem_, value)
                return piece_bank[bank]

            def project(b, n):
                pe.wait_ge(c_low, at(b, CT, n + 1))
                bank = take_bank(("kv", n), kv_raw, at(b, CT, n + 1))
                for k in range(KD):
                    m = split_matmul(pe, bank[0:CW, 0:2 * KVW], [s[:, k, :] for s in cpair[n % 2]],
                                     [s[:, k, :] for s in wkv], k == 0, k == KD - 1)
                m.then_inc(kv_done, 1)

            def turn_k(b, n):
                half, c = n // 3, n % 3
                pe.wait_ge(k_scaled, at(b, 3, 3))
                bank = take_bank(("kt", n), kt_low, at(b, 6, n + 1))
                for j in range(2):
                    for i in range(2):
                        m = pe.transpose(bank[:, (2 * j + i) * CW:(2 * j + i + 1) * CW],
                                         kn[:, 2 * c + i, 2 * half + j, :, :].rearrange("p a d -> p (a d)"),
                                         ident[0:CW, 0:CW])
                m.then_inc(kt_done, 1)

            def turn_q(b, n):
                pe.wait_ge(q_in[n % 4], at(b, 128, 64 * (n // 4) + 64))
                bank = take_bank(("qt", n), qt_low, at(b, 8, n + 1))
                for h in range(2):
                    for q in range(NQ):
                        c = h * SEQ + q * TQ
                        m = pe.transpose(bank[:, c:c + TQ], q2[n % 4][:, q, h, :, :].rearrange("p a d -> p (a d)"),
                                         ident[0:TQ, 0:TQ])
                m.then_inc(qt_done, 1)

            def output(b, q):
                pe.wait_ge(attn_low, at(b, U, U))
                bank = take_bank(("wo", q), wo_read, at(b, 2, q + 1))
                for k in range(NWO):
                    m = split_matmul(pe, bank[0:TQ, 0:D], [t[:, k, q * TQ:(q + 1) * TQ] for t in attnt],
                                     [t[:, k, :] for t in wo], k == 0, k == NWO - 1)
                m.then_inc(wo_done, 1)

            def rough_scores(b, u, s):
                h, q, j = 2 * u + s // 2, s % 2, u // 2
                pe.wait_ge(qt_low, at(b, 8, u + 1))
                pe.wait_ge(kt_high, at(b, 6, 3 * (j // 2) + 3))
                wait(pe, max_done, at(b, 32, 4 * u + s))
                for c0, c1 in ((0, 512), (512, CTX)):
                    m = pe.matmul(max_bank[0:TQ, c0:c1], qs[:, h, q * TQ:(q + 1) * TQ], k_high[:, j, c0:c1], start=True, stop=True)
                m.then_inc(rough_done, 1)

            def spread_max(b, u, _):
                pe.wait_ge(max_done, at(b, 32, 4 * u + 4))
                bank = take_bank(("x", u), shift_done, at(b, U, u + 1))
                pe.matmul(bank[0:4, 0:2 * SEQ], neg_max[:, :], eye4[:, :, :].rearrange("p s t -> p (s t)"), start=True,
                          stop=True).then_inc(spread_done, 1)

            def scores(b, u, t):
                j, cols = u // 2, slice(t * CW, (t + 1) * CW)
                pe.wait_ge(shift_done, at(b, U, u + 1))
                pe.wait_ge(kt_low, at(b, 6, 3 * (j // 2) + 3))
                wait(pe, exp_done, at(b, 48, 6 * u + t - 1))
                bank = score_bank[t % 2][0:CW, 0:2 * SEQ]
                pe.matmul(bank, k_high[:, j, cols], qs[:, 2 * u:2 * u + 2, :].rearrange("p h t -> p (h t)"), start=True, stop=False)
                pe.matmul(bank, k_low[:, j, cols], q_max[u % 2][:, :, :].rearrange("p h t -> p (h t)"), start=False,
                          stop=True).then_inc(score_done, 1)

            def weigh_values(b, u, t):
                j = u // 2
                pe.wait_ge(prob_low, at(b, 48, 6 * u + t + 1))
                pe.wait_ge(v_low, at(b, 2, j // 2 + 1))
                if t == 0:
                    wait(pe, attn_done, at(b, U, u - 1))
                pair_ = slice(0, 2) if j % 2 == 0 else slice(1, 3)
                split_matmul(pe, pv_bank[u % 2][:, 0:2 * SEQ], [s[:, t, j // 2, pair_, :].rearrange("p a d -> p (a d)") for s in v],
                             [s[:, place(u, t), :] for s in probt], t == 0, t == CT - 1).then_inc(ring_used, 1)

            do = {"s": scores, "m": rough_scores, "x": spread_max, "w": weigh_values,
                  "wo": output, "kv": project, "kt": turn_k, "qt": turn_q}

            def slot(b, u, front, back):
                if u == 0:
                    held[BANK[("qt", 5)]] = (qt_low, at(b, 8, 6))
                    held[BANK[("x", 0)]] = (shift_done, at(b, U, 1))
                walk(b, u, front, back, do)

            def last():
                for t in (3, 4, 5):
                    weigh_values(NB - 1, U - 1, t)
                for q in range(NQ):
                    output(NB - 1, q)

            assert BANK[("qt", 5)] != BANK[("x", 0)]
            steps(pe, lambda: first(do), slot, last)

        @block.scalar
        def _(act):
            own = Own(act, own_act)

            def high_ctx(b, n):
                act.wait_ge(c_in[n % 2], at(b, 48, 16 * (n // 2) + 16))
                wait(act, kv_done, at(b, CT, n - 1))
                act.activation(cpair[n % 2][0][:, :, :], craw[n % 2][:, :, :], ACT.Copy).then_inc(c_high, 1)

            def keys_values(b, n):
                act.wait_ge(kv_done, at(b, CT, n + 1))
                if n == 0:
                    wait(act, v_low, at(b - 1, 2, 2))
                    wait(act, k_scaled, at(b - 1, 3, 3))
                act.activation(kv[:, n, :, :, :].rearrange("p a j d -> p (a j d)"), piece_bank[BANK[("kv", n)]][0:CW, 0:2 * KVW],
                               ACT.Copy).then_inc(kv_raw, 1)
                if n + 2 < CT:
                    high_ctx(b, n + 2)

            def key_root(b, _):
                act.wait_ge(var_done, at(b, 1, 1))
                own.done(act.activation(k_root[:, :], mean_sq[:, :], ACT.Ln))
                act.activation(k_root[:, :], k_root[:, :], ACT.Exp, scale=-0.5).then_inc(root_done, 1)

            def high_k(b, n):
                half, c = n // 3, n % 3
                act.wait_ge(kt_done, at(b, 6, n + 1))
                if n % 3 == 0:
                    wait(act, score_done, at(b - 1, 48, 24 * half + 24))
                act.activation(k_high[:, 2 * half:2 * half + 2, 2 * c * CW:2 * (c + 1) * CW],
                               piece_bank[BANK[("kt", n)]][:, 0:4 * CW].rearrange("p (j t) -> p j t", j=2), ACT.Copy,
                               scale=k_weight[:, 0:1]).then_inc(kt_high, 1)

            def high_q(b, n):
                act.wait_ge(qt_done, at(b, 8, n + 1))
                wait(act, score_done, at(b - 1, 48, 6 * n + 6))
                act.activation(qs[:, 2 * n:2 * n + 2, :], piece_bank[BANK[("qt", n)]][:, 0:2 * SEQ].rearrange("p (h t) -> p h t", h=2),
                               ACT.Copy).then_inc(qt_high, 1)

            def exponent(b, u, t):
                i = 6 * u + t
                act.wait_ge(score_done, at(b, 48, i + 1))
                wait(act, prob_low, at(b, 48, i - 3))
                act.activation(expo[place(u, t)][:, :], score_bank[t % 2][0:CW, 0:2 * SEQ], ACT.Exp).then_inc(exp_done, 1)

            def high_prob(b, u, t):
                i = 6 * u + t
                act.wait_ge(exp_done, at(b, 48, i + 1))
                wait(act, ring_used, at(b, 48, i - 3))
                act.activation(probt[0][:, place(u, t), :], expo[place(u, t)][:, :], ACT.Copy).then_inc(prob_high, 1)

            def quotients(b, u, part):
                j = u // 2
                out, sums = rows(j)
                if part == 0:
                    act.wait_ge(ring_used, at(b, 48, 6 * u + 6))
                    wait(act, attn_done, at(b, U, u))
                    own.done(act.activation(recip[sums, :], pv_bank[u % 2][sums, 0:2 * SEQ], ACT.Ln))
                    act.activation(recip[sums, :], recip[sums, :], ACT.Exp, scale=-1.0).then_inc(recip_done, 1)
                if part == 2:
                    act.wait_ge(attn_done, at(b, U, u + 1))
                    wait(act, wo_done, at(b - 1, 2, 2))
                    k = (j // 2) * XG + 2 * (u % 2)
                    act.activation(attnt[0][out, k:k + 2, :], attn[out, :].rearrange("p (h t) -> p h t", h=2),
                                   ACT.Copy).then_inc(attn_high, 1)

            def split_values(b, half):
                act.wait_ge(kv_raw, at(b, CT, CT))
                wait(act, ring_used, at(b - 1, 48, 24 * half + 24))
                act.activation(v[0][:, :, half, 0:3:2, :], kv[:, :, 1, 2 * half:2 * half + 2, :], ACT.Copy).then_inc(v_high, 1)

            do = {"s": exponent, "h": high_prob, "n": quotients, "kv": keys_values, "kr": key_root, "kt": high_k, "qt": high_q}

            def slot(b, u, front, back):
                if u == 0 and front:
                    for n in range(2):
                        high_ctx(b + 1, n)
                walk(b, u, front, back, do)
                if u == 6 and front:
                    split_values(b + 1, 0)
                if u == 0:
                    split_values(b, 1)

            def front0():
                for n in range(2):
                    high_ctx(0, n)
                first(do)
                split_values(0, 0)

            def last():
                for part in (0, 2):
                    quotients(NB - 1, U - 1, part)

            act.preload_act_table_set("natural_log_exp_and_others")
            steps(act, front0, slot, last, own.restart)

        @block.vector
        def _(dve):
            own = Own(dve, own_dve)

            def mean_squares(b, n):
                dve.wait_ge(square_done, at(b, CT, n + 1))
                if n == 0:
                    wait(dve, root_done, at(b - 1, 1, 1))
                dve.tensor_reduce(mean_sq[:, n * KVH:(n + 1) * KVH], square[:, :, :], AX.X, ALU.add).then_inc(mean_done, 1)

            def key_root(b, _):
                dve.wait_ge(mean_done, at(b, CT, CT))
                dve.tensor_scalar(mean_sq[:, :], mean_sq[:, :], 1.0 / XD, RMS_EPS, ALU.mult, ALU.add).then_inc(var_done, 1)
                dve.wait_ge(var_done, at(b, 1, 1))
                dve.wait_ge(root_done, at(b, 1, 1))
                refine_root(dve, own, k_root[:, :], mean_sq[:, :], newton[:, :])

            def scale_keys(b, n):
                wait(dve, kt_done, at(b - 1, 6, 6))
                for t in (2 * n, 2 * n + 1):
                    keys = kv[:, t, 0, :, :]
                    m = dve.tensor_tensor(kn[:, t, :, :, :], keys[:, :, None, :].broadcast_to([CW, KVH, 2, XD]),
                                          k_root[:, t * KVH:(t + 1) * KVH, None, None].broadcast_to([CW, KVH, 2, XD]), ALU.mult)
                m.then_inc(k_scaled, 1)

            def low_k(b, n):
                half, c = n // 3, n % 3
                dve.wait_ge(kt_high, at(b, 6, n + 1))
                sel = (slice(0, XD), slice(2 * half, 2 * half + 2), slice(2 * c * CW, 2 * (c + 1) * CW))
                bank = piece_bank[BANK[("kt", n)]]
                dve.scalar_tensor_tensor(k_low[sel], bank[0:XD, 0:4 * CW].rearrange("p (j t) -> p j t", j=2),
                                         k_weight[0:XD, 0:1], bits(k_high[sel]), ALU.mult, ALU.subtract).then_inc(kt_low, 1)

            def low_q(b, n):
                dve.wait_ge(qt_high, at(b, 8, n + 1))
                low = qs[XD:P, 2 * n:2 * n + 2, :]
                dve.tensor_tensor(low, piece_bank[BANK[("qt", n)]][XD:P, 0:2 * SEQ].rearrange("p (h t) -> p h t", h=2), bits(low),
                                  ALU.subtract).then_inc(qt_low, 1)

            def maximum(b, u, s):
                dve.wait_ge(rough_done, at(b, 32, 4 * u + s + 1))
                if s == 0:
                    wait(dve, spread_done, at(b, U, u))
                dve.tensor_reduce(neg_max[:, s:s + 1], max_bank[0:TQ, 0:CTX], AX.X, ALU.max, negate=True).then_inc(max_done, 1)

            def shift(b, u, _):
                wait(dve, score_done, at(b, 48, 6 * (u - 1)))
                dve.tensor_copy(q_max[u % 2][0:XD, :, :], bits(qs[0:XD, 2 * u:2 * u + 2, :]))
                dve.wait_ge(spread_done, at(b, U, u + 1))
                dve.tensor_tensor(q_max[u % 2][XD:KROWS, :, :].rearrange("p h t -> p (h t)"),
                                  piece_bank[BANK[("x", u)]][0:4, 0:2 * SEQ], own_tile[:, :, :].rearrange("p s t -> p (s t)"),
                                  ALU.mult).then_inc(shift_done, 1)

            def quotients(b, u, part):
                j = u // 2
                out, sums = rows(j)
                bank = pv_bank[u % 2]
                if part == 1:
                    dve.wait_ge(recip_done, at(b, U, u + 1))
                    own.done(dve.tensor_tensor(excess[sums, :], bank[sums, 0:2 * SEQ], recip[sums, :], ALU.mult))
                    own.done(dve.scalar_tensor_tensor(excess[out, :], excess[sums, :], -2.0, recip[sums, :], ALU.add, ALU.mult))
                    wait(dve, attn_low, at(b, U, u))
                    dve.scalar_tensor_tensor(attn[out, :], excess[out, :], -1.0, bank[out, 0:2 * SEQ], ALU.mult,
                                             ALU.mult).then_inc(attn_done, 1)
                if part == 2:
                    dve.wait_ge(attn_high, at(b, U, u + 1))
                    k = (j // 2) * XG + 2 * (u % 2)
                    dve.tensor_tensor(attnt[1][out, k:k + 2, :], attn[out, :].rearrange("p (h t) -> p h t", h=2),
                                      bits(attnt[0][out, k:k + 2, :]), ALU.subtract).then_inc(attn_low, 1)

            def residual(b, q):
                dve.wait_ge(wo_done, at(b, 2, q + 1))
                if q == 0:
                    dve.wait_ge(res_in, at(b, 16, 16))
                    wait(dve, x2_out, at(b, 16, 0))
                dve.tensor_tensor(xout[:, q, :], piece_bank[BANK[("wo", q)]][0:TQ, 0:D], xres[:, q, :], ALU.add).then_inc(wo_read, 1)

            def split_values(b, half):
                dve.wait_ge(v_high, at(b, 2, half + 1))
                sel = (slice(None), slice(None), half, slice(0, 3, 2))
                dve.tensor_tensor(v[1][:, :, half, 0:3:2, :], kv[:, :, 1, 2 * half:2 * half + 2, :],
                                  bits(v[0][:, :, half, 0:3:2, :]), ALU.subtract).then_inc(v_low, 1)

            do = {"m": maximum, "x": shift, "n": quotients, "wo": residual, "km": mean_squares,
                  "kr": key_root, "ks": scale_keys, "kt": low_k, "qt": low_q}

            def slot(b, u, front, back):
                walk(b, u, front, back, do)
                if u == 6 and front:
                    split_values(b + 1, 0)
                if u == 0:
                    split_values(b, 1)

            def constants():
                dve.memset(bits(v[0][:, :, :, 1, :]), 1.0)
                dve.memset(bits(v[1][:, :, :, 1, :]), 0.0)
                dve.memset(bits(k_low[XD:KROWS, :, :]), 1.0)
                dve.tensor_copy(eye4[:, :, :], ident[0:TQ, None, 0:TQ].broadcast_to([TQ, 4, TQ]))
                dve.tensor_copy(own_tile[:, :, :], ident[0:4, 0:4, None].broadcast_to([4, 4, TQ]))
                dve.wait_ge(w_in, 64)
                own.done(dve.tensor_tensor(k_weight[:, :], weights[:, 0:1], weights[:, 1:2], ALU.mult))

            def front0():
                constants()
                first(do)
                split_values(0, 0)

            def last():
                for part in (1, 2):
                    quotients(NB - 1, U - 1, part)
                for q in range(NQ):
                    residual(NB - 1, q)

            steps(dve, front0, slot, last, own.restart)

        @block.gpsimd
        def _(pool):
            def low_ctx(b, n):
                pool.wait_ge(c_high, at(b, CT, n + 1))
                pool.tensor_tensor(cpair[n % 2][1][:, :, :], craw[n % 2][:, :, :], bits(cpair[n % 2][0][:, :, :]),
                                   ALU.subtract).then_inc(c_low, 1)

            def squares(b, n):
                pool.wait_ge(kv_raw, at(b, CT, n + 1))
                wait(pool, mean_done, at(b, CT, n))
                pool.tensor_tensor(square[:, :, :], kv[:, n, 0, :, :], kv[:, n, 0, :, :], ALU.mult).then_inc(square_done, 1)
                if n + 2 < CT:
                    low_ctx(b, n + 2)

            def low_prob(b, u, t):
                i = 6 * u + t
                pool.wait_ge(prob_high, at(b, 48, i + 1))
                pool.tensor_tensor(probt[1][:, place(u, t), :], expo[place(u, t)][:, :], bits(probt[0][:, place(u, t), :]),
                                   ALU.subtract).then_inc(prob_low, 1)

            do = {"h": low_prob, "kv": squares}

            def slot(b, u, front, back):
                if u == 0 and front:
                    for n in range(2):
                        low_ctx(b + 1, n)
                walk(b, u, front, back, do)

            def front0():
                for n in range(2):
                    low_ctx(0, n)
                first(do)

            steps(pool, front0, slot, lambda: None)


FF = 1536
FT = FF // P
WBLOCK = 32
NB_BLOCK = D // WBLOCK
W_MAX, A_MAX = 7.0, 32767.0
SIG_STEPS = 65536.0
TINY = 1e-12
CHUNK = 512
NCH = BATCH * SEQ // CHUNK
CTILES = CHUNK // P


def quantise_weights(nc, name, ident, outer, ring, src, dst):
    with semaphores(nc) as new_semaphore, ExitStack() as ctx:
        def sb(nm, shape, dt=F32):
            return ctx.enter_context(nc.sbuf_tensor(f"{name}_{nm}", shape, dt))

        def sem(nm):
            return new_semaphore(f"{name}_{nm}")

        raw = [sb(f"raw{r}", [P, NB_BLOCK, WBLOCK]) for r in range(ring)]
        steps_ = [sb(f"steps{r}", [P, NB_BLOCK, WBLOCK], I16) for r in range(ring)]
        scale = [sb(f"scale{r}", [P, NB_BLOCK]) for r in range(ring)]
        inv = sb("inv", [P, NB_BLOCK])
        bank = [ctx.enter_context(nc.psum_tensor(f"{name}_turn{r}", [P, 512], F32)) for r in range(ring)]
        loaded = [sem(f"loaded{r}") for r in range(ring)]
        stepped, valued, turned, high_done, low_done, own_dve = (
            sem("stepped"), sem("valued"), sem("turned"), sem("high_done"), sem("low_done"), sem("own_dve"))

        def each(eng, step, restart=lambda: None):
            for r in range(ring):
                step(0, r)
            with eng.Fori(0, outer - 1) as j:
                restart()
                for r in range(ring):
                    step(j + 1, r)

        def before(i, r):
            return (i, r - 1) if r else (i - 1, ring - 1)

        block = ctx.enter_context(nc.Block())

        @block.sync
        def _(sp):
            def step(i, r):
                wait(sp, turned, at(i - 1, ring, r + 1))
                sp.dma_start(raw[r][:, :, :].rearrange("p b w -> p (b w)"), src(i, r)).then_inc(loaded[r], 16)

            each(sp, step)

        @block.vector
        def _(dve):
            own = Own(dve, own_dve)

            def quantise(i, r):
                dve.wait_ge(loaded[r], at(i, 16, 16))
                own.done(dve.tensor_reduce(scale[r][:, :], raw[r][:, :, :], AX.X, ALU.max, apply_absolute_value=True))
                own.done(dve.tensor_scalar(scale[r][:, :], scale[r][:, :], 1.0 / W_MAX, TINY, ALU.mult, ALU.max))
                own.done(dve.reciprocal(inv[:, :], scale[r][:, :]))
                dve.tensor_tensor(steps_[r][:, :, :], raw[r][:, :, :], inv[:, :, None].broadcast_to([P, NB_BLOCK, WBLOCK]),
                                  ALU.mult).then_inc(stepped, 1)
                dve.wait_ge(stepped, at(i, ring, r + 1))
                dve.tensor_tensor(raw[r][:, :, :], steps_[r][:, :, :], scale[r][:, :, None].broadcast_to([P, NB_BLOCK, WBLOCK]),
                                  ALU.mult).then_inc(valued, 1)

            def low(i, r):
                dve.wait_ge(high_done, at(i, ring, r + 1))
                hi, lo = dst(i, r)
                dve.tensor_tensor(lo, bank[r][:, :].rearrange("p (k o) -> p k o", k=4), bits(hi), ALU.subtract).then_inc(low_done, 1)

            def step(i, r):
                quantise(i, r)
                if not (isinstance(i, int) and i == 0 and r == 0):
                    low(*before(i, r))

            each(dve, step, own.restart)
            low(outer - 1, ring - 1)

        @block.tensor
        def _(pe):
            def step(i, r):
                pe.wait_ge(valued, at(i, ring, r + 1))
                wait(pe, low_done, at(i - 1, ring, r + 1))
                flat = raw[r][:, :, :].rearrange("p b w -> p (b w)")
                for k in range(4):
                    m = pe.transpose(bank[r][:, k * P:(k + 1) * P], flat[:, k * P:(k + 1) * P], ident)
                m.then_inc(turned, 1)

            each(pe, step)

        @block.scalar
        def _(act):
            def step(i, r):
                act.wait_ge(turned, at(i, ring, r + 1))
                act.activation(dst(i, r)[0], bank[r][:, :].rearrange("p (k o) -> p k o", k=4), ACT.Copy).then_inc(high_done, 1)

            each(act, step)


class Scalars:

    def __init__(self, ctx, nc):
        def sb(name, n=1):
            return ctx.enter_context(nc.sbuf_tensor("s_" + name, [P, n], F32))

        self.peak_x = sb("peak_x", BATCH * SEQ // P)
        self.peak_g, self.peak_u = sb("peak_g", 2 * NCH * FT), sb("peak_u", 2 * NCH * FT)
        self.peak_p, self.peak_o = sb("peak_p", NCH * FT), sb("peak_o", NCH * FT)
        self.s_x, self.r_x = sb("s_x"), sb("r_x")
        self.s_g, self.r_g = sb("s_g"), sb("r_g")
        self.s_u, self.r_u = sb("s_u"), sb("r_u")
        self.s_p, self.r_p = sb("s_p"), sb("r_p")
        self.s_o, self.r_o = sb("s_o"), sb("r_o")
        self.unit = sb("unit")


def scale_from_peak(nc, name, jobs):
    n = len(jobs)
    with semaphores(nc) as new_semaphore, ExitStack() as ctx:
        peak = ctx.enter_context(nc.sbuf_tensor(f"{name}_peak", [P, n], F32))
        whole = ctx.enter_context(nc.sbuf_tensor(f"{name}_whole", [P, n], F32))
        unit_ = ctx.enter_context(nc.sbuf_tensor(f"{name}_unit", [P, n], F32))
        inv = ctx.enter_context(nc.sbuf_tensor(f"{name}_inv", [P, n], F32))
        peak_done, whole_done, own_dve = [new_semaphore(f"{name}_{s}") for s in ("peak_done", "whole_done", "own_dve")]
        block = ctx.enter_context(nc.Block())

        @block.vector
        def _(dve):
            own = Own(dve, own_dve)
            for i, (peaks, _, _, _) in enumerate(jobs):
                dve.tensor_reduce(peak[:, i:i + 1], peaks, AX.X, ALU.max).then_inc(peak_done, 1)
            dve.wait_ge(whole_done, 1)
            for i, (_, (ua, ub), scale, factor) in enumerate(jobs):
                u = unit_[:, i:i + 1]
                own.done(dve.tensor_scalar(u, ua, ub, None, ALU.mult) if ua is not None else dve.memset(u, ub))
                own.done(dve.tensor_scalar(scale[:, :], whole[:, i:i + 1], u, 1.0 / A_MAX, ALU.mult, ALU.mult))
                own.done(dve.tensor_scalar(scale[:, :], scale[:, :], TINY, None, ALU.max))
                own.done(dve.reciprocal(inv[:, i:i + 1], scale[:, :]))
                own.done(dve.tensor_scalar(factor[:, :], inv[:, i:i + 1], u, None, ALU.mult))

        @block.gpsimd
        def _(pool):
            pool.wait_ge(peak_done, n)
            pool.partition_all_reduce(whole[:, :], peak[:, :], P, MAXIMUM).then_inc(whole_done, 1)


def normalise_tokens(nc, x2, xn, peaks, TILES):
    x_v = x2.rearrange("b s d -> (b s) d").rearrange("(t p) d -> p t d", p=P)
    RING = 4
    GROUPS = TILES // RING
    with semaphores(nc) as new_semaphore, ExitStack() as ctx:
        def sb(nm, shape, dt=F32):
            return ctx.enter_context(nc.sbuf_tensor("n_" + nm, shape, dt))

        def sem(nm):
            return new_semaphore("n_" + nm)

        stats, moments = sb("stats", [P, RING, 6]), sb("moments", [P, RING, 2])
        var, root, newton = sb("var", [P, RING]), sb("root", [P, RING]), sb("newton", [P, RING])
        loaded = [sem(f"loaded{i}") for i in range(2)]
        seen, var_done, root_done, own_dve, own_act = (
            sem("seen"), sem("var_done"), sem("root_done"), sem("own_dve"), sem("own_act"))

        def each(eng, step, restart=lambda: None):
            step(0, 0, 0)
            step(1, 1, 0)
            rest = (GROUPS - 2) // 2
            if rest:
                with eng.Fori(0, rest) as j:
                    restart()
                    for v in range(2):
                        step(2 * j + 2 + v, v, j + 1)
            for i in range(2 + 2 * rest, GROUPS):
                step(i, i % 2, i // 2)

        block = ctx.enter_context(nc.Block())

        @block.sync
        def _(sp):
            def step(i, par, r):
                wait(sp, seen, i - 1)
                sp.dma_start(xn[:, bass.ds(i * RING, RING), :], x_v[:, bass.ds(i * RING, RING), :]).then_inc(loaded[par], 16)

            each(sp, step)

        @block.scalar
        def _(act):
            own = Own(act, own_act)
            act.preload_act_table_set("natural_log_exp_and_others")

            def step(i, par, r):
                act.wait_ge(var_done, i + 1)
                own.done(act.activation(root[:, :], var[:, :], ACT.Ln))
                act.activation(root[:, :], root[:, :], ACT.Exp, scale=-0.5).then_inc(root_done, 1)

            each(act, step, own.restart)

        @block.vector
        def _(dve):
            own = Own(dve, own_dve)

            def step(i, par, r):
                dve.wait_ge(loaded[par], at(r, 16, 16))
                for t in range(RING):
                    m = dve.bn_stats(stats[:, t, :], xn[:, i * RING + t, :])
                own.done(m)
                for t in range(RING):
                    m = dve.bn_aggr(moments[:, t, :], stats[:, t, :])
                m.then_inc(seen, 1)
                dve.wait_ge(seen, i + 1)
                dve.tensor_scalar(var[:, :], moments[:, :, 1], LN_EPS, None, ALU.add).then_inc(var_done, 1)
                dve.wait_ge(var_done, i + 1)
                dve.wait_ge(root_done, i + 1)
                refine_root(dve, own, root[:, :], var[:, :], newton[:, :])
                for t in range(RING):
                    tile = xn[:, i * RING + t, :]
                    m = dve.tensor_scalar(tile, tile, moments[:, t, 0:1], root[:, t:t + 1], ALU.subtract, ALU.mult)
                own.done(m)
                own.done(dve.tensor_reduce(peaks[:, bass.ds(i * RING, RING)], xn[:, bass.ds(i * RING, RING), :], AX.X, ALU.max,
                                           apply_absolute_value=True))

            each(dve, step, own.restart)


def gate_and_up(nc, ident, xn, wg, wu, s, g_dram, u_dram, CH):
    with semaphores(nc) as new_semaphore, ExitStack() as ctx:
        def sb(nm, shape, dt=F32):
            return ctx.enter_context(nc.sbuf_tensor("g_" + nm, shape, dt))

        def sem(nm):
            return new_semaphore("g_" + nm)

        xs = [sb(f"xs{i}", [P, D]) for i in range(2)]
        xq = sb("xq", [P, KD, P], I16)
        xt = [[sb(f"xt{i}_{h}", [P, KD, CHUNK], F32R) for h in ("high", "low")] for i in range(2)]
        out = [sb(f"out{i}", [P, CHUNK]) for i in range(4)]
        turn_bank = [ctx.enter_context(nc.psum_tensor(f"g_turn{i}", [P, 512], F32)) for i in range(2)]
        prod_bank = [ctx.enter_context(nc.psum_tensor(f"g_prod{i}", [P, 512], F32)) for i in range(4)]
        stored = [sem(f"stored{i}") for i in range(4)]
        staged, turned, quantised = sem("staged"), sem("turned"), sem("quantised")
        x_high, x_low = sem("x_high"), sem("x_low")
        prod_done, copied, peaked = sem("prod_done"), sem("copied"), sem("peaked")
        NPROD = 2 * FT

        def steps(eng, front0, chunk, restart=lambda: None):
            front0()
            chunk(0, 0, CH > 1)
            rest = CH - 2 if CH > 2 else 0
            pairs = rest // 2
            if pairs:
                with eng.Fori(0, pairs) as j:
                    restart()
                    for u in range(2):
                        chunk(2 * j + 1 + u, (1 + u) % 2, True)
            for c in range(1 + 2 * pairs, CH):
                chunk(c, c % 2, c < CH - 1)

        block = ctx.enter_context(nc.Block())

        @block.tensor
        def _(pe):
            def turn(c, t):
                pe.wait_ge(staged, at(c, CTILES, t + 1))
                wait(pe, quantised, at(c, CTILES, t - 1))
                for k in range(KD):
                    m = pe.transpose(turn_bank[t % 2][:, k * P:(k + 1) * P], xs[t % 2][:, k * P:(k + 1) * P], ident)
                m.then_inc(turned, 1)

            def product(c, par, n):
                f, w = n // 2, (wg, wu)[n % 2]
                wait(pe, peaked, at(c, NPROD, n - 3))
                for k in range(KD):
                    m = split_matmul(pe, prod_bank[n % 4][:, :], [s_[:, f, k, :] for s_ in w], [s_[:, k, :] for s_ in xt[par]],
                                     k == 0, k == KD - 1)
                m.then_inc(prod_done, 1)

            def chunk(c, par, front):
                pe.wait_ge(x_low, at(c, CTILES, CTILES))
                for n in range(NPROD):
                    product(c, par, n)
                    if front and n % 6 == 3:
                        turn(c + 1, n // 6)

            def front0():
                for t in range(CTILES):
                    turn(0, t)

            steps(pe, front0, chunk)

        @block.gpsimd
        def _(pool):
            def stage(c):
                for t in range(CTILES):
                    wait(pool, turned, at(c, CTILES, t - 1))
                    pool.tensor_copy(xs[t % 2][:, :], xn[:, c * CTILES + t, :]).then_inc(staged, 1)

            stage(0)
            with pool.Fori(0, CH - 1) as c:
                stage(c + 1)

        @block.scalar
        def _(act):
            def high(c, par, t):
                act.wait_ge(quantised, at(c, CTILES, t + 1))
                wait(act, prod_done, at(c - 1, NPROD, 0))
                act.activation(xt[par][0][:, :, t * P:(t + 1) * P], xq[:, :, :], ACT.Copy).then_inc(x_high, 1)

            def copy(c, n):
                act.wait_ge(prod_done, at(c, NPROD, n + 1))
                if not (isinstance(c, int) and c == 0 and n < 4):
                    act.wait_ge(stored[n % 4], at(c, 16 * NPROD // 4, 16 * (n // 4)))
                    act.wait_ge(peaked, at(c, NPROD, n - 3))
                act.activation(out[n % 4][:, :], prod_bank[n % 4][:, :], ACT.Copy).then_inc(copied, 1)

            def chunk(c, par, front):
                for n in range(NPROD):
                    copy(c, n)
                    if front and n % 6 == 3:
                        high(c + 1, 1 - par, n // 6)

            def front0():
                for t in range(CTILES):
                    high(0, 0, t)

            steps(act, front0, chunk)

        @block.vector
        def _(dve):
            def quantise(c, t):
                dve.wait_ge(turned, at(c, CTILES, t + 1))
                wait(dve, x_low, at(c, CTILES, t))
                dve.tensor_scalar(xq[:, :, :], turn_bank[t % 2][:, :].rearrange("p (k t) -> p k t", k=KD), s.r_x[:, 0:1], None,
                                  ALU.mult).then_inc(quantised, 1)

            def low(c, par, t):
                dve.wait_ge(x_high, at(c, CTILES, t + 1))
                cols = slice(t * P, (t + 1) * P)
                dve.tensor_tensor(xt[par][1][:, :, cols], xq[:, :, :], bits(xt[par][0][:, :, cols]), ALU.subtract).then_inc(x_low, 1)

            def peak(c, n):
                f = n // 2
                dve.wait_ge(copied, at(c, NPROD, n + 1))
                dst = (s.peak_g, s.peak_u)[n % 2]
                dve.tensor_reduce(dst[:, bass.ds(c * FT + f, 1)], out[n % 4][:, :], AX.X, ALU.max,
                                  apply_absolute_value=True).then_inc(peaked, 1)

            def chunk(c, par, front):
                for n in range(NPROD):
                    if front and n % 6 == 4:
                        low(c + 1, 1 - par, n // 6)
                    peak(c, n)
                    if front and n % 6 == 3:
                        quantise(c + 1, n // 6)

            def front0():
                for t in range(CTILES):
                    quantise(0, t)
                    low(0, 0, t)

            steps(dve, front0, chunk)

        @block.sync
        def _(sp):
            def chunk(c, par, front):
                for n in range(NPROD):
                    sp.wait_ge(copied, at(c, NPROD, n + 1))
                    sp.dma_start((g_dram, u_dram)[n % 2][c, n // 2], out[n % 4][:, :]).then_inc(stored[n % 4], 16)

            steps(sp, lambda: None, chunk)
            for i in range(4):
                sp.wait_ge(stored[i], 16 * (NPROD // 4) * CH)


WIDE = 2 * CHUNK


def product_peak(nc, g_dram, prod, s, CH):
    N = CH * FT // 2
    with semaphores(nc) as new_semaphore, ExitStack() as ctx:
        def sb(nm, shape, dt=F32):
            return ctx.enter_context(nc.sbuf_tensor("p_" + nm, shape, dt))

        def sem(nm):
            return new_semaphore("p_" + nm)

        g = [sb(f"g{i}", [P, WIDE]) for i in range(2)]
        gq = [sb(f"gq{i}", [P, WIDE], I16) for i in range(2)]
        sig = [sb(f"sig{i}", [P, WIDE]) for i in range(2)]
        sq = [sb(f"sq{i}", [P, WIDE], I32) for i in range(2)]
        loaded = [sem(f"loaded{i}") for i in range(2)]
        g_done, sig_done, sq_done, prod_done, peaked = sem("g_done"), sem("sig_done"), sem("sq_done"), sem("prod_done"), sem("peaked")
        g_v = g_dram.rearrange("c f p t -> (c f) p t").rearrange("(n f) p t -> n p f t", f=2)

        def tile(n):
            return prod[:, bass.ds(n * WIDE, WIDE)]

        def each(eng, step):
            for n in range(2):
                step(n, n)
            with eng.Fori(0, (N - 2) // 2) as j:
                for u in range(2):
                    step(2 * j + 2 + u, u)

        block = ctx.enter_context(nc.Block())

        @block.sync
        def _(sp):
            def step(n, par):
                wait(sp, g_done, n - 1)
                sp.dma_start(g[par][:, :].rearrange("p (f t) -> p f t", f=2), g_v[n]).then_inc(loaded[par], 16)

            each(sp, step)

        @block.scalar
        def _(act):
            def step(n, par):
                act.wait_ge(g_done, n + 1)
                act.activation(sig[par][:, :], gq[par][:, :], ACT.Sigmoid, scale=s.s_g[:, 0:1]).then_inc(sig_done, 1)
                act.wait_ge(sig_done, n + 1)
                wait(act, prod_done, n - 1)
                act.activation(sq[par][:, :], sig[par][:, :], ACT.Copy, scale=SIG_STEPS).then_inc(sq_done, 1)

            each(act, step)

        @block.vector
        def _(dve):
            def quantise(n, par):
                dve.wait_ge(loaded[par], 16 * (n // 2) + 16)
                wait(dve, sig_done, n - 1)
                wait(dve, prod_done, n - 1)
                dve.tensor_scalar(gq[par][:, :], g[par][:, :], s.r_g[:, 0:1], None, ALU.mult).then_inc(g_done, 1)

            def multiply(n, par):
                dve.wait_ge(sq_done, n + 1)
                dve.scalar_tensor_tensor(tile(n), sq[par][:, :], SIG_STEPS - 1.0, gq[par][:, :], ALU.min,
                                         ALU.mult).then_inc(prod_done, 1)

            def peak(n, par):
                dve.wait_ge(prod_done, n + 1)
                dve.tensor_reduce(s.peak_p[:, bass.ds(n, 1)], tile(n), AX.X, ALU.max,
                                  apply_absolute_value=True).then_inc(peaked, 1)

            def step(n, par):
                if not (isinstance(n, int) and n < 2):
                    multiply(n - 2, par)
                quantise(n, par)
                if not (isinstance(n, int) and n < 2):
                    peak(n - 2, par)

            each(dve, step)
            for n in (N - 2, N - 1):
                multiply(n, n % 2)
                peak(n, n % 2)


def gated_product(nc, prod, u_dram, o_dram, s, CH):
    N = CH * FT // 2
    with semaphores(nc) as new_semaphore, ExitStack() as ctx:
        def sb(nm, shape, dt=F32):
            return ctx.enter_context(nc.sbuf_tensor("o_" + nm, shape, dt))

        def sem(nm):
            return new_semaphore("o_" + nm)

        u = [sb(f"u{i}", [P, WIDE]) for i in range(3)]
        uq = [sb(f"uq{i}", [P, WIDE], I16) for i in range(3)]
        pq = [sb(f"pq{i}", [P, WIDE], I16) for i in range(3)]
        loaded = [sem(f"loaded{i}") for i in range(3)]
        stored = sem("stored")
        u_done, pq_done, o_done, peaked = sem("u_done"), sem("pq_done"), sem("o_done"), sem("peaked")
        u_v = u_dram.rearrange("c f p t -> (c f) p t").rearrange("(n f) p t -> n p f t", f=2)
        o_v = o_dram.rearrange("c f p t -> (c f) p t").rearrange("(n f) p t -> n p f t", f=2)

        def tile(n):
            return prod[:, bass.ds(n * WIDE, WIDE)]

        def each(eng, step):
            for n in range(3):
                step(n, n, 0)
            with eng.Fori(0, (N - 3) // 3) as j:
                for v in range(3):
                    step(3 * j + 3 + v, v, j + 1)

        block = ctx.enter_context(nc.Block())

        @block.sync
        def _(sp):
            def step(n, slot, i):
                wait(sp, u_done, n - 2)
                sp.dma_start(u[slot][:, :].rearrange("p (f t) -> p f t", f=2), u_v[n]).then_inc(loaded[slot], 16)

            each(sp, step)

        @block.gpsimd
        def _(pool):
            def step(n, slot, i):
                pool.wait_ge(o_done, n + 1)
                pool.dma_start(o_v[n], tile(n).rearrange("p (f t) -> p f t", f=2)).then_inc(stored, 16)

            each(pool, step)
            pool.wait_ge(stored, 16 * N)

        @block.scalar
        def _(act):
            def step(n, slot, i):
                wait(act, o_done, n - 2)
                act.activation(pq[slot][:, :], tile(n), ACT.Copy, scale=s.r_p[:, 0:1]).then_inc(pq_done, 1)
                act.wait_ge(loaded[slot], at(i, 16, 16))
                act.activation(uq[slot][:, :], u[slot][:, :], ACT.Copy, scale=s.r_u[:, 0:1]).then_inc(u_done, 1)

            each(act, step)

        @block.vector
        def _(dve):
            def multiply(n, slot):
                dve.wait_ge(u_done, n + 1)
                dve.wait_ge(pq_done, n + 1)
                dve.tensor_tensor(tile(n), pq[slot][:, :], uq[slot][:, :], ALU.mult).then_inc(o_done, 1)

            def peak(n):
                dve.wait_ge(o_done, n + 1)
                dve.tensor_reduce(s.peak_o[:, bass.ds(n, 1)], tile(n), AX.X, ALU.max,
                                  apply_absolute_value=True).then_inc(peaked, 1)

            def step(n, slot, i):
                multiply(n, slot)
                if not (isinstance(n, int) and n == 0):
                    peak(n - 1)

            each(dve, step)
            peak(N - 1)


def down_product(nc, o_dram, wd, s, x2, out, CH):
    x2_v = x2.rearrange("b s d -> (b s) d").rearrange("(t p) d -> t p d", p=P)
    out_v = out.rearrange("b s d -> (b s) d").rearrange("(t p) d -> t p d", p=P)
    with semaphores(nc) as new_semaphore, ExitStack() as ctx:
        def sb(nm, shape, dt=F32):
            return ctx.enter_context(nc.sbuf_tensor("d_" + nm, shape, dt))

        def sem(nm):
            return new_semaphore("d_" + nm)

        o = [sb(f"o{i}", [P, CHUNK]) for i in range(4)]
        oq = [sb(f"oq{i}", [P, CHUNK], I16) for i in range(2)]
        ot = [[sb(f"ot{i}_{h}", [P, FT, CHUNK], F32R) for h in ("high", "low")] for i in range(2)]
        x = [sb(f"x{i}", [P, D]) for i in range(2)]
        y = [sb(f"y{i}", [P, D]) for i in range(2)]
        bank = [ctx.enter_context(nc.psum_tensor(f"d_prod{i}", [P, 512], F32)) for i in range(2)]
        loaded = [sem(f"loaded{i}") for i in range(4)]
        x_in = [sem(f"x_in{i}") for i in range(2)]
        y_out = [sem(f"y_out{i}") for i in range(2)]
        quantised, high_done, low_done = sem("quantised"), sem("high_done"), sem("low_done")
        prod_done, added = sem("prod_done"), sem("added")

        def steps(eng, front0, chunk):
            front0()
            chunk(0, 0, CH > 1)
            pairs = (CH - 2) // 2 if CH > 2 else 0
            if pairs:
                with eng.Fori(0, pairs) as j:
                    for v in range(2):
                        chunk(2 * j + 1 + v, (1 + v) % 2, True)
            for c in range(1 + 2 * pairs, CH):
                chunk(c, c % 2, c < CH - 1)

        PER = FT // CTILES

        block = ctx.enter_context(nc.Block())

        @block.sync
        def _(sp):
            def load(c, f):
                wait(sp, quantised, at(c, FT, f - 3))
                sp.dma_start(o[f % 4][:, :], o_dram[c, f]).then_inc(loaded[f % 4], 16)

            def load_x(c, t):
                wait(sp, added, at(c, CTILES, t - 1))
                sp.dma_start(x[t % 2][:, :], x2_v[c * CTILES + t]).then_inc(x_in[t % 2], 16)

            def store(c, t):
                sp.wait_ge(added, at(c, CTILES, t + 1))
                sp.dma_start(out_v[c * CTILES + t], y[t % 2][:, :]).then_inc(y_out[t % 2], 16)

            def chunk(c, par, front):
                for t in range(CTILES):
                    load_x(c, t)
                    if front:
                        for f in range(PER * t, PER * (t + 1)):
                            load(c + 1, f)
                    store(c, t)

            def front0():
                for f in range(FT):
                    load(0, f)

            steps(sp, front0, chunk)
            for i in range(2):
                sp.wait_ge(y_out[i], 16 * CH * CTILES // 2)

        @block.tensor
        def _(pe):
            def chunk(c, par, front):
                for t in range(CTILES):
                    if t == 0:
                        pe.wait_ge(low_done, at(c, FT, FT))
                    wait(pe, added, at(c, CTILES, t - 1))
                    for f in range(FT):
                        m = split_matmul(pe, bank[t % 2][:, :], [s_[:, f, t * P:(t + 1) * P] for s_ in ot[par]],
                                         [s_[:, f, :] for s_ in wd], f == 0, f == FT - 1)
                    m.then_inc(prod_done, 1)

            steps(pe, lambda: None, chunk)

        @block.scalar
        def _(act):
            def high(c, par, f):
                act.wait_ge(quantised, at(c, FT, f + 1))
                if f == 0:
                    wait(act, prod_done, at(c - 1, CTILES, 0))
                act.activation(ot[par][0][:, f, :], oq[f % 2][:, :], ACT.Copy).then_inc(high_done, 1)

            def chunk(c, par, front):
                if front:
                    for f in range(FT):
                        high(c + 1, 1 - par, f)

            def front0():
                for f in range(FT):
                    high(0, 0, f)

            steps(act, front0, chunk)

        @block.vector
        def _(dve):
            def quantise(c, f):
                dve.wait_ge(loaded[f % 4], at(c, 16 * FT // 4, 16 * (f // 4) + 16))
                wait(dve, low_done, at(c, FT, f - 1))
                dve.tensor_scalar(oq[f % 2][:, :], o[f % 4][:, :], s.r_o[:, 0:1], None, ALU.mult).then_inc(quantised, 1)

            def low(c, par, f):
                dve.wait_ge(high_done, at(c, FT, f + 1))
                dve.tensor_tensor(ot[par][1][:, f, :], oq[f % 2][:, :], bits(ot[par][0][:, f, :]), ALU.subtract).then_inc(low_done, 1)

            def add(c, t):
                dve.wait_ge(prod_done, at(c, CTILES, t + 1))
                dve.wait_ge(x_in[t % 2], at(c, 16 * CTILES // 2, 16 * (t // 2) + 16))
                if not (isinstance(c, int) and c == 0 and t < 2):
                    dve.wait_ge(y_out[t % 2], at(c, 16 * CTILES // 2, 16 * (t // 2)))
                dve.scalar_tensor_tensor(y[t % 2][:, :], bank[t % 2][:, :], s.s_o[:, 0:1], x[t % 2][:, :], ALU.mult,
                                         ALU.add).then_inc(added, 1)

            def prepare(c, par, t):
                for f in range(PER * t, PER * (t + 1)):
                    quantise(c, f)
                    if f:
                        low(c, par, f - 1)
                if t == CTILES - 1:
                    low(c, par, FT - 1)

            def chunk(c, par, front):
                for t in range(CTILES):
                    if front:
                        prepare(c + 1, 1 - par, t)
                    add(c, t)

            def front0():
                for t in range(CTILES):
                    prepare(0, 0, t)

            steps(dve, front0, chunk)


def feed_forward(nc, ident, x2, w_gate, w_up, w_down, g_dram, u_dram, o_dram, out, CH=NCH):
    T = BATCH * SEQ // P if CH == NCH else CH * CTILES
    NF = CH * FT
    with ExitStack() as ctx:
        s = Scalars(ctx, nc)
        with ExitStack() as inner:
            xn = inner.enter_context(nc.sbuf_tensor("f_xn", [P, T, D], F32))
            wgu = [[inner.enter_context(nc.sbuf_tensor(f"f_w{w}_{h}", [P, FT, KD, P], F32R)) for h in ("high", "low")]
                   for w in "gu"]
            src = [w.rearrange("(f p) i -> f p i", p=P) for w in (w_gate, w_up)]
            quantise_weights(nc, "fw", ident, FT, 2, lambda i, r: src[r][i], lambda i, r: [h[:, i, :, :] for h in wgu[r]])
            normalise_tokens(nc, x2, xn, s.peak_x, T)
            scale_from_peak(nc, "fx", [(s.peak_x[:, 0:T], (None, 1.0), s.s_x, s.r_x)])
            gate_and_up(nc, ident, xn, wgu[0], wgu[1], s, g_dram, u_dram, CH)
        scale_from_peak(nc, "fg", [(s.peak_g[:, 0:NF], (s.s_x[:, 0:1], 1.0), s.s_g, s.r_g),
                                   (s.peak_u[:, 0:NF], (s.s_x[:, 0:1], 1.0), s.s_u, s.r_u)])
        with nc.sbuf_tensor("f_prod", [P, NF * CHUNK], F32) as prod:
            product_peak(nc, g_dram, prod, s, CH)
            scale_from_peak(nc, "fp", [(s.peak_p[:, 0:NF // 2], (s.s_g[:, 0:1], 1.0 / SIG_STEPS), s.s_p, s.r_p)])
            gated_product(nc, prod, u_dram, o_dram, s, CH)
        scale_from_peak(nc, "fo", [(s.peak_o[:, 0:NF // 2], (s.s_p[:, 0:1], s.s_u[:, 0:1]), s.s_o, s.r_o)])
        wd = [ctx.enter_context(nc.sbuf_tensor(f"f_wd_{h}", [P, FT, D], F32R)) for h in ("high", "low")]
        wd_src = w_down.rearrange("(o p) (c i) -> o c p i", p=P, i=512)
        quantise_weights(nc, "fd", ident, D // P, 3, lambda i, r: wd_src[i, r],
                         lambda i, r: [h[:, 4 * r:4 * r + 4, bass.ds(i * P, P)] for h in wd])
        down_product(nc, o_dram, wd, s, x2, out, CH)


def build(nc, t):
    x1 = nc.dram_tensor("x1", (BATCH, SEQ, D), F32, kind="Internal").ap()
    x2 = nc.dram_tensor("x2", (BATCH, SEQ, D), F32, kind="Internal").ap()
    qn = nc.dram_tensor("qn", (BATCH, SEQ, XH * XD), F32, kind="Internal").ap()
    g_dram, u_dram, o_dram = [nc.dram_tensor(n, (NCH, FT, P, CHUNK), F32, kind="Internal").ap()
                              for n in ("gate", "up", "gated")]
    with nc.sbuf_tensor("ident", [P, P], F32) as ident:
        eye = ident[:, :]
        self_attention(nc, eye, t["x"], t["wqkv_t"], t["self_wo_t"], t["theta_base"], t["log_xi"], t["pi_gate"], t["e_gate"], x1)
        query_projection(nc, eye, x1, t["wq_t"], qn)
        cross_attention(nc, eye, t["ctx_t"], qn, x1, t["wkv_t"], t["cross_wo_t"], (t["q_norm_w"], t["k_norm_w"]), x2)
        feed_forward(nc, eye, x2, t["w_gate"], t["w_up"], t["w_down"], g_dram, u_dram, o_dram, t["out"])


def kernel(**inputs):
    import numpy as _np
    import concourse.bacc as _bacc
    from concourse import mybir as _mybir
    from concourse.bass_utils import run_bass_kernel_spmd as _run

    a = {name: _np.asarray(v) for name, v in inputs.items()}
    freq = (_np.float32(_np.pi) ** (1 - _np.arange(0, ADH, 2, dtype=_np.float32) / ADH)).astype(_np.float32)
    theta = _np.arange(SEQ, dtype=_np.float32)[:, None] * freq[None]
    laid = {
        "x": a["x"],
        "ctx_t": a["ctx_1024"].reshape(BATCH, CT, CW, KD, P).transpose(0, 1, 4, 3, 2),
        "wqkv_t": a["L0_attn_Wqkv"].T.reshape(KD, P, 3 * D).transpose(1, 0, 2),
        "self_wo_t": a["L0_attn_Wo"].T.reshape(KD, P, D).transpose(1, 0, 2),
        "theta_base": theta.reshape(NQ, TQ, ADH // 2).transpose(1, 0, 2),
        "log_xi": a["L0_attn_log_xi"], "pi_gate": a["L0_attn_pi_gate_logit"], "e_gate": a["L0_attn_e_gate_logit"],
        "wq_t": a["L0_xattn_wq"].T.reshape(KD, P, XH * XD).transpose(1, 0, 2),
        "wkv_t": _np.concatenate([a["L0_xattn_wk"], a["L0_xattn_wv"]], 0).T.reshape(KD, P, 2 * KVW).transpose(1, 0, 2),
        "cross_wo_t": a["L0_xattn_wo"].T.reshape(2, 2, XG, XD, D).transpose(1, 3, 0, 2, 4).reshape(P, 2 * XG, D),
        "q_norm_w": a["L0_xattn_q_norm_w"], "k_norm_w": a["L0_xattn_k_norm_w"],
        "w_gate": a["L0_ffn_w_gate"], "w_up": a["L0_ffn_w_up"], "w_down": a["L0_ffn_w_down"],
    }
    nc = _bacc.Bacc("TRN2", target_bir_lowering=False, num_devices=1)
    arrays, t = {}, {}
    for name, v in laid.items():
        arrays[f"in_{name}_dram"] = v = _np.ascontiguousarray(v)
        t[name] = nc.dram_tensor(f"in_{name}_dram", v.shape, _mybir.dt.from_np(v.dtype), kind="ExternalInput").ap()
    t["out"] = nc.dram_tensor("out_0_dram", (BATCH, SEQ, D), F32, kind="ExternalOutput").ap()
    build(nc, t)
    r = _run(nc, [arrays], core_ids=[0])
    return r.results[0]["out_0_dram"]
```
